# Optimizing a Trainium2 kernel written in Bass

```python
import numpy as np
import jax
import jax.numpy as jnp

def _softmax(x, axis=-1):
    return jax.nn.softmax(x, axis=axis)

def _gelu(x):
    return jax.nn.gelu(x, approximate=True)

def _silu(x):
    return jax.nn.silu(x)

def _sigmoid(x):
    return jax.nn.sigmoid(x)

def _layernorm(x, axis=-1, eps=1e-05):
    m = jnp.mean(x, axis=axis, keepdims=True)
    v = jnp.var(x, axis=axis, keepdims=True)
    return (x - m) / jnp.sqrt(v + eps)

def _scatter_add(tgt, idx, src, axis=0):
    return tgt.at[idx].add(src)

def _segment_sum(src, seg, n):
    return jax.ops.segment_sum(src, seg, n)
kernel_name = 'mk_adaln_d1_jaxref_r8_c4fe39'

def setup_inputs(seed: int=0):
    np.random.seed(seed)
    _w = jnp.asarray

    def _L0_attn_setup():
        import jax, jax.numpy as jnp
        import numpy as np
        N_HEADS = 16
        N_KV_HEADS = 4
        HEAD_DIM = 128
        WINDOW = 128
        ROPE_THETA = 10000.0

        def _rope_angles(seq_len, head_dim):
            inv_freq = 1.0 / ROPE_THETA ** (jnp.arange(0, head_dim, 2, dtype=jnp.float32) / head_dim)
            t = jnp.arange(seq_len, dtype=jnp.float32)
            return jnp.outer(t, inv_freq)

        def _apply_rope(x, angles):
            B, S, H, hd = x.shape
            xr = x.reshape(B, S, H, hd // 2, 2)
            x0, x1 = (xr[..., 0], xr[..., 1])
            cos = jnp.cos(angles)[None, :, None, :]
            sin = jnp.sin(angles)[None, :, None, :]
            y0 = x0 * cos - x1 * sin
            y1 = x0 * sin + x1 * cos
            return jnp.stack([y0, y1], axis=-1).reshape(B, S, H, hd)
        key = jax.random.key(seed)
        ks = jax.random.split(key, 5)
        B, S, D = (2, 256, 256)
        kv_dim = N_KV_HEADS * HEAD_DIM
        w = 0.02
        return {'x': jax.random.normal(ks[0], (B, S, D), dtype=jnp.float32), 'wq': jax.random.normal(ks[1], (D, N_HEADS * HEAD_DIM), dtype=jnp.float32) * w, 'wk': jax.random.normal(ks[2], (D, kv_dim), dtype=jnp.float32) * w, 'wv': jax.random.normal(ks[3], (D, kv_dim), dtype=jnp.float32) * w, 'wo': jax.random.normal(ks[4], (N_HEADS * HEAD_DIM, D), dtype=jnp.float32) * w}
    _L0_attn_in = _L0_attn_setup()

    def _L0_ffn_setup():
        import jax, jax.numpy as jnp
        import numpy as np
        E, K, H, I = (64, 6, 256, 176)
        NS = 2
        IS = NS * I
        CAP = 32
        T_TOKENS = (1, 128)
        SCALE = 0.02

        def _moe_infer(x, gate_w, w_gate, w_up, w_down):
            T = x.shape[0]
            TK = T * K
            logits = x @ gate_w.T
            scores = jax.nn.softmax(logits, axis=-1)
            topk_w, topk_i = jax.lax.top_k(scores, K)
            flat_i = topk_i.reshape(-1)
            flat_w = topk_w.reshape(-1)
            token_ids = jnp.arange(TK, dtype=jnp.int32) // K
            order = jnp.argsort(flat_i)
            sorted_e = flat_i[order]
            counts = jnp.bincount(flat_i, length=E)
            starts = jnp.concatenate([jnp.zeros((1,), counts.dtype), jnp.cumsum(counts)[:-1]])
            pos_sorted = jnp.arange(TK) - starts[sorted_e]
            pos = jnp.zeros((TK,), jnp.int32).at[order].set(pos_sorted.astype(jnp.int32))
            valid = pos < CAP
            slot = jnp.where(valid, pos, CAP)
            buf = jnp.zeros((E, CAP + 1, H), x.dtype).at[flat_i, slot].set(x[token_ids])
            g = jnp.einsum('ech,ehi->eci', buf, w_gate)
            u = jnp.einsum('ech,ehi->eci', buf, w_up)
            y = jnp.einsum('eci,eih->ech', jax.nn.silu(g) * u, w_down)
            out_slots = y[flat_i, slot] * (flat_w * valid)[:, None]
            return out_slots.reshape(T, K, H).sum(axis=1)
        key = jax.random.key(seed)
        ks = jax.random.split(key, 8)
        f32 = jnp.float32
        return {'hidden_states': jax.random.normal(ks[0], (*T_TOKENS, H), f32), 'gate_w': jax.random.normal(ks[1], (E, H), f32) * SCALE, 'w_gate': jax.random.normal(ks[2], (E, H, I), f32) * SCALE, 'w_up': jax.random.normal(ks[3], (E, H, I), f32) * SCALE, 'w_down': jax.random.normal(ks[4], (E, I, H), f32) * SCALE, 'sw_gate': jax.random.normal(ks[5], (H, IS), f32) * SCALE, 'sw_up': jax.random.normal(ks[6], (H, IS), f32) * SCALE, 'sw_down': jax.random.normal(ks[7], (IS, H), f32) * SCALE}
    _L0_ffn_in = _L0_ffn_setup()
    _L0_c = _w((lambda *s: np.random.randn(*s).astype(np.float32) * 0.05)(4, 256))
    _L0_wmod = _w((lambda *s: np.random.randn(*s).astype(np.float32) * 0.05)(256, 6 * 256) * 256 ** (-0.5))
    _d = {'L0_attn_x': _L0_attn_in['x'], 'L0_attn_wq': _L0_attn_in['wq'], 'L0_attn_wk': _L0_attn_in['wk'], 'L0_attn_wv': _L0_attn_in['wv'], 'L0_attn_wo': _L0_attn_in['wo'], 'L0_ffn_gate_w': _L0_ffn_in['gate_w'], 'L0_ffn_w_gate': _L0_ffn_in['w_gate'], 'L0_ffn_w_up': _L0_ffn_in['w_up'], 'L0_ffn_w_down': _L0_ffn_in['w_down'], 'L0_ffn_sw_gate': _L0_ffn_in['sw_gate'], 'L0_ffn_sw_up': _L0_ffn_in['sw_up'], 'L0_ffn_sw_down': _L0_ffn_in['sw_down'], 'L0_c': _L0_c, 'L0_wmod': _L0_wmod}
    _x0 = _d['L0_attn_x']
    _d['L0_attn_x'] = jax.random.normal(jax.random.fold_in(jax.random.key(seed), 1), (4, 256, 256), dtype=_x0.dtype)
    del _x0
    return _d

def reference(L0_attn_x, L0_attn_wq, L0_attn_wk, L0_attn_wv, L0_attn_wo, L0_ffn_gate_w, L0_ffn_w_gate, L0_ffn_w_up, L0_ffn_w_down, L0_ffn_sw_gate, L0_ffn_sw_up, L0_ffn_sw_down, L0_c, L0_wmod):

    def _L0_attn_ref(x, wq, wk, wv, wo):
        import jax, jax.numpy as jnp
        import numpy as np
        N_HEADS = 16
        N_KV_HEADS = 4
        HEAD_DIM = 128
        WINDOW = 128
        ROPE_THETA = 10000.0

        def _rope_angles(seq_len, head_dim):
            inv_freq = 1.0 / ROPE_THETA ** (jnp.arange(0, head_dim, 2, dtype=jnp.float32) / head_dim)
            t = jnp.arange(seq_len, dtype=jnp.float32)
            return jnp.outer(t, inv_freq)

        def _apply_rope(x, angles):
            B, S, H, hd = x.shape
            xr = x.reshape(B, S, H, hd // 2, 2)
            x0, x1 = (xr[..., 0], xr[..., 1])
            cos = jnp.cos(angles)[None, :, None, :]
            sin = jnp.sin(angles)[None, :, None, :]
            y0 = x0 * cos - x1 * sin
            y1 = x0 * sin + x1 * cos
            return jnp.stack([y0, y1], axis=-1).reshape(B, S, H, hd)
        B, S, D = x.shape
        hd = HEAD_DIM
        n_rep = N_HEADS // N_KV_HEADS
        angles = _rope_angles(S, hd)
        q = (x @ wq).reshape(B, S, N_HEADS, hd)
        k = (x @ wk).reshape(B, S, N_KV_HEADS, hd)
        v = (x @ wv).reshape(B, S, N_KV_HEADS, hd)
        q = _apply_rope(q, angles)
        k = _apply_rope(k, angles)
        k = jnp.repeat(k, n_rep, axis=2)
        v = jnp.repeat(v, n_rep, axis=2)
        i = jnp.arange(S)[:, None]
        j = jnp.arange(S)[None, :]
        allowed = (j <= i) & (j > i - (WINDOW + 1))
        scale = 1.0 / jnp.sqrt(jnp.float32(hd))
        scores = jnp.einsum('bqhd,bkhd->bhqk', q, k) * scale
        scores = jnp.where(allowed[None, None], scores, jnp.float32(-jnp.inf))
        probs = jax.nn.softmax(scores, axis=-1)
        out = jnp.einsum('bhqk,bkhd->bqhd', probs, v).reshape(B, S, N_HEADS * hd)
        return out @ wo

    def _L0_ffn_ref(hidden_states, gate_w, w_gate, w_up, w_down, sw_gate, sw_up, sw_down):
        import jax, jax.numpy as jnp
        import numpy as np
        E, K, H, I = (64, 6, 256, 176)
        NS = 2
        IS = NS * I
        CAP = 32
        T_TOKENS = (1, 128)
        SCALE = 0.02

        def _moe_infer(x, gate_w, w_gate, w_up, w_down):
            T = x.shape[0]
            TK = T * K
            logits = x @ gate_w.T
            scores = jax.nn.softmax(logits, axis=-1)
            topk_w, topk_i = jax.lax.top_k(scores, K)
            flat_i = topk_i.reshape(-1)
            flat_w = topk_w.reshape(-1)
            token_ids = jnp.arange(TK, dtype=jnp.int32) // K
            order = jnp.argsort(flat_i)
            sorted_e = flat_i[order]
            counts = jnp.bincount(flat_i, length=E)
            starts = jnp.concatenate([jnp.zeros((1,), counts.dtype), jnp.cumsum(counts)[:-1]])
            pos_sorted = jnp.arange(TK) - starts[sorted_e]
            pos = jnp.zeros((TK,), jnp.int32).at[order].set(pos_sorted.astype(jnp.int32))
            valid = pos < CAP
            slot = jnp.where(valid, pos, CAP)
            buf = jnp.zeros((E, CAP + 1, H), x.dtype).at[flat_i, slot].set(x[token_ids])
            g = jnp.einsum('ech,ehi->eci', buf, w_gate)
            u = jnp.einsum('ech,ehi->eci', buf, w_up)
            y = jnp.einsum('eci,eih->ech', jax.nn.silu(g) * u, w_down)
            out_slots = y[flat_i, slot] * (flat_w * valid)[:, None]
            return out_slots.reshape(T, K, H).sum(axis=1)
        orig_shape = hidden_states.shape
        x = hidden_states.reshape(-1, orig_shape[-1])
        y = _moe_infer(x, gate_w, w_gate, w_up, w_down).reshape(orig_shape)
        shared = jax.nn.silu(hidden_states @ sw_gate) * (hidden_states @ sw_up) @ sw_down
        return y + shared
    x = L0_attn_x
    mod = (_silu(L0_c) @ L0_wmod).reshape(L0_c.shape[0], 6, 1, -1)
    sa, ca, ga, sb, cb, gb = (mod[:, 0], mod[:, 1], mod[:, 2], mod[:, 3], mod[:, 4], mod[:, 5])
    ga = (2 * (ga >= 0) - 1) * jnp.maximum(jnp.abs(ga), 0.25)
    gb = (2 * (gb >= 0) - 1) * jnp.maximum(jnp.abs(gb), 0.25)
    h = _layernorm(x, axis=-1) * (1 + ca) + sa
    x = x + ga * _L0_attn_ref(h, L0_attn_wq, L0_attn_wk, L0_attn_wv, L0_attn_wo)
    h = _layernorm(x, axis=-1) * (1 + cb) + sb
    x = x + gb * _L0_ffn_ref(h, L0_ffn_gate_w, L0_ffn_w_gate, L0_ffn_w_up, L0_ffn_w_down, L0_ffn_sw_gate, L0_ffn_sw_up, L0_ffn_sw_down)
    return x

_drawn_inputs = setup_inputs


def setup_inputs(seed=0):
    import zlib

    import numpy as np

    out = dict(_drawn_inputs(seed))
    spreads = {}
    factors = {'L0_attn_wq': 8.0,
     'L0_attn_wk': 8.0,
     'L0_attn_wv': 5.013,
     'L0_attn_wo': 4.942,
     'L0_ffn_gate_w': 8.0,
     'L0_ffn_w_gate': 8.0,
     'L0_ffn_w_up': 8.0,
     'L0_ffn_w_down': 8.0,
     'L0_ffn_sw_gate': 8.0,
     'L0_ffn_sw_up': 8.0,
     'L0_ffn_sw_down': 8.0,
     'L0_c': 4.641,
     'L0_wmod': 4.636}
    for name, (base, spread) in spreads.items():
        noise = np.random.default_rng([zlib.crc32(name.encode()), seed]).standard_normal(out[name].shape)
        drawn = base * np.exp(spread * noise) if base else spread * noise
        out[name] = jnp.asarray(drawn.astype(out[name].dtype))
    for name, factor in factors.items():
        out[name] = (out[name] * factor).astype(out[name].dtype)
    return out
```

```python
from contextlib import ExitStack

import concourse.bass as bass
from concourse import mybir
from concourse.alu_op_type import AluOpType as ALU

ACT = mybir.ActivationFunctionType
F32 = mybir.dt.float32
F32R = mybir.dt.float32r
BF16 = mybir.dt.bfloat16
U32 = mybir.dt.uint32
AX_X = mybir.AxisListType.X

P = 128
BATCH, SEQ, D = 4, 256, 256
HEADS, KV_HEADS, HD = 16, 4, 128
GROUP = HEADS // KV_HEADS
EXPERTS, TOPK, CAP = 64, 6, 32
INTER, SHARED = 176, 352
T = BATCH * SEQ
TT = T // P
DC = D // P
BT = SEQ // P
EPS = 1e-5
PER = P // CAP
GROUPS = EXPERTS // PER
IA, IB = 96, 80
SM = [128, 128, 96]
RING = 4
ROW = D + EXPERTS
BIG = 3.0e38

PJ_ROPE = [0, 1, 2, 3, 6, 7, 8, 9, 12, 13]
PJ_V = [4, 5]
PJ_MIX = [(10, 11), (14, 15), (16, 17), (18, 19)]
PJ_USES = 20
IN_LOOP = ["h_t", "logits", "gu0", "gu1", "key_t", "gu2", "down"]
AT_END = ["h_t", "logits", "key_t", "gu0", "gu1", "gu2", "down"]
POST_USES = len(IN_LOOP)


def need(eng, sem, value):
    if not isinstance(value, int) or value > 0:
        eng.wait_ge(sem, value)


def alone(eng, passed):
    eng.sem_inc(passed)


class Steps:

    def __init__(self, eng, sem, base):
        self.eng, self.sem, self.base, self.n = eng, sem, base, 0

    def done(self, ins):
        self.n += 1
        ins.then_inc(self.sem, 1)

    def wait(self):
        self.eng.wait_ge(self.sem, self.base + self.n)


def bass_adaln_attention_moe(nc, x, c_t, wmod, wq, wk, wv, wo, gate_t, w_gate, w_up, w_down_a, w_down_b,
                             sw_gate, sw_up, sw_down, rope, masks, small, iota_row, out):
    ctx = ExitStack()
    with ctx:
        def sb(name, shape, dt=F32):
            return ctx.enter_context(nc.sbuf_tensor(name, shape, dt))

        def sem(name):
            return ctx.enter_context(nc.semaphore(name))

        bank = [ctx.enter_context(nc.psum_tensor(f"bank{i}", [P, 512], F32)) for i in range(8)]
        pj, sc, tr, wo_bank, post = bank[0:2], bank[2:4], bank[4:6], bank[6], bank[7]
        acc, gt_bank, ht_bank, gu_bank, y_bank = bank[0:4], bank[4], bank[5], bank[6], bank[7]

        SLOT = 2 * PER * DC * INTER + 2 * PER * D
        dense = sb("dense", [P, 2 * SLOT + 512])
        wq_s = dense[:, 0:4096].rearrange("p (c n) -> p c n", c=DC)
        wk_s = dense[:, 4096:5120].rearrange("p (c n) -> p c n", c=DC)
        wv_s = dense[:, 5120:6144].rearrange("p (c n) -> p c n", c=DC)
        wo_s = dense[:, 6144:10240].rearrange("p (h n) -> p h n", h=HEADS)
        slots01 = sb("slots01", [P, 2 * SLOT])
        wmod_s = slots01[:, SLOT:SLOT + 3072].rearrange("p (c n) -> p c n", c=DC)

        def slot(u):
            base = slots01[:, u * SLOT:(u + 1) * SLOT] if u < 2 else dense[:, (u - 2) * SLOT:(u - 1) * SLOT]
            n = PER * DC * INTER
            gu = base[:, 0:2 * n].rearrange("p (m j c i) -> p m j c i", m=2, j=PER, c=DC)
            wa = base[0:IA, 2 * n:2 * n + PER * D].rearrange("p (j d) -> p j d", j=PER)
            wb = base[0:IB, 2 * n + PER * D:SLOT].rearrange("p (j d) -> p j d", j=PER)
            return gu, wa, wb

        area = sb("area", [P, 7168])
        q_s = area[:, 0:2048].rearrange("p (g h s) -> p g h s", g=2, h=GROUP)
        mix_s = area[:, 2048:4096].rearrange("p (g t n) -> p g t n", g=2, t=BT)
        prob_near = area[:, 4096:5120].rearrange("p (g h s) -> p g h s", g=2, h=GROUP)
        prob_far = area[:, 5120:7168].rearrange("p (g h s) -> p g h s", g=2, h=GROUP)
        xn_s = area[:, 0:512].rearrange("p (t d) -> p t d", t=BT)
        mask_in = area[:, 4096:4480].rearrange("p (m k) -> p m k", m=3)
        iota_s = area[:, 0:1024]
        key_b = area[0:EXPERTS, 1024:2048]
        hb_t = area[:, 2048:2560].rearrange("p (g c s) -> p g c s", g=2, c=DC)
        rows_s = area[:, 2560:3200].rearrange("p (g n) -> p g n", g=2)
        eg_x = area[:, 3200:3376]
        tg_x = area[:, 3376:3552]
        hid_x = area[:, 3552:3728]
        hid_ta = area[0:IA, 3728:3856]
        hid_tb = area[0:IB, 3856:3984]
        gb_all = area[:, 3984:5008].rearrange("p (b d) -> p b d", b=BATCH)
        w_tmp = area[:, 5008:5012]

        x_s = sb("x_s", [P, TT, D])
        h_all = sb("h_all", [P, DC, T])
        h_cur = sb("h_cur", [P, DC, SEQ])
        k_s = sb("k_s", [P, KV_HEADS, SEQ])
        v_s = sb("v_s", [P, BT, KV_HEADS * HD])
        prob_t = sb("prob_t", [P, 3, GROUP * P])
        swap_s = sb("swap_s", [P, 2, 2, SEQ])
        mod_s = sb("mod_s", [P, 4 * D])
        rope_s = sb("rope_s", [P, 4, SEQ])
        mask_near = sb("mask_near", [P, GROUP, P], BF16)
        mask_far = sb("mask_far", [P, 2, 2, P], BF16)
        ident_b = sb("ident_b", [P, P], BF16)
        ident = sb("ident", [P, P])
        gate_s = sb("gate_s", [P, DC, EXPERTS])
        swg_s = sb("swg_s", [P, DC, SHARED])
        swu_s = sb("swu_s", [P, DC, SHARED])
        swd_s = sb("swd_s", [P, 3, D])
        small_s = sb("small_s", [P, TT + PER])
        rank = small_s[:, 0:TT]
        quad = small_s[:, TT:TT + PER]
        row_s = sb("row_s", [P, BT, ROW])
        h_t = sb("h_t", [P, DC, SEQ])
        sh_s = sb("sh_s", [P, 3, SEQ])
        eg_s = sb("eg_s", [P, SEQ])
        tg_s = sb("tg_s", [P, SEQ])
        tmp_s = sb("tmp_s", [P, BT, D])
        key_all = sb("key_all", [EXPERTS, T])
        ct_s = sb("ct_s", [P, DC, BATCH])
        ce_s = sb("ce_s", [P, DC, BATCH])
        modt_s = sb("modt_s", [P, 2, DC, BATCH])
        modr_s = sb("modr_s", [BATCH, 4 * D])
        modq_s = sb("modq_s", [BATCH, 4, D])
        stat = sb("stat", [P, BT, 6])
        mv = sb("mv", [P, BT, 2])
        var = sb("var", [P, BT])
        half = sb("half", [P, BT])
        rstd = sb("rstd", [P, BT])
        nmax = sb("nmax", [P, 2, 8])
        psum_p = sb("psum_p", [P, 2, 8])
        rinv = sb("rinv", [P, 2, 8])
        lg = sb("lg", [P, BT, EXPERTS + 2])
        rp = sb("rp", [P, BT, EXPERTS + 2])
        top = sb("top", [P, BT, 8])
        pick = sb("pick", [P, BT, 8])
        nv = sb("nv", [P, BT])
        sm = sb("sm", [P, BT])
        key = sb("key", [P, BT, EXPERTS])
        first = sb("first", [EXPERTS, CAP])
        tok_e = sb("tok_e", [EXPERTS, CAP])
        tok = sb("tok", [P, GROUPS])
        tok_f = sb("tok_f", [P, GROUPS])
        tok_i = sb("tok_i", [P, GROUPS], U32)
        w_slot = sb("w_slot", [P, 2])
        zero_s = sb("zero_s", [P, 512], BF16)
        place = [sb(f"place{i}", [P, T], F32R) for i in range(2)]
        y_hi = [sb(f"y_hi{i}", [P, D], F32R) for i in range(2)]
        y_lo = [sb(f"y_lo{i}", [P, D], F32R) for i in range(2)]

        mod_d = nc.dram_tensor("mod_d", (BATCH, 4 * D), F32, kind="Internal").ap()
        rows_d = nc.dram_tensor("rows_d", (T, ROW), F32, kind="Internal").ap()

        in_c, in_x, in_mod, in_small = sem("in_c"), sem("in_x"), sem("in_mod"), sem("in_small")
        in_rope, in_mask, in_qkv, in_wo, in_tail = (sem("in_rope"), sem("in_mask"), sem("in_qkv"),
                                                     sem("in_wo"), sem("in_tail"))
        in_iota, in_gb, in_modrow = sem("in_iota"), sem("in_gb"), sem("in_modrow")
        in_gu = [sem(f"in_gu{u}") for u in range(RING)]
        in_wd = [sem(f"in_wd{u}") for u in range(RING)]
        mod_stored, row_stored, out_stored = sem("mod_stored"), sem("row_stored"), sem("out_stored")
        ce_ready, silu_c, mod_mm, modt_mm, mod_rows, modt_ready = (
            sem("ce_ready"), sem("silu_c"), sem("mod_mm"), sem("modt_mm"), sem("mod_rows"), sem("modt_ready"))
        pre_step = sem("pre_step")
        consts, sentinels = sem("consts"), sem("sentinels")
        var1, rstd1, xn_ready, xt_full, xt_free = (sem("var1"), sem("rstd1"), sem("xn_ready"), sem("xt_full"),
                                                  sem("xt_free"))
        ln_step, att_step, post_step = sem("ln_step"), sem("att_step"), sem("post_step")
        h_ready, pj_full, sc_full, tr_full, wo_full, post_full = (
            sem("h_ready"), sem("pj_full"), sem("sc_full"), sem("tr_full"), sem("wo_full"), sem("post_full"))
        cos_done, swap_done, sin_done, rope_done = (sem("cos_done"), sem("swap_done"), sem("sin_done"),
                                                    sem("rope_done"))
        v_out, mix_out0, mix_out1 = sem("v_out"), sem("mix_out0"), sem("mix_out1")
        max_done, exp_done, rinv_done, norm_done = (sem("max_done"), sem("exp_done"), sem("rinv_done"),
                                                    sem("norm_done"))
        trans_out0, trans_out12 = sem("trans_out0"), sem("trans_out12")
        wo_free, post_free, var2, rstd2, h2_ready = (sem("wo_free"), sem("post_free"), sem("var2"), sem("rstd2"),
                                                     sem("h2_ready"))
        nv_ready, se_ready, score_ready, key_ready, eg_ready, post_done = (
            sem("nv_ready"), sem("se_ready"), sem("score_ready"), sem("key_ready"), sem("eg_ready"), sem("post_done"))
        tok_step, tok_e_ready, tok_t, tok_ready = sem("tok_step"), sem("tok_e_ready"), sem("tok_t"), sem("tok_ready")
        rows_in = [sem("rows_in0"), sem("rows_in1")]
        acc_zero, gt_full, hb_ready, gu_full, eg_x_ready, hid_ready = (
            sem("acc_zero"), sem("gt_full"), sem("hb_ready"), sem("gu_full"), sem("eg_x_ready"), sem("hid_ready"))
        ht_full, hid_t_ready, y_full, hi_ready, lo_ready = (sem("ht_full"), sem("hid_t_ready"), sem("y_full"),
                                                            sem("hi_ready"), sem("lo_ready"))
        w_ready, place_ready, back_done, exp_step, out_ready = (sem("w_ready"), sem("place_ready"), sem("back_done"),
                                                                sem("exp_step"), sem("out_ready"))

        dve_passed, pe_passed = sem("dve_passed"), sem("pe_passed")

        POST_STEPS, EXP_STEPS = 18, 4

        def pj_release(b, n):
            if n in PJ_ROPE:
                return swap_done, 10 * b + PJ_ROPE.index(n) + 1
            if n in PJ_V:
                return v_out, 2 * b + PJ_V.index(n) + 1
            g = [n in m for m in PJ_MIX].index(True)
            return (mix_out0, 4 * b + g + 1) if PJ_MIX[g][0] == n else (mix_out1, 4 * b + g + 1)

        def tr_release(b, n):
            g, i = divmod(n, 3)
            return (trans_out0, 4 * b + g + 1) if i == 0 else (trans_out12, 8 * b + 2 * g + i)

        block = ctx.enter_context(nc.Block())

        @block.sync
        def _(sp):
            sp.dma_start(ct_s[:], c_t.rearrange("(c p) b -> p c b", p=P)).then_inc(in_c, 16)
            sp.dma_start(wmod_s, wmod.rearrange("(c p) n -> p c n", p=P)).then_inc(in_mod, 16)
            sp.dma_start(x_s[:], x.rearrange("b (t p) d -> p (b t) d", p=P)).then_inc(in_x, 16)
            sp.dma_start(small_s[:], small).then_inc(in_small, 16)
            sp.dma_start(ident[:], masks[:, 2, :]).then_inc(in_small, 16)
            sp.dma_start(wk_s, wk.rearrange("(c p) n -> p c n", p=P)).then_inc(in_qkv, 16)
            sp.dma_start(wq_s, wq.rearrange("(c p) n -> p c n", p=P)).then_inc(in_qkv, 16)
            sp.dma_start(wv_s, wv.rearrange("(c p) n -> p c n", p=P)).then_inc(in_qkv, 16)
            sp.dma_start(rope_s[:], rope).then_inc(in_rope, 16)
            sp.dma_start(mask_in, masks).then_inc(in_mask, 16)
            sp.dma_start(wo_s, wo.rearrange("(h p) n -> p h n", p=P)).then_inc(in_wo, 16)
            sp.wait_ge(mod_rows, 4)
            sp.dma_start(mod_d, modr_s[:]).then_inc(mod_stored, 16)
            sp.dma_start(gate_s[:], gate_t.rearrange("(c p) n -> p c n", p=P)).then_inc(in_tail, 16)
            sp.dma_start(swg_s[:], sw_gate.rearrange("(c p) n -> p c n", p=P)).then_inc(in_tail, 16)
            sp.dma_start(swu_s[:], sw_up.rearrange("(c p) n -> p c n", p=P)).then_inc(in_tail, 16)
            sp.dma_start(swd_s[:, 0:2, :], sw_down[0:256, :].rearrange("(m p) n -> p m n", p=P)).then_inc(in_tail, 16)
            sp.dma_start(swd_s[0:SM[2], 2, :], sw_down[256:SHARED, :]).then_inc(in_tail, 16)
            sp.wait_ge(mod_stored, 16)
            sp.dma_start(mod_s[:], mod_d[0, :].partition_broadcast(P)).then_inc(in_modrow, 16)

            def load_slot(u, g):
                gu, wa, wb = slot(u)
                for m, w in enumerate((w_gate, w_up)):
                    sp.dma_start(gu[:, m].rearrange("p j c i -> p (j c i)"),
                                 w[bass.ds(g, 1)].rearrange("g p n -> (g p) n")).then_inc(in_gu[u], 16)
                sp.dma_start(wa.rearrange("p j d -> p (j d)"),
                             w_down_a[bass.ds(g, 1)].rearrange("g p n -> (g p) n")).then_inc(in_wd[u], 16)
                sp.dma_start(wb.rearrange("p j d -> p (j d)"),
                             w_down_b[bass.ds(g, 1)].rearrange("g p n -> (g p) n")).then_inc(in_wd[u], 16)

            load_slot(0, 0)
            sp.wait_ge(modt_mm, 1)
            load_slot(1, 1)
            with sp.Fori(1, BATCH) as b:
                sp.wait_ge(score_ready, b)
                sp.dma_start(rows_d[bass.ds((b - 1) * SEQ, SEQ), :].rearrange("(t p) n -> p t n", p=P),
                             row_s[:]).then_inc(row_stored, 16)
                sp.wait_ge(row_stored, 16 * b)
                sp.wait_ge(post_done, b)
                sp.dma_start(mod_s[:], mod_d[bass.ds(b, 1), :].rearrange("b n -> (b n)").partition_broadcast(P))\
                  .then_inc(in_modrow, 16)
            sp.wait_ge(pj_full, PJ_USES * (BATCH - 1) + PJ_ROPE[-1] + 1)
            load_slot(2, 2)
            sp.wait_ge(wo_full, BATCH)
            load_slot(3, 3)
            sp.dma_start(iota_s, iota_row.partition_broadcast(P)).then_inc(in_iota, 16)
            for b in range(BATCH):
                sp.dma_start(gb_all[:, b, :], mod_d[b, 3 * D:4 * D].partition_broadcast(P)).then_inc(in_gb, 16)
            sp.wait_ge(score_ready, BATCH)
            sp.dma_start(rows_d[(BATCH - 1) * SEQ:T, :].rearrange("(t p) n -> p t n", p=P),
                         row_s[:]).then_inc(row_stored, 16)
            with sp.Fori(1, GROUPS // RING) as k:
                for u in range(RING):
                    sp.wait_ge(y_full, RING * (k - 1) + u + 1)
                    load_slot(u, RING * k + u)
            for b in range(BATCH):
                sp.wait_ge(out_ready, b + 1)
                sp.dma_start(out[b].rearrange("(t p) d -> p t d", p=P), x_s[:, BT * b:BT * b + BT, :])\
                  .then_inc(out_stored, 16)
            sp.wait_ge(out_stored, 16 * BATCH)
            sp.wait_ge(row_stored, 16 * BATCH)

        @block.gpsimd
        def _(pool):
            nc.gpsimd.memset(half[:], -0.5).then_inc(sentinels, 1)
            nc.gpsimd.memset(lg[:, :, EXPERTS:], -BIG).then_inc(sentinels, 1)
            nc.gpsimd.memset(pick[:, :, TOPK:], -BIG).then_inc(sentinels, 1)
            nc.gpsimd.memset(zero_s[:], 0.0).then_inc(sentinels, 1)
            pool.wait_ge(sentinels, 1)
            with pool.Fori(0, BATCH) as b:
                pool.wait_ge(var1, b + 1)
                nc.gpsimd.tensor_tensor(rstd[:], var[:], half[:], ALU.pow).then_inc(rstd1, 1)
            pool.wait_ge(in_rope, 16)

            def sines(b, r):
                pool.wait_ge(swap_done, 10 * b + r + 1)
                sin = rope_s[:, 3 if r < 2 else 1, :]
                nc.gpsimd.tensor_tensor(swap_s[:, r % 2], swap_s[:, r % 2],
                                        sin.unsqueeze(1).to_broadcast([P, 2, SEQ]), ALU.mult).then_inc(sin_done, 1)

            def normalise(b, g):
                pool.wait_ge(rinv_done, 4 * b + g + 1)
                for probs, lo, s in ((prob_near, 0, P), (prob_far, GROUP, SEQ)):
                    last = nc.gpsimd.tensor_tensor(
                        probs[:, g % 2], probs[:, g % 2],
                        rinv[:, g % 2, lo:lo + GROUP].unsqueeze(2).to_broadcast([P, GROUP, s]), ALU.mult)
                last.then_inc(norm_done, 1)

            def row_step(b, tail):
                need(pool, pj_full, PJ_USES * (b - 1) + PJ_ROPE[-1] + 1)
                pool.wait_ge(xt_free, b + 1)
                nc.gpsimd.tensor_copy(h_cur[:], h_all[:, :, bass.ds(b * SEQ, SEQ)]).then_inc(h_ready, 1)
                sines(b, 0)
                sines(b, 1)
                if tail:
                    pool.wait_ge(var2, b)
                    nc.gpsimd.tensor_tensor(rstd[:], var[:], half[:], ALU.pow).then_inc(rstd2, 1)
                for r in range(2, 8):
                    sines(b, r)
                normalise(b, 0)
                sines(b, 8)
                sines(b, 9)
                for g in range(1, KV_HEADS):
                    normalise(b, g)

            row_step(0, False)
            with pool.Fori(1, BATCH) as b:
                row_step(b, True)
            pool.wait_ge(var2, BATCH)
            nc.gpsimd.tensor_tensor(rstd[:], var[:], half[:], ALU.pow).then_inc(rstd2, 1)

            pool.wait_ge(tok_ready, 1)
            pool.wait_ge(row_stored, 16 * BATCH)
            for g in range(GROUPS):
                if g >= 2:
                    pool.wait_ge(gt_full, g - 1)
                    pool.wait_ge(w_ready, g - 1)
                nc.gpsimd.indirect_dma_start(
                    rows_s[:, g % 2, :], None, rows_d, bass.IndirectOffsetOnAxis(tok_i[:, g:g + 1], axis=0),
                    bounds_check=T - 1, oob_is_err=False).then_inc(rows_in[g % 2], 16)

        @block.scalar
        def _(act):
            act.wait_ge(in_c, 16)
            nc.scalar.activation(ce_s[:], ct_s[:], ACT.Exp, scale=-1.0).then_inc(ce_ready, 1)

            def swap(b, r):
                act.wait_ge(cos_done, 10 * b + r + 1)
                need(act, rope_done, 10 * b + r - 1)
                src = pj[PJ_ROPE[r] % 2][:].rearrange("p (h s) -> p h s", h=2)
                nc.scalar.activation(swap_s[0:64, r % 2], src[64:128], ACT.Copy)
                nc.scalar.activation(swap_s[64:128, r % 2], src[0:64], ACT.Copy).then_inc(swap_done, 1)

            def values(b, t):
                act.wait_ge(pj_full, PJ_USES * b + PJ_V[t] + 1)
                nc.scalar.activation(v_s[:, t, :], pj[PJ_V[t] % 2][:], ACT.Copy).then_inc(v_out, 1)

            def exps(b, g):
                for i in range(3):
                    s = 3 * g + i
                    act.wait_ge(max_done, 12 * b + s + 1)
                    scores = sc[s % 2]
                    heads = range(GROUP) if i == 0 else (2 * i - 2, 2 * i - 1)
                    for n, h in enumerate(heads):
                        w = P if i == 0 else SEQ
                        col = h if i == 0 else GROUP + h
                        dst = prob_near if i == 0 else prob_far
                        last = nc.scalar.activation(dst[:, g % 2, h, :], scores[:, n * w:(n + 1) * w], ACT.Exp,
                                                    bias=nmax[:, g % 2, col:col + 1],
                                                    accum_out=psum_p[:, g % 2, col:col + 1])
                    last.then_inc(exp_done, 1)

            def take_far(b, g):
                for i in (1, 2):
                    act.wait_ge(tr_full, 12 * b + 3 * g + i + 1)
                    nc.scalar.activation(prob_t[:, i, :], tr[(3 * g + i) % 2][:], ACT.Copy).then_inc(trans_out12, 1)

            def take_mix(b, g):
                n = PJ_MIX[g][1]
                act.wait_ge(pj_full, PJ_USES * b + n + 1)
                nc.scalar.activation(mix_s[:, g % 2, 1, :], pj[n % 2][:], ACT.Copy).then_inc(mix_out1, 1)

            def router_exp(pb):
                act.wait_ge(nv_ready, pb + 1)
                for t in range(BT):
                    last = nc.scalar.activation(row_s[:, t, D:ROW], lg[:, t, 0:EXPERTS], ACT.Exp,
                                                bias=nv[:, t:t + 1], accum_out=sm[:, t:t + 1])
                last.then_inc(se_ready, 1)

            def shared_exp(pb, m, order):
                act.wait_ge(post_full, POST_USES * pb + order.index(f"gu{m}") + 1)
                nc.scalar.activation(eg_s[0:SM[m], :], post[0:SM[m], 0:SEQ], ACT.Exp, scale=-1.0)\
                  .then_inc(eg_ready, 1)

            def row_step(b, tail):
                swap(b, 0)
                swap(b, 1)
                swap(b, 2)
                swap(b, 3)
                values(b, 0)
                values(b, 1)
                swap(b, 4)
                if tail:
                    router_exp(b - 1)
                swap(b, 5)
                exps(b, 0)
                if tail:
                    shared_exp(b - 1, 0, IN_LOOP)
                swap(b, 6)
                swap(b, 7)
                exps(b, 1)
                if tail:
                    shared_exp(b - 1, 1, IN_LOOP)
                take_far(b, 0)
                take_mix(b, 0)
                swap(b, 8)
                swap(b, 9)
                exps(b, 2)
                if tail:
                    shared_exp(b - 1, 2, IN_LOOP)
                take_far(b, 1)
                take_mix(b, 1)
                exps(b, 3)
                take_far(b, 2)
                take_mix(b, 2)
                take_far(b, 3)
                take_mix(b, 3)

            row_step(0, False)
            with act.Fori(1, BATCH) as b:
                row_step(b, True)
            router_exp(BATCH - 1)
            for m in range(3):
                shared_exp(BATCH - 1, m, AT_END)

            def group_step(g, u, rows=True, ends=True):
                if rows:
                    act.wait_ge(gt_full, g + 1)
                    nc.scalar.activation(hb_t[:, u % 2], gt_bank[:, 0:DC * P].rearrange("p (c s) -> p c s", c=DC),
                                         ACT.Copy).then_inc(hb_ready, 1)
                if ends:
                    act.wait_ge(ht_full, g)
                    nc.scalar.activation(hid_ta, ht_bank[0:IA, 0:P], ACT.Copy)
                    nc.scalar.activation(hid_tb, ht_bank[0:IB, P:2 * P], ACT.Copy).then_inc(hid_t_ready, 1)
                if rows:
                    act.wait_ge(gu_full, g + 1)
                    nc.scalar.activation(eg_x, gu_bank[:, 0:INTER], ACT.Exp, scale=-1.0).then_inc(eg_x_ready, 1)
                if ends:
                    act.wait_ge(y_full, g)
                    act.wait_ge(w_ready, g)
                    v = (u + 1) % 2
                    need(act, back_done, g - 2)
                    nc.scalar.activation(y_hi[v][:], y_bank[:, 0:D], ACT.Copy, scale=w_slot[:, v:v + 1])\
                      .then_inc(hi_ready, 1)

            group_step(0, 0, ends=False)
            for u in range(1, RING):
                group_step(u, u)
            with act.Fori(1, GROUPS // RING) as k:
                for u in range(RING):
                    group_step(RING * k + u, u)
            group_step(GROUPS, 0, rows=False)

        @block.vector
        def _(dve):
            V = nc.vector
            pre = Steps(dve, pre_step, 0)
            dve.wait_ge(ce_ready, 1)
            pre.done(V.tensor_scalar(ce_s[:], ce_s[:], 1.0, None, ALU.add))
            pre.wait()
            pre.done(V.reciprocal(ce_s[:], ce_s[:]))
            pre.wait()
            V.tensor_tensor(ct_s[:], ct_s[:], ce_s[:], ALU.mult).then_inc(silu_c, 1)
            dve.wait_ge(modt_mm, 1)
            mt = tr[0][:, 0:16].rearrange("p (m c b) -> p m c b", m=2, c=DC)
            V.tensor_copy(modt_s[:, 0], mt[:, 0]).then_inc(modt_ready, 1)
            V.tensor_scalar(modt_s[:, 1], mt[:, 1], 1.0, None, ALU.add).then_inc(modt_ready, 1)
            dve.wait_ge(mod_mm, 2)
            V.tensor_copy(modr_s[:, D:2 * D], sc[0][0:BATCH, D:2 * D]).then_inc(mod_rows, 1)
            V.tensor_scalar(modr_s[:, 2 * D:3 * D], sc[1][0:BATCH, 0:D], 1.0, None, ALU.add).then_inc(mod_rows, 1)
            for i, (src, at) in enumerate(((sc[0][0:BATCH, 0:D], 0), (sc[1][0:BATCH, D:2 * D], 3))):
                sign, size = modq_s[:, 2 * i], modq_s[:, 2 * i + 1]
                pre.done(V.tensor_scalar(sign, src, 0.0, 2.0, ALU.is_ge, ALU.mult))
                pre.wait()
                pre.done(V.tensor_scalar(sign, sign, -1.0, None, ALU.add))
                pre.wait()
                pre.done(V.tensor_tensor(size, src, sign, ALU.mult))
                pre.wait()
                V.scalar_tensor_tensor(modr_s[:, at * D:(at + 1) * D], size, 0.25, sign, ALU.max, ALU.mult)\
                 .then_inc(mod_rows, 1)

            dve.wait_ge(in_x, 16)
            dve.wait_ge(modt_ready, 2)

            def norm_stats(step, tile0, var_sem):
                for t in range(BT):
                    last = V.bn_stats(stat[:, t, :], x_s[:, bass.ds(tile0 + t, 1), :].rearrange("p t d -> p (t d)"))
                step.done(last)
                step.wait()
                alone(dve, dve_passed)
                for t in range(BT):
                    last = V.bn_aggr(mv[:, t, :], stat[:, t, :])
                step.done(last)
                step.wait()
                V.tensor_scalar(var[:], mv[:, :, 1], EPS, None, ALU.add).then_inc(var_sem, 1)

            def norm_apply(dst, tile0, t):
                return V.tensor_scalar(dst, x_s[:, bass.ds(tile0 + t, 1), :].rearrange("p t d -> p (t d)"),
                                       mv[:, t, 0:1], rstd[:, t:t + 1], ALU.subtract, ALU.mult)

            with dve.Fori(0, BATCH) as b:
                step = Steps(dve, ln_step, b * 2)
                norm_stats(step, b * BT, var1)
                dve.wait_ge(rstd1, b + 1)
                for t in range(BT):
                    last = norm_apply(xn_s[:, t, :], b * BT, t)
                last.then_inc(xn_ready, 1)
                dve.wait_ge(xt_full, b + 1)
                xt = pj[0][:].rearrange("p (c s) -> p c s", c=DC)
                for c in range(DC):
                    last = V.tensor_scalar(h_all[:, c, bass.ds(b * SEQ, SEQ)], xt[:, c],
                                           modt_s[:, 1, c, bass.ds(b, 1)], modt_s[:, 0, c, bass.ds(b, 1)],
                                           ALU.mult, ALU.add)
                last.then_inc(xt_free, 1)

            dve.wait_ge(in_mask, 16)
            V.tensor_copy(mask_near[:], mask_in[:, 0].unsqueeze(1).to_broadcast([P, GROUP, P])).then_inc(consts, 1)
            V.tensor_copy(mask_far[:, :, 0], mask_in[:, 1].unsqueeze(1).to_broadcast([P, 2, P])).then_inc(consts, 1)
            V.tensor_copy(mask_far[:, :, 1], mask_in[:, 0].unsqueeze(1).to_broadcast([P, 2, P])).then_inc(consts, 1)
            V.tensor_copy(ident_b[:], mask_in[:, 2]).then_inc(consts, 1)
            dve.wait_ge(consts, 4)
            dve.wait_ge(in_rope, 16)

            def heads_of(r):
                return k_s[:, 2 * r:2 * r + 2] if r < 2 else q_s[:, (r // 2 - 1) % 2, 2 * (r % 2):2 * (r % 2) + 2]

            def cosines(b, r):
                dve.wait_ge(pj_full, PJ_USES * b + PJ_ROPE[r] + 1)
                cos = rope_s[:, 2 if r < 2 else 0, :].unsqueeze(1).to_broadcast([P, 2, SEQ])
                V.tensor_tensor(heads_of(r), pj[PJ_ROPE[r] % 2][:].rearrange("p (h s) -> p h s", h=2), cos,
                                ALU.mult).then_inc(cos_done, 1)

            def rotate(b, r):
                dve.wait_ge(sin_done, 10 * b + r + 1)
                dve.wait_ge(cos_done, 10 * b + r + 1)
                V.tensor_tensor(heads_of(r), heads_of(r), swap_s[:, r % 2], ALU.add).then_inc(rope_done, 1)

            def maxima(b, g):
                for i in range(3):
                    s = 3 * g + i
                    dve.wait_ge(sc_full, 12 * b + s + 1)
                    heads = GROUP if i == 0 else 2
                    lo = 0 if i == 0 else GROUP + 2 * (i - 1)
                    V.tensor_reduce(nmax[:, g % 2, lo:lo + heads], sc[s % 2][:].rearrange("p (h k) -> p h k", h=heads),
                                    AX_X, ALU.max, negate=True).then_inc(max_done, 1)

            def inverses(b, g):
                dve.wait_ge(exp_done, 12 * b + 3 * g + 3)
                V.reciprocal(rinv[:, g % 2], psum_p[:, g % 2]).then_inc(rinv_done, 1)

            def take_near(b, g):
                dve.wait_ge(tr_full, 12 * b + 3 * g + 1)
                V.tensor_copy(prob_t[:, 0, :], tr[(3 * g) % 2][:]).then_inc(trans_out0, 1)

            def take_mix(b, g):
                n = PJ_MIX[g][0]
                dve.wait_ge(pj_full, PJ_USES * b + n + 1)
                V.tensor_copy(mix_s[:, g % 2, 0, :], pj[n % 2][:]).then_inc(mix_out0, 1)

            class Tail:

                def __init__(self, pb, order):
                    self.pb, self.order, self.step = pb, order, Steps(dve, post_step, pb * POST_STEPS)
                    self.tiles = x_s[:, bass.ds(pb * BT, BT), :]

                def residual(self):
                    dve.wait_ge(wo_full, self.pb + 1)
                    dve.wait_ge(in_modrow, 16 * (self.pb + 1))
                    V.tensor_tensor(tmp_s[:], wo_bank[:].rearrange("p (t d) -> p t d", t=BT),
                                    mod_s[:, 0:D].unsqueeze(1).to_broadcast([P, BT, D]), ALU.mult)\
                     .then_inc(wo_free, 1)
                    dve.wait_ge(wo_free, self.pb + 1)
                    self.step.done(V.tensor_tensor(self.tiles, self.tiles, tmp_s[:], ALU.add))
                    self.step.wait()

                def stats(self):
                    norm_stats(self.step, self.pb * BT, var2)

                def rows(self):
                    dve.wait_ge(rstd2, self.pb + 1)
                    for t in range(BT):
                        last = norm_apply(row_s[:, t, 0:D], self.pb * BT, t)
                    self.step.done(last)
                    self.step.wait()
                    self.step.done(V.tensor_tensor(row_s[:, :, 0:D], row_s[:, :, 0:D],
                                                   mod_s[:, 2 * D:3 * D].unsqueeze(1).to_broadcast([P, BT, D]),
                                                   ALU.mult))
                    self.step.wait()
                    V.tensor_tensor(row_s[:, :, 0:D], row_s[:, :, 0:D],
                                    mod_s[:, D:2 * D].unsqueeze(1).to_broadcast([P, BT, D]), ALU.add)\
                     .then_inc(h2_ready, 1)

                def full(self, use):
                    dve.wait_ge(post_full, POST_USES * self.pb + self.order.index(use) + 1)

                def take_h(self):
                    self.full("h_t")
                    V.tensor_copy(h_t[:], post[:].rearrange("p (c s) -> p c s", c=DC)).then_inc(post_free, 1)

                def top6(self):
                    self.full("logits")
                    V.tensor_copy(lg[:, :, 0:EXPERTS], post[:, 0:BT * EXPERTS].rearrange("p (t e) -> p t e", t=BT))\
                     .then_inc(post_free, 1)
                    dve.wait_ge(post_free, POST_USES * self.pb + self.order.index("logits") + 1)
                    alone(dve, dve_passed)
                    for t in range(BT):
                        last = V.max(top[:, t, :], lg[:, t, 0:EXPERTS])
                    self.step.done(last)
                    self.step.wait()
                    V.tensor_scalar(nv[:], top[:, :, 0], -1.0, None, ALU.mult).then_inc(nv_ready, 1)
                    self.step.done(V.tensor_copy(pick[:, :, 0:TOPK], top[:, :, 0:TOPK]))
                    self.step.wait()
                    alone(dve, dve_passed)
                    for t in range(BT):
                        last = V.match_replace(rp[:, t, :], pick[:, t, :], lg[:, t, :], BIG)
                    self.step.done(last)
                    self.step.wait()
                    for t in range(BT):
                        last = V.tensor_scalar(key[:, t, :], rp[:, t, 0:EXPERTS], BIG / 2,
                                               rank[:, bass.ds(self.pb * BT + t, 1)], ALU.is_ge, ALU.mult)
                    last.then_inc(key_ready, 1)

                def scores(self):
                    dve.wait_ge(se_ready, self.pb + 1)
                    self.step.done(V.reciprocal(sm[:], sm[:]))
                    self.step.wait()
                    for t in range(BT):
                        last = V.tensor_scalar(row_s[:, t, D:ROW], row_s[:, t, D:ROW], sm[:, t:t + 1], None, ALU.mult)
                    last.then_inc(score_ready, 1)

                def shared_hidden(self, m):
                    dve.wait_ge(eg_ready, 3 * self.pb + m + 1)
                    n = SM[m]
                    self.step.done(V.tensor_scalar(eg_s[0:n], eg_s[0:n], 1.0, None, ALU.add))
                    self.step.wait()
                    self.step.done(V.reciprocal(eg_s[0:n], eg_s[0:n]))
                    self.step.wait()
                    self.step.done(V.tensor_tensor(tg_s[0:n], post[0:n, 0:SEQ], eg_s[0:n], ALU.mult))
                    self.step.wait()
                    V.tensor_tensor(sh_s[0:n, m], post[0:n, SEQ:2 * SEQ], tg_s[0:n], ALU.mult).then_inc(post_free, 1)

                def take_key(self):
                    self.full("key_t")
                    V.tensor_copy(key_all[:, bass.ds(self.pb * SEQ, SEQ)], post[0:EXPERTS, 0:SEQ])\
                     .then_inc(post_free, 1)

                def shared_out(self):
                    self.full("down")
                    V.tensor_tensor(tmp_s[:], post[:].rearrange("p (t d) -> p t d", t=BT),
                                    mod_s[:, 3 * D:4 * D].unsqueeze(1).to_broadcast([P, BT, D]), ALU.mult)\
                     .then_inc(post_free, 1)
                    dve.wait_ge(post_free, POST_USES * (self.pb + 1))
                    V.tensor_tensor(self.tiles, self.tiles, tmp_s[:], ALU.add).then_inc(post_done, 1)

            def row_step(b, tail):
                cosines(b, 0)
                if tail:
                    tail.residual()
                cosines(b, 1)
                if tail:
                    tail.stats()
                rotate(b, 0)
                cosines(b, 2)
                rotate(b, 1)
                if tail:
                    tail.rows()
                cosines(b, 3)
                rotate(b, 2)
                if tail:
                    tail.take_h()
                rotate(b, 3)
                cosines(b, 4)
                if tail:
                    tail.top6()
                cosines(b, 5)
                rotate(b, 4)
                if tail:
                    tail.scores()
                rotate(b, 5)
                maxima(b, 0)
                if tail:
                    tail.shared_hidden(0)
                cosines(b, 6)
                cosines(b, 7)
                rotate(b, 6)
                rotate(b, 7)
                inverses(b, 0)
                maxima(b, 1)
                if tail:
                    tail.shared_hidden(1)
                take_near(b, 0)
                take_mix(b, 0)
                if tail:
                    tail.take_key()
                cosines(b, 8)
                cosines(b, 9)
                rotate(b, 8)
                rotate(b, 9)
                inverses(b, 1)
                maxima(b, 2)
                if tail:
                    tail.shared_hidden(2)
                take_near(b, 1)
                take_mix(b, 1)
                inverses(b, 2)
                maxima(b, 3)
                if tail:
                    tail.shared_out()
                take_near(b, 2)
                take_mix(b, 2)
                inverses(b, 3)
                take_near(b, 3)
                take_mix(b, 3)

            row_step(0, None)
            with dve.Fori(1, BATCH) as b:
                tail = Tail(b - 1, IN_LOOP)
                row_step(b, tail)
                assert tail.step.n == POST_STEPS, tail.step.n
            tail = Tail(BATCH - 1, AT_END)
            tail.residual()
            tail.stats()
            tail.rows()
            tail.take_h()
            tail.top6()
            tail.take_key()
            step = Steps(dve, tok_step, 0)
            dve.wait_ge(post_free, POST_USES * (BATCH - 1) + 3)
            cur, nxt = key_all[:], key_b
            for r in range(CAP // 8):
                step.done(V.max(first[:, 8 * r:8 * r + 8], cur))
                step.wait()
                if r < CAP // 8 - 1:
                    step.done(V.match_replace(nxt, first[:, 8 * r:8 * r + 8], cur, -1.0))
                    step.wait()
                    cur, nxt = nxt, cur
            V.tensor_scalar(tok_e[:], first[:], -1.0, float(T), ALU.mult, ALU.add).then_inc(tok_e_ready, 1)
            tail.scores()
            dve.wait_ge(tok_t, 1)
            for j in range(PER):
                last = V.tensor_copy(tok[CAP * j:CAP * j + CAP, :],
                                     tr[0][0:CAP, 0:EXPERTS].rearrange("p (g j) -> p g j", j=PER)[:, :, j])
            step.done(last)
            step.wait()
            step.done(V.tensor_scalar(tok_f[:], tok[:], float(T - 1), None, ALU.min))
            step.wait()
            V.tensor_copy(tok_i[:], tok_f[:]).then_inc(tok_ready, 1)
            for m in range(3):
                tail.shared_hidden(m)
            tail.shared_out()
            assert tail.step.n == POST_STEPS
            dve.wait_ge(in_iota, 16)

            def group_step(g, u, rows=True, ends=True, count=None):
                ex = Steps(dve, exp_step, EXP_STEPS * g)
                if rows:
                    v = u % 2
                    need(dve, back_done, g - 1)
                    col = tok[:, bass.ds(g, 1)]
                    V.tensor_scalar(place[v][:], iota_s, col, None, ALU.is_equal).then_inc(place_ready, 1)
                    dve.wait_ge(rows_in[v], count)
                    ex.done(V.tensor_tensor(w_tmp, rows_s[:, v, bass.ds(PER * g + D, PER)], quad, ALU.mult))
                    ex.wait()
                    need(dve, hi_ready, g - 1)
                    V.tensor_reduce(w_slot[:, v:v + 1], w_tmp, AX_X, ALU.add).then_inc(w_ready, 1)
                    dve.wait_ge(eg_x_ready, g + 1)
                    ex.done(V.tensor_scalar(eg_x, eg_x, 1.0, None, ALU.add))
                    ex.wait()
                    ex.done(V.reciprocal(eg_x, eg_x))
                    ex.wait()
                    ex.done(V.tensor_tensor(tg_x, gu_bank[:, 0:INTER], eg_x, ALU.mult))
                    ex.wait()
                    need(dve, ht_full, g)
                    V.tensor_tensor(hid_x, gu_bank[:, INTER:2 * INTER], tg_x, ALU.mult).then_inc(hid_ready, 1)
                if ends:
                    v = (u + 1) % 2
                    dve.wait_ge(hi_ready, g)
                    V.scalar_tensor_tensor(y_lo[v][:], y_bank[:, 0:D], w_slot[:, v:v + 1], y_hi[v][:].bitcast(F32),
                                           ALU.mult, ALU.subtract).then_inc(lo_ready, 1)

            for u in range(RING):
                group_step(u, u, ends=u > 0, count=16 * (u // 2 + 1))
            with dve.Fori(1, GROUPS // RING) as k:
                for u in range(RING):
                    group_step(RING * k + u, u, count=RING * 8 * k + 16 * (u // 2 + 1))
            group_step(GROUPS, 0, rows=False)

            dve.wait_ge(in_gb, 16 * BATCH)
            dve.wait_ge(back_done, GROUPS)
            dve.wait_ge(post_done, BATCH)
            for b in range(BATCH):
                step.done(V.tensor_tensor(tmp_s[:], acc[b][:].rearrange("p (t d) -> p t d", t=BT),
                                          gb_all[:, b, :].unsqueeze(1).to_broadcast([P, BT, D]), ALU.mult))
                step.wait()
                tiles = x_s[:, BT * b:BT * b + BT, :]
                V.tensor_tensor(tiles, tiles, tmp_s[:], ALU.add).then_inc(out_ready, 1)
                dve.wait_ge(out_ready, b + 1)

        @block.tensor
        def _(pe):
            mm = nc.tensor.matmul
            pe.wait_ge(in_mod, 16)
            pe.wait_ge(silu_c, 1)
            for m in range(2):
                for c2 in range(DC):
                    at = (m * DC + c2) * BATCH
                    for c in range(DC):
                        last = mm(tr[0][:, at:at + BATCH], wmod_s[:, c, m * D + c2 * P:m * D + c2 * P + P],
                                  ct_s[:, c, :], start=(c == 0), stop=(c == DC - 1))
            for m in range(2):
                for c in range(DC):
                    last2 = mm(sc[m][0:BATCH, :], ct_s[:, c, :], wmod_s[:, c, 512 * (m + 1):512 * (m + 2)],
                               start=(c == 0), stop=(c == DC - 1))
                last2.then_inc(mod_mm, 1)
            last.then_inc(modt_mm, 1)
            pe.wait_ge(in_small, 32)
            with pe.Fori(0, BATCH) as b:
                pe.wait_ge(xn_ready, b + 1)
                for c in range(DC):
                    for t in range(BT):
                        last = nc.tensor.transpose(pj[0][:, c * SEQ + t * P:c * SEQ + t * P + P],
                                                   xn_s[:, t, c * P:c * P + P], ident[:])
                last.then_inc(xt_full, 1)
            pe.wait_ge(in_qkv, 48)
            pe.wait_ge(xt_free, BATCH)
            pe.wait_ge(consts, 4)
            pe.wait_ge(mod_rows, 4)

            def pj_take(b, n):
                need(pe, *(pj_release(b, n - 2) if n >= 2 else pj_release(b - 1, n + PJ_USES - 2)))
                return pj[n % 2]

            def project(b, r):
                dst = pj_take(b, PJ_ROPE[r])
                for i in range(2):
                    w = wk_s if r < 2 else wq_s
                    h = 2 * r + i if r < 2 else 2 * (r - 2) + i
                    for c in range(DC):
                        last = mm(dst[:, i * SEQ:(i + 1) * SEQ], w[:, c, h * HD:(h + 1) * HD], h_cur[:, c, :],
                                  start=(c == 0), stop=(c == DC - 1))
                last.then_inc(pj_full, 1)

            def project_v(b, t):
                dst = pj_take(b, PJ_V[t])
                for c in range(DC):
                    last = mm(dst[:], h_cur[:, c, t * P:(t + 1) * P], wv_s[:, c, :], start=(c == 0), stop=(c == DC - 1))
                last.then_inc(pj_full, 1)

            def score(b, g):
                pe.wait_ge(rope_done, 10 * b + 2 * g + 4)
                for i in range(3):
                    s = 3 * g + i
                    need(pe, exp_done, 12 * b + s - 1)
                    dst = sc[s % 2]
                    if i == 0:
                        mm(dst[:], ident_b[:], mask_near[:].rearrange("p h k -> p (h k)"), start=True, stop=True)
                        for h in range(GROUP):
                            last = mm(dst[:, h * P:(h + 1) * P], q_s[:, g % 2, h, 0:P], k_s[:, g, 0:P],
                                      start=False, stop=True, skip_group_check=True)
                    else:
                        mm(dst[:], ident_b[:], mask_far[:].rearrange("p h m k -> p (h m k)"), start=True, stop=True)
                        for n in range(2):
                            last = mm(dst[:, n * SEQ:(n + 1) * SEQ], q_s[:, g % 2, 2 * (i - 1) + n, P:SEQ], k_s[:, g, :],
                                      start=False, stop=True, skip_group_check=True)
                    last.then_inc(sc_full, 1)

            def transpose_probs(b, g):
                pe.wait_ge(norm_done, 4 * b + g + 1)
                for i in range(3):
                    n = 3 * g + i
                    need(pe, *(tr_release(b, n - 2) if n >= 2 else tr_release(b - 1, n + 10)))
                    for h in range(GROUP):
                        src = (prob_near[:, g % 2, h, :] if i == 0
                               else prob_far[:, g % 2, h, (i - 1) * P:i * P])
                        last = nc.tensor.transpose(tr[n % 2][:, h * P:(h + 1) * P], src, ident[:])
                    last.then_inc(tr_full, 1)

            def mix(b, g):
                v = [v_s[:, t, g * HD:(g + 1) * HD] for t in range(BT)]
                pe.wait_ge(v_out, 2 * b + 2)
                dst = pj_take(b, PJ_MIX[g][0])
                pe.wait_ge(trans_out0, 4 * b + g + 1)
                mm(dst[:], v[0], prob_t[:, 0, :], start=True, stop=True).then_inc(pj_full, 1)
                dst = pj_take(b, PJ_MIX[g][1])
                pe.wait_ge(trans_out12, 8 * b + 2 * g + 2)
                mm(dst[:], v[0], prob_t[:, 1, :], start=True, stop=False)
                mm(dst[:], v[1], prob_t[:, 2, :], start=False, stop=True).then_inc(pj_full, 1)

            def project_out(b, g):
                if g == 0:
                    need(pe, wo_free, b)
                    pe.wait_ge(in_wo, 16)
                for t, out_sem in enumerate((mix_out0, mix_out1)):
                    pe.wait_ge(out_sem, 4 * b + g + 1)
                    for h in range(GROUP):
                        last = mm(wo_bank[:, t * D:(t + 1) * D], mix_s[:, g % 2, t, h * P:(h + 1) * P],
                                  wo_s[:, GROUP * g + h, :], start=(g == 0 and t == 0 and h == 0),
                                  stop=(g == KV_HEADS - 1 and h == GROUP - 1), skip_group_check=True)
                if g == KV_HEADS - 1:
                    last.then_inc(wo_full, 1)

            class Tail:

                def __init__(self, pb, order):
                    self.pb, self.order = pb, order

                def take(self, use):
                    need(pe, post_free, POST_USES * self.pb + self.order.index(use))

                def rows_t(self):
                    pe.wait_ge(h2_ready, self.pb + 1)
                    for c in range(DC):
                        for t in range(BT):
                            last = nc.tensor.transpose(post[:, c * SEQ + t * P:c * SEQ + t * P + P],
                                                       row_s[:, t, c * P:c * P + P], ident[:])
                    last.then_inc(post_full, 1)

                def logits(self):
                    self.take("logits")
                    for t in range(BT):
                        for c in range(DC):
                            last = mm(post[:, t * EXPERTS:(t + 1) * EXPERTS], h_t[:, c, t * P:(t + 1) * P],
                                      gate_s[:, c, :], start=(c == 0), stop=(c == DC - 1))
                    last.then_inc(post_full, 1)

                def gate_up(self, m):
                    self.take(f"gu{m}")
                    n = SM[m]
                    for i, w in enumerate((swg_s, swu_s)):
                        for c in range(DC):
                            last = mm(post[0:n, i * SEQ:(i + 1) * SEQ], w[:, c, m * P:m * P + n], h_t[:, c, :],
                                      start=(c == 0), stop=(c == DC - 1))
                    last.then_inc(post_full, 1)

                def keys_t(self):
                    self.take("key_t")
                    pe.wait_ge(key_ready, self.pb + 1)
                    alone(pe, pe_passed)
                    for t in range(BT):
                        last = nc.tensor.transpose(post[0:EXPERTS, t * P:(t + 1) * P], key[:, t, :], ident[:])
                    last.then_inc(post_full, 1)

                def down(self):
                    self.take("down")
                    for t in range(BT):
                        for m, n in enumerate(SM):
                            last = mm(post[:, t * D:(t + 1) * D], sh_s[0:n, m, t * P:(t + 1) * P], swd_s[0:n, m, :],
                                      start=(m == 0), stop=(m == 2))
                    last.then_inc(post_full, 1)

            def row_step(b, tail):
                pe.wait_ge(h_ready, b + 1)
                project(b, 0)
                project(b, 1)
                project(b, 2)
                project(b, 3)
                if tail:
                    tail.rows_t()
                project_v(b, 0)
                project_v(b, 1)
                if tail:
                    tail.logits()
                project(b, 4)
                project(b, 5)
                score(b, 0)
                if tail:
                    tail.gate_up(0)
                project(b, 6)
                project(b, 7)
                score(b, 1)
                if tail:
                    tail.gate_up(1)
                transpose_probs(b, 0)
                mix(b, 0)
                project_out(b, 0)
                if tail:
                    tail.keys_t()
                project(b, 8)
                project(b, 9)
                score(b, 2)
                if tail:
                    tail.gate_up(2)
                transpose_probs(b, 1)
                mix(b, 1)
                project_out(b, 1)
                score(b, 3)
                if tail:
                    tail.down()
                transpose_probs(b, 2)
                mix(b, 2)
                project_out(b, 2)
                transpose_probs(b, 3)
                mix(b, 3)
                project_out(b, 3)

            row_step(0, None)
            pe.wait_ge(in_tail, 80)
            with pe.Fori(1, BATCH) as b:
                row_step(b, Tail(b - 1, IN_LOOP))
            tail = Tail(BATCH - 1, AT_END)
            for n, a in enumerate(acc):
                need(pe, *(pj_release(BATCH - 1, PJ_USES - 2 + n) if n < 2 else (exp_done, 12 * BATCH)))
                mm(a[:], zero_s[:, 0:P], zero_s[:], start=True, stop=True, skip_group_check=True)
            tail.rows_t()
            tail.logits()
            tail.keys_t()
            pe.wait_ge(tok_e_ready, 1)
            need(pe, *tr_release(BATCH - 1, 10))
            nc.tensor.transpose(tr[0][0:CAP, 0:EXPERTS], tok_e[:], ident[0:EXPERTS, 0:EXPERTS]).then_inc(tok_t, 1)
            for m in range(3):
                tail.gate_up(m)
            tail.down()

            def group_step(g, u, rows=True, ends=True, back=True, count=None, fills=None):
                gu, wa, wb = slot(u)
                if rows:
                    pe.wait_ge(rows_in[u % 2], count)
                    need(pe, hb_ready, g)
                    if isinstance(g, int) and g == 0:
                        pe.wait_ge(tok_ready, 1)
                    for c in range(DC):
                        last = nc.tensor.transpose(gt_bank[:, c * P:(c + 1) * P], rows_s[:, u % 2, c * P:(c + 1) * P],
                                                   ident[:])
                    last.then_inc(gt_full, 1)
                if ends:
                    pe.wait_ge(hid_ready, g)
                    need(pe, hid_t_ready, g - 1)
                    nc.tensor.transpose(ht_bank[0:IA, 0:P], hid_x[:, 0:IA], ident[:])
                    nc.tensor.transpose(ht_bank[0:IB, P:2 * P], hid_x[:, IA:INTER], ident[:]).then_inc(ht_full, 1)
                if back:
                    v = u % 2
                    pe.wait_ge(lo_ready, g - 1)
                    pe.wait_ge(place_ready, g - 1)
                    for t in range(TT):
                        at = acc[t // BT][:, (t % BT) * D:(t % BT + 1) * D]
                        for part in (y_hi[v], y_lo[v]):
                            last = mm(at, place[v][:, t * P:(t + 1) * P], part[:], start=False, stop=True,
                                      skip_group_check=True)
                    last.then_inc(back_done, 1)
                if rows:
                    pe.wait_ge(hb_ready, g + 1)
                    need(pe, hid_ready, g)
                    pe.wait_ge(in_gu[u], fills)
                    for c in range(DC):
                        for j in range(PER):
                            last = mm(gu_bank[CAP * j:CAP * (j + 1), 0:2 * INTER],
                                      hb_t[:, u % 2, c, CAP * j:CAP * (j + 1)], gu[:, :, j, c, :],
                                      start=(c == 0), stop=(c == DC - 1))
                    last.then_inc(gu_full, 1)
                if ends:
                    gu, wa, wb = slot((u - 1) % RING)
                    pe.wait_ge(hid_t_ready, g)
                    need(pe, lo_ready, g - 1)
                    pe.wait_ge(in_wd[(u - 1) % RING], fills if u > 0 else fills - 32)
                    for i, (hid, w) in enumerate(((hid_ta, wa), (hid_tb, wb))):
                        for j in range(PER):
                            last = mm(y_bank[CAP * j:CAP * (j + 1), 0:D], hid[:, CAP * j:CAP * (j + 1)], w[:, j, :],
                                      start=(i == 0), stop=(i == 1))
                    last.then_inc(y_full, 1)

            pe.wait_ge(post_free, POST_USES * BATCH)
            pe.wait_ge(wo_free, BATCH)
            need(pe, *tr_release(BATCH - 1, 11))
            for u in range(RING):
                group_step(u, u, ends=u > 0, back=u > 1, count=16 * (u // 2 + 1), fills=32)
            with pe.Fori(1, GROUPS // RING) as k:
                for u in range(RING):
                    group_step(RING * k + u, u, count=RING * 8 * k + 16 * (u // 2 + 1), fills=32 * k + 32)
            group_step(GROUPS, 0, rows=False, fills=32 * (GROUPS // RING) + 32)
            group_step(GROUPS + 1, 1, rows=False, ends=False)


def kernel(L0_attn_x, L0_attn_wq, L0_attn_wk, L0_attn_wv, L0_attn_wo, L0_ffn_gate_w, L0_ffn_w_gate, L0_ffn_w_up,
           L0_ffn_w_down, L0_ffn_sw_gate, L0_ffn_sw_up, L0_ffn_sw_down, L0_c, L0_wmod):
    import numpy as np
    import concourse.bacc as bacc
    from concourse.bass_utils import run_bass_kernel_spmd

    f32 = np.float32

    def halves(w, heads):
        return np.ascontiguousarray(np.asarray(w).reshape(D, heads, HD // 2, 2).transpose(0, 1, 3, 2).reshape(D, -1))

    def by_group(w):
        w = np.asarray(w).reshape(GROUPS, PER, DC, P, INTER)
        return np.ascontiguousarray(w.transpose(0, 3, 1, 2, 4)).reshape(GROUPS, P, PER * DC * INTER)

    down = np.asarray(L0_ffn_w_down).reshape(GROUPS, PER, INTER, D).transpose(0, 2, 1, 3)

    inv = (1.0 / np.power(f32(10000.0), np.arange(0, HD, 2, dtype=f32) / f32(HD))).astype(f32)
    ang = np.outer(np.arange(SEQ, dtype=f32), inv).astype(f32).T
    cos, sin = np.cos(ang).astype(f32), np.sin(ang).astype(f32)
    cos2, sin2 = np.concatenate([cos, cos]), np.concatenate([-sin, sin])
    scale = f32(1.0 / np.sqrt(f32(HD)))
    rope = np.stack([cos2 * scale, sin2 * scale, cos2, sin2], axis=1).astype(f32)
    qi, ki = np.arange(P)[:, None], np.arange(P)[None, :]
    masks = np.stack([np.where(ki <= qi, 0.0, -1e30), np.where(ki >= qi, 0.0, -1e30), np.eye(P)], axis=1).astype(f32)
    rank = T - (np.arange(TT)[None, :] * P + np.arange(P)[:, None])
    quad = np.arange(P)[:, None] // CAP == np.arange(PER)[None, :]
    small = np.concatenate([rank, quad], axis=1).astype(f32)

    arrays = {
        "x": np.asarray(L0_attn_x), "c_t": np.asarray(L0_c).T, "wmod": np.asarray(L0_wmod),
        "wq": halves(L0_attn_wq, HEADS), "wk": halves(L0_attn_wk, KV_HEADS), "wv": np.asarray(L0_attn_wv),
        "wo": np.asarray(L0_attn_wo), "gate_t": np.asarray(L0_ffn_gate_w).T,
        "w_gate": by_group(L0_ffn_w_gate), "w_up": by_group(L0_ffn_w_up),
        "w_down_a": down[:, 0:IA].reshape(GROUPS, IA, PER * D), "w_down_b": down[:, IA:].reshape(GROUPS, IB, PER * D),
        "sw_gate": np.asarray(L0_ffn_sw_gate), "sw_up": np.asarray(L0_ffn_sw_up),
        "sw_down": np.asarray(L0_ffn_sw_down), "rope": rope, "masks": masks, "small": small,
        "iota_row": np.arange(T, dtype=f32),
    }
    nc = bacc.Bacc("TRN2", target_bir_lowering=False, num_devices=1)
    ins, given = [], {}
    for name, a in arrays.items():
        a = np.ascontiguousarray(a)
        given[f"in_{name}"] = a
        ins.append(nc.dram_tensor(f"in_{name}", a.shape, mybir.dt.from_np(a.dtype), kind="ExternalInput").ap())
    res = nc.dram_tensor("out_0", (BATCH, SEQ, D), F32, kind="ExternalOutput").ap()
    bass_adaln_attention_moe(nc, *ins, res)
    r = run_bass_kernel_spmd(nc, [given], core_ids=[0])
    return r.results[0]["out_0"]
```

```python
from contextlib import ExitStack

import concourse.bass as bass
from concourse import mybir
from concourse.alu_op_type import AluOpType as ALU

ACT = mybir.ActivationFunctionType
F32 = mybir.dt.float32
F32R = mybir.dt.float32r
BF16 = mybir.dt.bfloat16
U32 = mybir.dt.uint32
AX_X = mybir.AxisListType.X

P = 128
BATCH, SEQ, D = 4, 256, 256
HEADS, KV_HEADS, HD = 16, 4, 128
GROUP = HEADS // KV_HEADS
EXPERTS, TOPK, CAP = 64, 6, 32
INTER, SHARED = 176, 352
T = BATCH * SEQ
TT = T // P
DC = D // P
BT = SEQ // P
EPS = 1e-5
PER = P // CAP
GROUPS = EXPERTS // PER
IA, IB = 96, 80
SM = [128, 128, 96]
RING = 6
ROW = D + EXPERTS
PEELED = GROUPS % RING
ROUNDS = GROUPS // RING
BIG = 3.0e38

PASSES = [(0, 0), (0, 1), (1, 0)]
CHUNK = 1024
CH_K, CH_V, CH_Q, CH_O = 0, 2, [1, 3, 4, 5], [6, 7, 8, 9]
CHUNKS = 10

PJ_ROPE = [0, 1, 2, 3, 6, 7, 8, 9, 10, 11]
PJ_V = [4, 5]
PJ_MIX = [(12, 13), (14, 15), (16, 17), (18, 19)]
PJ_USES = 20
WORK_SCORE = [0, 1, 2, 3, 4, 5, 9, 10, 11, 15, 16, 17]
WORK_TRANS = [6, 7, 8, 12, 13, 14, 18, 19, 20, 21, 22, 23]
WORK_USES = 24
IN_LOOP = ["h_t", "logits", "gu0", "gu1", "key_t", "gu2", "down"]
AT_END = ["h_t", "logits", "key_t", "tok_t", "down"]
POST_USES = len(IN_LOOP)


def need(eng, sem, value):
    if not isinstance(value, int) or value > 0:
        eng.wait_ge(sem, value)


def alone(eng, passed):
    eng.sem_inc(passed)


class Steps:

    def __init__(self, eng, sem, base):
        self.eng, self.sem, self.base, self.n = eng, sem, base, 0

    def done(self, ins):
        self.n += 1
        ins.then_inc(self.sem, 1)

    def wait(self):
        self.eng.wait_ge(self.sem, self.base + self.n)


def bass_adaln_attention_moe(nc, x, c_t, wmod, wq, wk, wv, wo, gate_t, w_gate, w_up, w_down_a, w_down_b,
                             sw_gate, sw_up, sw_down, rope, masks, small, iota_row, out):
    ctx = ExitStack()
    with ctx:
        def sb(name, shape, dt=F32):
            return ctx.enter_context(nc.sbuf_tensor(name, shape, dt))

        def sem(name):
            return ctx.enter_context(nc.semaphore(name))

        bank = [ctx.enter_context(nc.psum_tensor(f"bank{i}", [P, 512], F32)) for i in range(8)]
        pj, work, wo_bank, post = bank[0:2], bank[2:6], bank[6], bank[7]
        acc, gt_bank, ht_bank, gu_bank, y_bank = bank[0:4], bank[4], bank[5], bank[6], bank[7]
        end_bank = bank[4:7]

        SLOT = 2 * PER * DC * INTER + 2 * PER * D
        with nc.sbuf_tensor("weights", [P, CHUNKS * 2 * CHUNK], F32R) as weights:
            pass
        slots = sb("slots", [P, CHUNKS * 2 * CHUNK])
        wmod_at = CH_O[0] * 2 * CHUNK
        wmod_s = slots[:, wmod_at:wmod_at + 3072].rearrange("p (c n) -> p c n", c=DC)

        def chunk(k):
            return weights[:, k * 2 * CHUNK:(k + 1) * 2 * CHUNK].rearrange("p (r n) -> p r n", r=2)

        def by_feature(k):
            return chunk(k).rearrange("p r (c n) -> p r c n", c=DC)

        def slot(u):
            base = slots[:, u * SLOT:(u + 1) * SLOT] if u < 4 else late[:, (u - 4) * SLOT:(u - 3) * SLOT]
            n = PER * DC * INTER
            gu = base[:, 0:2 * n].rearrange("p (m j c i) -> p m j c i", m=2, j=PER, c=DC)
            wa = base[0:IA, 2 * n:2 * n + PER * D].rearrange("p (j d) -> p j d", j=PER)
            wb = base[0:IB, 2 * n + PER * D:SLOT].rearrange("p (j d) -> p j d", j=PER)
            return gu, wa, wb

        LATE = 4000
        area = sb("area", [P, LATE + 2 * SLOT])
        late = area[:, LATE:LATE + 2 * SLOT]
        q_s = area[:, 0:2048].rearrange("p (g h s) -> p g h s", g=2, h=GROUP)
        prob_near = area[:, 2048:3072].rearrange("p (g h s) -> p g h s", g=2, h=GROUP)
        prob_far = area[:, 3072:5120].rearrange("p (g h s) -> p g h s", g=2, h=GROUP)
        h_all = area[:, 5120:7168].rearrange("p (c s) -> p c s", c=DC)
        k_s = area[:, 7168:8192].rearrange("p (h s) -> p h s", h=KV_HEADS)
        v_s = area[:, 8192:9216].rearrange("p (t n) -> p t n", t=BT)
        prob_t = area[:, 9216:10752].rearrange("p (i n) -> p i n", i=3)
        swap_s = area[:, 10752:11776].rearrange("p (g h s) -> p g h s", g=2, h=2)
        rope_s = area[:, 11776:12800].rearrange("p (i s) -> p i s", i=4)
        mask_in = area[:, 4096:4480].rearrange("p (m k) -> p m k", m=3)
        iota_s = area[:, 0:1024]
        hb_t = area[:, 1024:1536].rearrange("p (g c s) -> p g c s", g=2, c=DC)
        rows_s = area[:, 1536:2176].rearrange("p (g n) -> p g n", g=2)
        eg_x = area[:, 2176:2352]
        tg_x = area[:, 2352:2528]
        hid_x = area[:, 2528:2704]
        hid_ta = area[0:IA, 2704:2832]
        hid_tb = area[0:IB, 2832:2960]
        gb_all = area[:, 2960:3984].rearrange("p (b d) -> p b d", b=BATCH)
        w_tmp = area[:, 3984:3988]
        split_s = sb("split_s", [P, 4096], F32R)
        mix_s = split_s[:].rearrange("p (g t r n) -> p g t r n", g=2, t=BT, r=2)
        place = [split_s[:, i * T:(i + 1) * T] for i in range(2)]
        y_hi = [split_s[:, (8 + i) * D:(9 + i) * D] for i in range(2)]
        y_lo = [split_s[:, (10 + i) * D:(11 + i) * D] for i in range(2)]
        x_s = sb("x_s", [P, TT, D])
        h_cur = sb("h_cur", [P, 2, DC, SEQ], F32R)
        mod_s = sb("mod_s", [P, 4 * D])
        mask_near = sb("mask_near", [P, GROUP, P], BF16)
        mask_far = sb("mask_far", [P, 2, 2, P], BF16)
        ident_b = sb("ident_b", [P, P], BF16)
        ident = sb("ident", [P, P])
        gate_s = sb("gate_s", [P, DC, EXPERTS])
        swg_s = sb("swg_s", [P, DC, SHARED])
        swu_s = sb("swu_s", [P, DC, SHARED])
        swd_s = sb("swd_s", [P, 3, D])
        small_s = sb("small_s", [P, TT + PER])
        rank = small_s[:, 0:TT]
        quad = small_s[:, TT:TT + PER]
        row_s = sb("row_s", [P, BT, ROW])
        xn_s = row_s[:, :, 0:D]
        h_t = sb("h_t", [P, DC, SEQ])
        modr_s = mod_s[0:BATCH, :]
        modq_s = h_t[0:BATCH]
        tail_s = sb("tail_s", [P, 2 * CHUNK])
        stage = [tail_s[:, i * CHUNK:(i + 1) * CHUNK] for i in range(2)]
        sh_s = tail_s[:, 0:3 * SEQ].rearrange("p (m s) -> p m s", m=3)
        eg_s = tail_s[:, 3 * SEQ:5 * SEQ].rearrange("p (m s) -> p m s", m=2)
        tg_s = tail_s[:, 5 * SEQ:6 * SEQ]
        tmp_s = tail_s[:, 6 * SEQ:8 * SEQ].rearrange("p (t d) -> p t d", t=BT)
        cand = [sb(f"cand{i}", [EXPERTS, CAP + SEQ]) for i in range(2)]
        ct_s = sb("ct_s", [P, DC, BATCH])
        ce_s = sb("ce_s", [P, DC, BATCH])
        modt_s = sb("modt_s", [P, 2, DC, BATCH])
        stat = sb("stat", [P, BT, 6])
        mv = sb("mv", [P, BT, 2])
        var = sb("var", [P, BT])
        half = sb("half", [P, BT])
        rstd = sb("rstd", [P, BT])
        nmax = sb("nmax", [P, 2, 8])
        psum_p = sb("psum_p", [P, 2, 8])
        rinv = sb("rinv", [P, 2, 8])
        lg = sb("lg", [P, BT, EXPERTS + 2])
        rp = sb("rp", [P, BT, EXPERTS + 2])
        top = sb("top", [P, BT, 8])
        pick = sb("pick", [P, BT, 8])
        nv = sb("nv", [P, BT])
        sm = sb("sm", [P, BT])
        key = sb("key", [P, BT, EXPERTS])
        first = sb("first", [EXPERTS, CAP])
        tok_e = sb("tok_e", [EXPERTS, CAP])
        tok = sb("tok", [P, GROUPS])
        tok_f = sb("tok_f", [P, GROUPS])
        tok_i = sb("tok_i", [P, GROUPS], U32)
        w_slot = sb("w_slot", [P, 2])
        zero_s = sb("zero_s", [P, 512], BF16)

        mod_d = nc.dram_tensor("mod_d", (BATCH, 4 * D), F32, kind="Internal").ap()
        rows_d = nc.dram_tensor("rows_d", (T, ROW), F32, kind="Internal").ap()

        in_c, in_x0, in_x, in_mod_t, in_mod, in_small = (sem("in_c"), sem("in_x0"), sem("in_x"), sem("in_mod_t"),
                                                         sem("in_mod"), sem("in_small"))
        in_rope, in_mask, in_tail = sem("in_rope"), sem("in_mask"), sem("in_tail")
        in_stage = [sem("in_stage0"), sem("in_stage1")]
        w_hi_ready, w_lo_ready, h_hi_ready = sem("w_hi_ready"), sem("w_lo_ready"), sem("h_hi_ready")
        mix_hi0, mix_hi1 = sem("mix_hi0"), sem("mix_hi1")
        in_iota, in_gb, in_modrow = sem("in_iota"), sem("in_gb"), sem("in_modrow")
        in_gu = [sem(f"in_gu{u}") for u in range(RING)]
        in_wd = [sem(f"in_wd{u}") for u in range(RING)]
        mod_stored, row_stored, out_stored = sem("mod_stored"), sem("row_stored"), sem("out_stored")
        ce_ready, silu_c, mod_mm, modt_mm, mod_rows, modt_ready = (
            sem("ce_ready"), sem("silu_c"), sem("mod_mm"), sem("modt_mm"), sem("mod_rows"), sem("modt_ready"))
        pre_step = sem("pre_step")
        consts, sentinels = sem("consts"), sem("sentinels")
        var1, rstd1, xn_ready, xt_full, xt_free = (sem("var1"), sem("rstd1"), sem("xn_ready"), sem("xt_full"),
                                                  sem("xt_free"))
        end_full, end_free = sem("end_full"), sem("end_free")
        ln_step, att_step, post_step = sem("ln_step"), sem("att_step"), sem("post_step")
        h_ready, pj_full, sc_full, tr_full, wo_full, post_full = (
            sem("h_ready"), sem("pj_full"), sem("sc_full"), sem("tr_full"), sem("wo_full"), sem("post_full"))
        cos_done, swap_done, sin_done, rope_done = (sem("cos_done"), sem("swap_done"), sem("sin_done"),
                                                    sem("rope_done"))
        v_out, mix_out0, mix_out1 = sem("v_out"), sem("mix_out0"), sem("mix_out1")
        max_done, exp_done, rinv_done = sem("max_done"), sem("exp_done"), sem("rinv_done")
        norm_near, norm_far = sem("norm_near"), sem("norm_far")
        trans_out0, trans_out12 = sem("trans_out0"), sem("trans_out12")
        wo_free, post_free, var2, rstd2, h2_ready = (sem("wo_free"), sem("post_free"), sem("var2"), sem("rstd2"),
                                                     sem("h2_ready"))
        nv_ready, se_ready, score_ready, key_ready, eg_ready, post_done = (
            sem("nv_ready"), sem("se_ready"), sem("score_ready"), sem("key_ready"), sem("eg_ready"), sem("post_done"))
        tok_step, tok_e_ready, tok_ready, first_zero = (sem("tok_step"), sem("tok_e_ready"), sem("tok_ready"),
                                                        sem("first_zero"))
        rows_in = [sem("rows_in0"), sem("rows_in1")]
        acc_zero, gt_full, hb_ready, gu_full, eg_x_ready, hid_ready = (
            sem("acc_zero"), sem("gt_full"), sem("hb_ready"), sem("gu_full"), sem("eg_x_ready"), sem("hid_ready"))
        ht_full, hid_t_ready, y_full, hi_ready, lo_ready = (sem("ht_full"), sem("hid_t_ready"), sem("y_full"),
                                                            sem("hi_ready"), sem("lo_ready"))
        w_ready, place_ready, back_done, exp_step, out_ready = (sem("w_ready"), sem("place_ready"), sem("back_done"),
                                                                sem("exp_step"), sem("out_ready"))

        dve_passed, pe_passed, pool_passed = sem("dve_passed"), sem("pe_passed"), sem("pool_passed")

        POST_STEPS, EXP_STEPS = 20, 2

        def pj_release(b, n):
            if n in PJ_ROPE:
                return swap_done, 10 * b + PJ_ROPE.index(n) + 1
            if n in PJ_V:
                return v_out, 2 * b + PJ_V.index(n) + 1
            g = [n in m for m in PJ_MIX].index(True)
            return (mix_out0, 4 * b + g + 1) if PJ_MIX[g][0] == n else (mix_out1, 4 * b + g + 1)

        def work_release(b, n):
            if n < 0:
                return work_release(b - 1, n + WORK_USES)
            if n in WORK_SCORE:
                return exp_done, 12 * b + WORK_SCORE.index(n) + 1
            g, i = divmod(WORK_TRANS.index(n), 3)
            return (trans_out0, 4 * b + g + 1) if i == 0 else (trans_out12, 8 * b + 2 * g + i)

        block = ctx.enter_context(nc.Block())

        @block.sync
        def _(sp):
            wmod_d = wmod.rearrange("(c p) n -> p c n", p=P)
            x_d = x.rearrange("b (t p) d -> p (b t) d", p=P)
            sp.dma_start(x_s[:, 0:BT, :], x_d[:, 0:BT, :]).then_inc(in_x0, 16)
            sp.dma_start(ct_s[:], c_t.rearrange("(c p) b -> p c b", p=P)).then_inc(in_c, 16)
            sp.dma_start(small_s[:], small).then_inc(in_small, 16)
            sp.dma_start(ident[:], masks[:, 2, :]).then_inc(in_small, 16)
            sp.dma_start(wmod_s[:, :, 0:2 * D], wmod_d[:, :, 0:2 * D]).then_inc(in_mod_t, 16)

            def load_chunk(k):
                if k >= 2:
                    sp.wait_ge(w_lo_ready, k - 1)
                if k in CH_O:
                    g, n = CH_O.index(k), GROUP * HD
                    src, parts = wo[g * n:(g + 1) * n, :].rearrange("(h p) n -> p h n", p=P), GROUP
                elif k in CH_Q:
                    g, n = CH_Q.index(k), GROUP * HD
                    src, parts = wq.rearrange("(c p) n -> p c n", p=P)[:, :, g * n:(g + 1) * n], DC
                else:
                    src, parts = (wk if k == CH_K else wv).rearrange("(c p) n -> p c n", p=P), DC
                sp.dma_start(stage[k % 2].rearrange("p (c n) -> p c n", c=parts), src).then_inc(in_stage[k % 2], 16)

            load_chunk(0)
            sp.dma_start(rope_s, rope).then_inc(in_rope, 16)
            load_chunk(1)
            sp.dma_start(mask_in, masks).then_inc(in_mask, 16)
            load_chunk(2)
            sp.dma_start(wmod_s[:, :, 2 * D:], wmod_d[:, :, 2 * D:]).then_inc(in_mod, 16)
            sp.dma_start(x_s[:, BT:, :], x_d[:, BT:, :]).then_inc(in_x, 16)
            for k in range(3, CH_O[0]):
                load_chunk(k)
            sp.dma_start(gate_s[:], gate_t.rearrange("(c p) n -> p c n", p=P)).then_inc(in_tail, 16)
            sp.dma_start(swg_s[:], sw_gate.rearrange("(c p) n -> p c n", p=P)).then_inc(in_tail, 16)
            sp.dma_start(swu_s[:], sw_up.rearrange("(c p) n -> p c n", p=P)).then_inc(in_tail, 16)
            sp.dma_start(swd_s[:, 0:2, :], sw_down[0:256, :].rearrange("(m p) n -> p m n", p=P)).then_inc(in_tail, 16)
            sp.dma_start(swd_s[0:SM[2], 2, :], sw_down[256:SHARED, :]).then_inc(in_tail, 16)

            def load_slot(u, g):
                gu, wa, wb = slot(u)
                for m, w in enumerate((w_gate, w_up)):
                    sp.dma_start(gu[:, m].rearrange("p j c i -> p (j c i)"),
                                 w[bass.ds(g, 1)].rearrange("g p n -> (g p) n")).then_inc(in_gu[u], 16)
                sp.dma_start(wa.rearrange("p j d -> p (j d)"),
                             w_down_a[bass.ds(g, 1)].rearrange("g p n -> (g p) n")).then_inc(in_wd[u], 16)
                sp.dma_start(wb.rearrange("p j d -> p (j d)"),
                             w_down_b[bass.ds(g, 1)].rearrange("g p n -> (g p) n")).then_inc(in_wd[u], 16)

            sp.wait_ge(mod_mm, 2)
            load_chunk(CH_O[0])
            sp.wait_ge(mod_rows, 4)
            sp.dma_start(mod_d, modr_s).then_inc(mod_stored, 16)
            for k in CH_O[1:]:
                load_chunk(k)
            sp.wait_ge(mod_stored, 16)
            sp.dma_start(mod_s[:], mod_d[0, :].partition_broadcast(P)).then_inc(in_modrow, 16)
            with sp.Fori(1, BATCH) as b:
                sp.wait_ge(score_ready, b)
                sp.dma_start(rows_d[bass.ds((b - 1) * SEQ, SEQ), :].rearrange("(t p) n -> p t n", p=P),
                             row_s[:]).then_inc(row_stored, 16)
                sp.wait_ge(row_stored, 16 * b)
                sp.wait_ge(post_done, b)
                sp.dma_start(mod_s[:], mod_d[bass.ds(b, 1), :].rearrange("b n -> (b n)").partition_broadcast(P))\
                  .then_inc(in_modrow, 16)
            sp.wait_ge(pj_full, PJ_USES * (BATCH - 1) + PJ_ROPE[-1] + 1)
            load_slot(0, 0)
            load_slot(1, 1)
            sp.wait_ge(wo_full, BATCH)
            for u in range(2, RING):
                load_slot(u, u)
            sp.dma_start(iota_s, iota_row.partition_broadcast(P)).then_inc(in_iota, 16)
            for b in range(BATCH):
                sp.dma_start(gb_all[:, b, :], mod_d[b, 3 * D:4 * D].partition_broadcast(P)).then_inc(in_gb, 16)
            sp.wait_ge(score_ready, BATCH)
            sp.dma_start(rows_d[(BATCH - 1) * SEQ:T, :].rearrange("(t p) n -> p t n", p=P),
                         row_s[:]).then_inc(row_stored, 16)
            for g in range(RING, GROUPS):
                sp.wait_ge(y_full, g - RING + 1)
                load_slot(g % RING, g)
            for b in range(BATCH):
                sp.wait_ge(out_ready, b + 1)
                sp.dma_start(out[b].rearrange("(t p) d -> p t d", p=P), x_s[:, BT * b:BT * b + BT, :])\
                  .then_inc(out_stored, 16)
            sp.wait_ge(out_stored, 16 * BATCH)
            sp.wait_ge(row_stored, 16 * BATCH)

        @block.gpsimd
        def _(pool):
            nc.gpsimd.memset(half[:], -0.5).then_inc(sentinels, 1)
            nc.gpsimd.memset(lg[:, :, EXPERTS:], -BIG).then_inc(sentinels, 1)
            nc.gpsimd.memset(pick[:, :, TOPK:], -BIG).then_inc(sentinels, 1)
            nc.gpsimd.memset(zero_s[:], 0.0).then_inc(sentinels, 1)
            pool.wait_ge(sentinels, 1)

            def first_norm(b):
                pool.wait_ge(var1, b + 1)
                nc.gpsimd.tensor_tensor(rstd[:], var[:], half[:], ALU.pow).then_inc(rstd1, 1)

            def split_low(k):
                pool.wait_ge(w_hi_ready, k + 1)
                nc.gpsimd.tensor_tensor(chunk(k)[:, 1], stage[k % 2], chunk(k)[:, 0].bitcast(F32),
                                        ALU.subtract).then_inc(w_lo_ready, 1)

            first_norm(0)
            for k in range(3):
                split_low(k)
            pool.wait_ge(in_rope, 16)

            def sines(b, r):
                pool.wait_ge(swap_done, 10 * b + r + 1)
                sin = rope_s[:, 3 if r < 2 else 1, :]
                nc.gpsimd.tensor_tensor(swap_s[:, r % 2], swap_s[:, r % 2],
                                        sin.unsqueeze(1).to_broadcast([P, 2, SEQ]), ALU.mult).then_inc(sin_done, 1)

            def normalise(b, g):
                pool.wait_ge(rinv_done, 4 * b + g + 1)
                for t in range(BT):
                    probs = prob_far[:, g % 2, :, t * P:(t + 1) * P]
                    nc.gpsimd.tensor_tensor(probs, probs,
                                            rinv[:, g % 2, GROUP:].unsqueeze(2).to_broadcast([P, GROUP, P]),
                                            ALU.mult).then_inc(norm_far, 1)

            def row_step(b, tail):
                if tail:
                    pool.wait_ge(pj_full, PJ_USES * (b - 1) + PJ_ROPE[-1] + 1)
                    row = h_all[:, :, bass.ds(b * SEQ, SEQ)]
                    nc.gpsimd.tensor_copy(h_cur[:, 0], row).then_inc(h_hi_ready, 1)
                    pool.wait_ge(h_hi_ready, b)
                    alone(pool, pool_passed)
                    nc.gpsimd.tensor_tensor(h_cur[:, 1], row, h_cur[:, 0].bitcast(F32), ALU.subtract)\
                      .then_inc(h_ready, 1)
                sines(b, 0)
                sines(b, 1)
                if not tail:
                    split_low(3)
                sines(b, 2)
                if tail:
                    pool.wait_ge(var2, b)
                    nc.gpsimd.tensor_tensor(rstd[:], var[:], half[:], ALU.pow).then_inc(rstd2, 1)
                else:
                    first_norm(1)
                sines(b, 3)
                if not tail:
                    split_low(4)
                sines(b, 4)
                sines(b, 5)
                if not tail:
                    first_norm(2)
                    split_low(5)
                sines(b, 6)
                normalise(b, 0)
                if not tail:
                    split_low(6)
                sines(b, 7)
                if not tail:
                    first_norm(3)
                    split_low(7)
                sines(b, 8)
                if not tail:
                    split_low(8)
                normalise(b, 1)
                sines(b, 9)
                if not tail:
                    split_low(9)
                normalise(b, 2)
                normalise(b, 3)

            row_step(0, False)
            with pool.Fori(1, BATCH) as b:
                row_step(b, True)
            pool.wait_ge(var2, BATCH)
            nc.gpsimd.tensor_tensor(rstd[:], var[:], half[:], ALU.pow).then_inc(rstd2, 1)

            pool.wait_ge(tok_ready, 1)
            pool.wait_ge(row_stored, 16 * BATCH)
            for g in range(GROUPS):
                if g >= 2:
                    pool.wait_ge(gt_full, g - 1)
                    pool.wait_ge(w_ready, g - 1)
                nc.gpsimd.indirect_dma_start(
                    rows_s[:, g % 2, :], None, rows_d, bass.IndirectOffsetOnAxis(tok_i[:, g:g + 1], axis=0),
                    bounds_check=T - 1, oob_is_err=False).then_inc(rows_in[g % 2], 16)

        @block.scalar
        def _(act):
            act.wait_ge(in_c, 16)
            nc.scalar.activation(ce_s[:], ct_s[:], ACT.Exp, scale=-1.0).then_inc(ce_ready, 1)

            def swap(b, r):
                act.wait_ge(cos_done, 10 * b + r + 1)
                need(act, rope_done, 10 * b + r - 1)
                src = pj[PJ_ROPE[r] % 2][:].rearrange("p (h s) -> p h s", h=2)
                nc.scalar.activation(swap_s[0:64, r % 2], src[64:128], ACT.Copy)
                nc.scalar.activation(swap_s[64:128, r % 2], src[0:64], ACT.Copy).then_inc(swap_done, 1)

            def split_high(k):
                act.wait_ge(in_stage[k % 2], 16 * (k // 2 + 1))
                nc.scalar.activation(chunk(k)[:, 0], stage[k % 2], ACT.Copy).then_inc(w_hi_ready, 1)

            def values(b, t):
                act.wait_ge(pj_full, PJ_USES * b + PJ_V[t] + 1)
                nc.scalar.activation(v_s[:, t, :], pj[PJ_V[t] % 2][:], ACT.Copy).then_inc(v_out, 1)

            def exps(b, s):
                g, i = divmod(s, 3)
                act.wait_ge(max_done, 12 * b + s + 1)
                scores = work[WORK_SCORE[s] % 4]
                heads = range(GROUP) if i == 0 else (2 * i - 2, 2 * i - 1)
                for n, h in enumerate(heads):
                    w = P if i == 0 else SEQ
                    col = h if i == 0 else GROUP + h
                    dst = prob_near if i == 0 else prob_far
                    last = nc.scalar.activation(dst[:, g % 2, h, :], scores[:, n * w:(n + 1) * w], ACT.Exp,
                                                bias=nmax[:, g % 2, col:col + 1],
                                                accum_out=psum_p[:, g % 2, col:col + 1])
                last.then_inc(exp_done, 1)

            def take_far(b, g):
                for i in (1, 2):
                    act.wait_ge(tr_full, 12 * b + 3 * g + i + 1)
                    nc.scalar.activation(prob_t[:, i, :], work[WORK_TRANS[3 * g + i] % 4][:], ACT.Copy).then_inc(trans_out12, 1)

            def take_mix(b, g):
                n = PJ_MIX[g][1]
                act.wait_ge(pj_full, PJ_USES * b + n + 1)
                nc.scalar.activation(mix_s[:, g % 2, 1, 0], pj[n % 2][:], ACT.Copy).then_inc(mix_hi1, 1)

            def router_exp(pb):
                act.wait_ge(nv_ready, pb + 1)
                for t in range(BT):
                    last = nc.scalar.activation(row_s[:, t, D:ROW], lg[:, t, 0:EXPERTS], ACT.Exp,
                                                bias=nv[:, t:t + 1], accum_out=sm[:, t:t + 1])
                last.then_inc(se_ready, 1)

            def shared_tanh(pb, m):
                act.wait_ge(post_full, POST_USES * pb + IN_LOOP.index(f"gu{m}") + 1)
                nc.scalar.activation(eg_s[0:SM[m], m % 2], post[0:SM[m], 0:SEQ], ACT.Tanh, scale=0.5)\
                  .then_inc(eg_ready, 1)

            def row_step(b, tail):
                swap(b, 0)
                swap(b, 1)
                if not tail:
                    split_high(3)
                swap(b, 2)
                swap(b, 3)
                values(b, 0)
                values(b, 1)
                if not tail:
                    split_high(4)
                swap(b, 4)
                exps(b, 0)
                swap(b, 5)
                exps(b, 1)
                if tail:
                    router_exp(b - 1)
                else:
                    split_high(5)
                exps(b, 2)
                swap(b, 6)
                if tail:
                    shared_tanh(b - 1, 0)
                exps(b, 3)
                if not tail:
                    split_high(6)
                swap(b, 7)
                exps(b, 4)
                if tail:
                    shared_tanh(b - 1, 1)
                else:
                    split_high(7)
                exps(b, 5)
                swap(b, 8)
                take_far(b, 0)
                swap(b, 9)
                if not tail:
                    split_high(8)
                exps(b, 6)
                take_mix(b, 0)
                exps(b, 7)
                exps(b, 8)
                if tail:
                    shared_tanh(b - 1, 2)
                else:
                    split_high(9)
                take_far(b, 1)
                exps(b, 9)
                take_mix(b, 1)
                exps(b, 10)
                exps(b, 11)
                take_far(b, 2)
                take_mix(b, 2)
                take_far(b, 3)
                take_mix(b, 3)

            for k in range(3):
                split_high(k)
            row_step(0, False)
            with act.Fori(1, BATCH) as b:
                row_step(b, True)
            router_exp(BATCH - 1)
            for m in range(3):
                act.wait_ge(end_full, m + 1)
                need(act, end_free, m - 1)
                nc.scalar.activation(eg_s[0:SM[m], m % 2], end_bank[m][0:SM[m], 0:SEQ], ACT.Tanh, scale=0.5)\
                  .then_inc(eg_ready, 1)

            def group_step(g, u, rows=True, ends=True):
                if rows:
                    act.wait_ge(gt_full, g + 1)
                    nc.scalar.activation(hb_t[:, u % 2], gt_bank[:, 0:DC * P].rearrange("p (c s) -> p c s", c=DC),
                                         ACT.Copy).then_inc(hb_ready, 1)
                if ends:
                    act.wait_ge(ht_full, g)
                    nc.scalar.activation(hid_ta, ht_bank[0:IA, 0:P], ACT.Copy)
                    nc.scalar.activation(hid_tb, ht_bank[0:IB, P:2 * P], ACT.Copy).then_inc(hid_t_ready, 1)
                if rows:
                    act.wait_ge(gu_full, g + 1)
                    nc.scalar.activation(eg_x, gu_bank[:, 0:INTER], ACT.Tanh, scale=0.5).then_inc(eg_x_ready, 1)
                if ends:
                    act.wait_ge(y_full, g)
                    act.wait_ge(w_ready, g)
                    v = (u + 1) % 2
                    need(act, back_done, g - 2)
                    nc.scalar.activation(y_hi[v][:], y_bank[:, 0:D], ACT.Copy, scale=w_slot[:, v:v + 1])\
                      .then_inc(hi_ready, 1)

            for u in range(PEELED):
                group_step(u, u, ends=u > 0)
            with act.Fori(0, ROUNDS) as k:
                for i in range(RING):
                    group_step(RING * k + (PEELED + i), (PEELED + i) % RING)
            group_step(GROUPS, GROUPS % RING, rows=False)

        @block.vector
        def _(dve):
            V = nc.vector
            pre = Steps(dve, pre_step, 0)
            dve.wait_ge(ce_ready, 1)
            pre.done(V.tensor_scalar(ce_s[:], ce_s[:], 1.0, None, ALU.add))
            pre.wait()
            pre.done(V.reciprocal(ce_s[:], ce_s[:]))
            pre.wait()
            V.tensor_tensor(ct_s[:], ct_s[:], ce_s[:], ALU.mult).then_inc(silu_c, 1)

            def norm_stats(step, tile0, var_sem):
                for t in range(BT):
                    last = V.bn_stats(stat[:, t, :], x_s[:, bass.ds(tile0 + t, 1), :].rearrange("p t d -> p (t d)"))
                step.done(last)
                step.wait()
                alone(dve, dve_passed)
                for t in range(BT):
                    last = V.bn_aggr(mv[:, t, :], stat[:, t, :])
                step.done(last)
                step.wait()
                V.tensor_scalar(var[:], mv[:, :, 1], EPS, None, ALU.add).then_inc(var_sem, 1)

            def norm_apply(dst, tile0, t):
                return V.tensor_scalar(dst, x_s[:, bass.ds(tile0 + t, 1), :].rearrange("p t d -> p (t d)"),
                                       mv[:, t, 0:1], rstd[:, t:t + 1], ALU.subtract, ALU.mult)

            def first_stats(b):
                dve.wait_ge(in_x0 if b == 0 else in_x, 16)
                norm_stats(pre, b * BT, var1)

            def first_apply(b):
                dve.wait_ge(rstd1, b + 1)
                for t in range(BT):
                    last = norm_apply(xn_s[:, t, :], b * BT, t)
                last.then_inc(xn_ready, 1)

            def first_take(b):
                dve.wait_ge(xt_full, b + 1)
                dve.wait_ge(modt_ready, 2)
                xt = post[:].rearrange("p (c s) -> p c s", c=DC)
                row = h_all[:, :, b * SEQ:(b + 1) * SEQ]
                for c in range(DC):
                    last = V.tensor_scalar(row[:, c], xt[:, c], modt_s[:, 1, c, b:b + 1], modt_s[:, 0, c, b:b + 1],
                                           ALU.mult, ALU.add)
                last.then_inc(xt_free, 1)
                if b == 0:
                    dve.wait_ge(xt_free, 1)
                    pre.done(V.tensor_copy(h_cur[:, 0], row))
                    pre.wait()
                    V.tensor_tensor(h_cur[:, 1], row, h_cur[:, 0].bitcast(F32), ALU.subtract).then_inc(h_ready, 1)

            def take_modulation(m):
                dve.wait_ge(mod_mm, m + 1)
                if m == 0:
                    V.tensor_copy(modr_s[:, D:2 * D], post[0:BATCH, D:2 * D]).then_inc(mod_rows, 1)
                else:
                    V.tensor_scalar(modr_s[:, 2 * D:3 * D], post[0:BATCH, 0:D], 1.0, None, ALU.add)\
                     .then_inc(mod_rows, 1)
                src, at = (post[0:BATCH, 0:D], 0) if m == 0 else (post[0:BATCH, D:2 * D], 3 * D)
                sign, size = modq_s[:, 0], modq_s[:, 1]
                pre.done(V.tensor_scalar(sign, src, 0.0, 2.0, ALU.is_ge, ALU.mult))
                pre.wait()
                pre.done(V.tensor_scalar(sign, sign, -1.0, None, ALU.add))
                pre.wait()
                pre.done(V.tensor_tensor(size, src, sign, ALU.mult))
                pre.wait()
                V.scalar_tensor_tensor(modr_s[:, at:at + D], size, 0.25, sign, ALU.max, ALU.mult)\
                 .then_inc(mod_rows, 1)

            first_stats(0)
            first_apply(0)
            dve.wait_ge(modt_mm, 1)
            mt = wo_bank[:, 0:16].rearrange("p (m c b) -> p m c b", m=2, c=DC)
            V.tensor_copy(modt_s[:, 0], mt[:, 0]).then_inc(modt_ready, 1)
            V.tensor_scalar(modt_s[:, 1], mt[:, 1], 1.0, None, ALU.add).then_inc(modt_ready, 1)
            first_take(0)

            dve.wait_ge(in_mask, 16)
            V.tensor_copy(mask_near[:], mask_in[:, 0].unsqueeze(1).to_broadcast([P, GROUP, P])).then_inc(consts, 1)
            V.tensor_copy(mask_far[:, :, 0], mask_in[:, 1].unsqueeze(1).to_broadcast([P, 2, P])).then_inc(consts, 1)
            V.tensor_copy(mask_far[:, :, 1], mask_in[:, 0].unsqueeze(1).to_broadcast([P, 2, P])).then_inc(consts, 1)
            V.tensor_copy(ident_b[:], mask_in[:, 2]).then_inc(consts, 1)
            dve.wait_ge(consts, 4)
            dve.wait_ge(in_rope, 16)

            def heads_of(r):
                return k_s[:, 2 * r:2 * r + 2] if r < 2 else q_s[:, (r // 2 - 1) % 2, 2 * (r % 2):2 * (r % 2) + 2]

            def cosines(b, r):
                dve.wait_ge(pj_full, PJ_USES * b + PJ_ROPE[r] + 1)
                cos = rope_s[:, 2 if r < 2 else 0, :].unsqueeze(1).to_broadcast([P, 2, SEQ])
                V.tensor_tensor(heads_of(r), pj[PJ_ROPE[r] % 2][:].rearrange("p (h s) -> p h s", h=2), cos,
                                ALU.mult).then_inc(cos_done, 1)

            def rotate(b, r):
                dve.wait_ge(sin_done, 10 * b + r + 1)
                dve.wait_ge(cos_done, 10 * b + r + 1)
                V.tensor_tensor(heads_of(r), heads_of(r), swap_s[:, r % 2], ALU.add).then_inc(rope_done, 1)

            def maxima(b, s):
                g, i = divmod(s, 3)
                dve.wait_ge(sc_full, 12 * b + s + 1)
                heads = GROUP if i == 0 else 2
                lo = 0 if i == 0 else GROUP + 2 * (i - 1)
                V.tensor_reduce(nmax[:, g % 2, lo:lo + heads],
                                work[WORK_SCORE[s] % 4][:].rearrange("p (h k) -> p h k", h=heads),
                                AX_X, ALU.max, negate=True).then_inc(max_done, 1)

            def inverses(b, g):
                dve.wait_ge(exp_done, 12 * b + 3 * g + 3)
                V.reciprocal(rinv[:, g % 2], psum_p[:, g % 2]).then_inc(rinv_done, 1)
                dve.wait_ge(rinv_done, 4 * b + g + 1)
                V.tensor_tensor(prob_near[:, g % 2], prob_near[:, g % 2],
                                rinv[:, g % 2, 0:GROUP].unsqueeze(2).to_broadcast([P, GROUP, P]),
                                ALU.mult).then_inc(norm_near, 1)

            def take_near(b, g):
                dve.wait_ge(tr_full, 12 * b + 3 * g + 1)
                V.tensor_copy(prob_t[:, 0, :], work[WORK_TRANS[3 * g] % 4][:]).then_inc(trans_out0, 1)

            def take_mix(b, g):
                n = PJ_MIX[g][0]
                dve.wait_ge(pj_full, PJ_USES * b + n + 1)
                V.tensor_copy(mix_s[:, g % 2, 0, 0], pj[n % 2][:]).then_inc(mix_hi0, 1)
                for t, hi_sem, lo_sem in ((0, mix_hi0, mix_out0), (1, mix_hi1, mix_out1)):
                    dve.wait_ge(hi_sem, 4 * b + g + 1)
                    V.tensor_tensor(mix_s[:, g % 2, t, 1], pj[PJ_MIX[g][t] % 2][:],
                                    mix_s[:, g % 2, t, 0].bitcast(F32), ALU.subtract).then_inc(lo_sem, 1)

            class Tail:

                def __init__(self, pb, order):
                    self.pb, self.order, self.step = pb, order, Steps(dve, post_step, pb * POST_STEPS)
                    self.tiles = x_s[:, bass.ds(pb * BT, BT), :]

                def residual(self):
                    dve.wait_ge(wo_full, self.pb + 1)
                    dve.wait_ge(in_modrow, 16 * (self.pb + 1))
                    V.tensor_tensor(tmp_s[:], wo_bank[:].rearrange("p (t d) -> p t d", t=BT),
                                    mod_s[:, 0:D].unsqueeze(1).to_broadcast([P, BT, D]), ALU.mult)\
                     .then_inc(wo_free, 1)
                    dve.wait_ge(wo_free, self.pb + 1)
                    self.step.done(V.tensor_tensor(self.tiles, self.tiles, tmp_s[:], ALU.add))
                    self.step.wait()

                def stats(self):
                    norm_stats(self.step, self.pb * BT, var2)

                def rows(self):
                    dve.wait_ge(rstd2, self.pb + 1)
                    for t in range(BT):
                        last = norm_apply(row_s[:, t, 0:D], self.pb * BT, t)
                    self.step.done(last)
                    self.step.wait()
                    self.step.done(V.tensor_tensor(row_s[:, :, 0:D], row_s[:, :, 0:D],
                                                   mod_s[:, 2 * D:3 * D].unsqueeze(1).to_broadcast([P, BT, D]),
                                                   ALU.mult))
                    self.step.wait()
                    V.tensor_tensor(row_s[:, :, 0:D], row_s[:, :, 0:D],
                                    mod_s[:, D:2 * D].unsqueeze(1).to_broadcast([P, BT, D]), ALU.add)\
                     .then_inc(h2_ready, 1)

                def full(self, use):
                    dve.wait_ge(post_full, POST_USES * self.pb + self.order.index(use) + 1)

                def take_h(self):
                    self.full("h_t")
                    V.tensor_copy(h_t[:], post[:].rearrange("p (c s) -> p c s", c=DC)).then_inc(post_free, 1)

                def top6(self):
                    self.full("logits")
                    V.tensor_copy(lg[:, :, 0:EXPERTS], post[:, 0:BT * EXPERTS].rearrange("p (t e) -> p t e", t=BT))\
                     .then_inc(post_free, 1)
                    dve.wait_ge(post_free, POST_USES * self.pb + self.order.index("logits") + 1)
                    alone(dve, dve_passed)
                    for t in range(BT):
                        last = V.max(top[:, t, :], lg[:, t, 0:EXPERTS])
                    self.step.done(last)
                    self.step.wait()
                    V.tensor_scalar(nv[:], top[:, :, 0], -1.0, None, ALU.mult).then_inc(nv_ready, 1)
                    self.step.done(V.tensor_copy(pick[:, :, 0:TOPK], top[:, :, 0:TOPK]))
                    self.step.wait()
                    alone(dve, dve_passed)
                    for t in range(BT):
                        last = V.match_replace(rp[:, t, :], pick[:, t, :], lg[:, t, :], BIG)
                    self.step.done(last)
                    self.step.wait()
                    for t in range(BT):
                        last = V.tensor_scalar(key[:, t, :], rp[:, t, 0:EXPERTS], BIG / 2,
                                               rank[:, bass.ds(self.pb * BT + t, 1)], ALU.is_ge, ALU.mult)
                    last.then_inc(key_ready, 1)

                def scores(self):
                    dve.wait_ge(se_ready, self.pb + 1)
                    self.step.done(V.reciprocal(sm[:], sm[:]))
                    self.step.wait()
                    for t in range(BT):
                        last = V.tensor_scalar(row_s[:, t, D:ROW], row_s[:, t, D:ROW], sm[:, t:t + 1], None, ALU.mult)
                    last.then_inc(score_ready, 1)

                def shared_hidden(self, m, src=post, free=None):
                    dve.wait_ge(eg_ready, 3 * self.pb + m + 1)
                    n, eg = SM[m], eg_s[:, m % 2]
                    if free is not None and m:
                        dve.wait_ge(free, m)
                    self.step.done(V.scalar_tensor_tensor(tg_s[0:n], eg[0:n], 1.0, src[0:n, 0:SEQ],
                                                          ALU.add, ALU.mult))
                    self.step.wait()
                    V.scalar_tensor_tensor(sh_s[0:n, m], src[0:n, SEQ:2 * SEQ], 0.5, tg_s[0:n], ALU.mult, ALU.mult)\
                     .then_inc(post_free if free is None else free, 1)

                def take_key(self):
                    self.full("key_t")
                    V.tensor_copy(cand[0][:, CAP:], post[0:EXPERTS, 0:SEQ]).then_inc(post_free, 1)

                def first_tokens(self):
                    dve.wait_ge(post_free, POST_USES * self.pb + self.order.index("key_t") + 1)
                    self.step.done(V.tensor_copy(cand[0][:, 0:CAP], first[:]))
                    self.step.wait()
                    for r in range(CAP // 8):
                        alone(dve, dve_passed)
                        self.step.done(V.max(first[:, 8 * r:8 * r + 8], cand[r % 2][:]))
                        self.step.wait()
                        if r < CAP // 8 - 1:
                            alone(dve, dve_passed)
                            self.step.done(V.match_replace(cand[(r + 1) % 2][:], first[:, 8 * r:8 * r + 8],
                                                           cand[r % 2][:], -1.0))
                            self.step.wait()

                def shared_out(self):
                    self.full("down")
                    V.tensor_tensor(tmp_s[:], post[:].rearrange("p (t d) -> p t d", t=BT),
                                    mod_s[:, 3 * D:4 * D].unsqueeze(1).to_broadcast([P, BT, D]), ALU.mult)\
                     .then_inc(post_free, 1)
                    dve.wait_ge(post_free, POST_USES * self.pb + len(self.order))
                    V.tensor_tensor(self.tiles, self.tiles, tmp_s[:], ALU.add).then_inc(post_done, 1)

            def row_step(b, tail):
                cosines(b, 0)
                cosines(b, 1)
                rotate(b, 0)
                tail.residual() if tail else first_stats(1)
                cosines(b, 2)
                rotate(b, 1)
                cosines(b, 3)
                if tail:
                    tail.stats()
                rotate(b, 2)
                rotate(b, 3)
                tail.rows() if tail else first_apply(1)
                cosines(b, 4)
                maxima(b, 0)
                tail.take_h() if tail else take_modulation(0)
                cosines(b, 5)
                maxima(b, 1)
                rotate(b, 4)
                if tail:
                    tail.top6()
                else:
                    first_take(1)
                    first_stats(2)
                maxima(b, 2)
                rotate(b, 5)
                cosines(b, 6)
                inverses(b, 0)
                if tail:
                    tail.shared_hidden(0)
                else:
                    take_modulation(1)
                    first_apply(2)
                maxima(b, 3)
                cosines(b, 7)
                maxima(b, 4)
                if tail:
                    tail.scores()
                    tail.shared_hidden(1)
                else:
                    first_take(2)
                    first_stats(3)
                rotate(b, 6)
                maxima(b, 5)
                rotate(b, 7)
                cosines(b, 8)
                take_near(b, 0)
                inverses(b, 1)
                cosines(b, 9)
                tail.take_key() if tail else first_apply(3)
                rotate(b, 8)
                maxima(b, 6)
                take_mix(b, 0)
                rotate(b, 9)
                maxima(b, 7)
                maxima(b, 8)
                tail.shared_hidden(2) if tail else first_take(3)
                take_near(b, 1)
                inverses(b, 2)
                maxima(b, 9)
                take_mix(b, 1)
                maxima(b, 10)
                maxima(b, 11)
                take_near(b, 2)
                inverses(b, 3)
                take_mix(b, 2)
                if tail:
                    tail.shared_out()
                take_near(b, 3)
                if tail:
                    tail.first_tokens()
                take_mix(b, 3)

            V.memset(first[:], 0.0).then_inc(first_zero, 1)
            dve.wait_ge(first_zero, 1)
            row_step(0, None)
            with dve.Fori(1, BATCH) as b:
                tail = Tail(b - 1, IN_LOOP)
                row_step(b, tail)
                assert tail.step.n == POST_STEPS, tail.step.n
            tail = Tail(BATCH - 1, AT_END)
            tail.residual()
            tail.stats()
            tail.rows()
            tail.take_h()
            tail.top6()
            tail.take_key()
            tail.first_tokens()
            V.tensor_scalar(tok_e[:], first[:], -1.0, float(T), ALU.mult, ALU.add).then_inc(tok_e_ready, 1)
            tail.scores()
            step = Steps(dve, tok_step, 0)
            tail.full("tok_t")
            for j in range(PER):
                last = V.tensor_copy(tok[CAP * j:CAP * j + CAP, :],
                                     post[0:CAP, 0:EXPERTS].rearrange("p (g j) -> p g j", j=PER)[:, :, j])
            last.then_inc(post_free, 1)
            dve.wait_ge(post_free, POST_USES * (BATCH - 1) + AT_END.index("tok_t") + 1)
            step.done(V.tensor_scalar(tok_f[:], tok[:], float(T - 1), None, ALU.min))
            step.wait()
            V.tensor_copy(tok_i[:], tok_f[:]).then_inc(tok_ready, 1)
            for m in range(3):
                tail.shared_hidden(m, end_bank[m], end_free)
            tail.shared_out()
            assert tail.step.n == POST_STEPS
            dve.wait_ge(in_iota, 16)

            def group_step(g, u, rows=True, ends=True, count=None):
                ex = Steps(dve, exp_step, EXP_STEPS * g)
                if rows:
                    v = u % 2
                    dve.wait_ge(rows_in[v], count)
                    ex.done(V.tensor_tensor(w_tmp, rows_s[:, v, bass.ds(PER * g + D, PER)], quad, ALU.mult))
                    ex.wait()
                    need(dve, hi_ready, g - 1)
                    V.tensor_reduce(w_slot[:, v:v + 1], w_tmp, AX_X, ALU.add).then_inc(w_ready, 1)
                    dve.wait_ge(eg_x_ready, g + 1)
                    ex.done(V.scalar_tensor_tensor(tg_x, eg_x, 1.0, gu_bank[:, 0:INTER], ALU.add, ALU.mult))
                    ex.wait()
                    need(dve, ht_full, g)
                    V.scalar_tensor_tensor(hid_x, gu_bank[:, INTER:2 * INTER], 0.5, tg_x, ALU.mult, ALU.mult)\
                     .then_inc(hid_ready, 1)
                if ends:
                    v = (u + 1) % 2
                    need(dve, back_done, g - 2)
                    V.tensor_scalar(place[v][:], iota_s, tok[:, bass.ds(g - 1, 1)], None, ALU.is_equal)\
                     .then_inc(place_ready, 1)
                    dve.wait_ge(hi_ready, g)
                    V.scalar_tensor_tensor(y_lo[v][:], y_bank[:, 0:D], w_slot[:, v:v + 1], y_hi[v][:].bitcast(F32),
                                           ALU.mult, ALU.subtract).then_inc(lo_ready, 1)

            for u in range(PEELED):
                group_step(u, u, ends=u > 0, count=16 * (u // 2 + 1))
            with dve.Fori(0, ROUNDS) as k:
                for i in range(RING):
                    u = (PEELED + i) % RING
                    group_step(RING * k + (PEELED + i), u, count=8 * RING * k + 16 * ((PEELED + i) // 2 + 1))
            group_step(GROUPS, GROUPS % RING, rows=False)

            dve.wait_ge(in_gb, 16 * BATCH)
            dve.wait_ge(back_done, GROUPS)
            dve.wait_ge(post_done, BATCH)
            for b in range(BATCH):
                step.done(V.tensor_tensor(tmp_s[:], acc[b][:].rearrange("p (t d) -> p t d", t=BT),
                                          gb_all[:, b, :].unsqueeze(1).to_broadcast([P, BT, D]), ALU.mult))
                step.wait()
                tiles = x_s[:, BT * b:BT * b + BT, :]
                V.tensor_tensor(tiles, tiles, tmp_s[:], ALU.add).then_inc(out_ready, 1)
                dve.wait_ge(out_ready, b + 1)

        @block.tensor
        def _(pe):
            mm = nc.tensor.matmul
            def modulation(m):
                pe.wait_ge(in_mod, 16)
                for c in range(DC):
                    last = mm(post[0:BATCH, :], ct_s[:, c, :], wmod_s[:, c, 512 * (m + 1):512 * (m + 2)],
                              start=(c == 0), stop=(c == DC - 1))
                last.then_inc(mod_mm, 1)

            def first_rows(b):
                pe.wait_ge(xn_ready, b + 1)
                for c in range(DC):
                    for t in range(BT):
                        last = nc.tensor.transpose(post[:, c * SEQ + t * P:c * SEQ + t * P + P],
                                                   xn_s[:, t, c * P:c * P + P], ident[:])
                last.then_inc(xt_full, 1)

            pe.wait_ge(in_small, 32)
            first_rows(0)
            pe.wait_ge(in_mod_t, 16)
            pe.wait_ge(silu_c, 1)
            for m in range(2):
                for c2 in range(DC):
                    at = (m * DC + c2) * BATCH
                    for c in range(DC):
                        last = mm(wo_bank[:, at:at + BATCH], wmod_s[:, c, m * D + c2 * P:m * D + c2 * P + P],
                                  ct_s[:, c, :], start=(c == 0), stop=(c == DC - 1))
            last.then_inc(modt_mm, 1)

            def pj_take(b, n):
                need(pe, *(pj_release(b, n - 2) if n >= 2 else pj_release(b - 1, n + PJ_USES - 2)))
                return pj[n % 2]

            def project(b, r):
                dst = pj_take(b, PJ_ROPE[r])
                k = CH_K if r < 2 else CH_Q[(r - 2) // 2]
                if isinstance(b, int):
                    pe.wait_ge(w_lo_ready, k + 1)
                for i in range(2):
                    h = 2 * (r % 2) + i
                    for c in range(DC):
                        for u, v in PASSES:
                            last = mm(dst[:, i * SEQ:(i + 1) * SEQ], by_feature(k)[:, u, c, h * HD:(h + 1) * HD],
                                      h_cur[:, v, c, :], start=(c == u == v == 0), stop=(c == DC - 1 and u == 1))
                last.then_inc(pj_full, 1)

            def project_v(b, t):
                dst = pj_take(b, PJ_V[t])
                if isinstance(b, int):
                    pe.wait_ge(w_lo_ready, CH_V + 1)
                for c in range(DC):
                    for u, v in PASSES:
                        last = mm(dst[:], h_cur[:, u, c, t * P:(t + 1) * P], by_feature(CH_V)[:, v, c, :],
                                  start=(c == u == v == 0), stop=(c == DC - 1 and u == 1))
                last.then_inc(pj_full, 1)

            def score(b, s):
                g, i = divmod(s, 3)
                pe.wait_ge(rope_done, 10 * b + 2 * g + 4)
                need(pe, *work_release(b, WORK_SCORE[s] - 4))
                dst = work[WORK_SCORE[s] % 4]
                if i == 0:
                    mm(dst[:], ident_b[:], mask_near[:].rearrange("p h k -> p (h k)"), start=True, stop=True)
                    for h in range(GROUP):
                        last = mm(dst[:, h * P:(h + 1) * P], q_s[:, g % 2, h, 0:P], k_s[:, g, 0:P],
                                  start=False, stop=True, skip_group_check=True)
                else:
                    mm(dst[:], ident_b[:], mask_far[:].rearrange("p h m k -> p (h m k)"), start=True, stop=True)
                    for n in range(2):
                        last = mm(dst[:, n * SEQ:(n + 1) * SEQ], q_s[:, g % 2, 2 * (i - 1) + n, P:SEQ], k_s[:, g, :],
                                  start=False, stop=True, skip_group_check=True)
                last.then_inc(sc_full, 1)

            def transpose_probs(b, g):
                for i in range(3):
                    if i == 0:
                        pe.wait_ge(norm_near, 4 * b + g + 1)
                    else:
                        pe.wait_ge(norm_far, 8 * b + 2 * g + i)
                    n = WORK_TRANS[3 * g + i]
                    need(pe, *work_release(b, n - 4))
                    for h in range(GROUP):
                        src = (prob_near[:, g % 2, h, :] if i == 0
                               else prob_far[:, g % 2, h, (i - 1) * P:i * P])
                        last = nc.tensor.transpose(work[n % 4][:, h * P:(h + 1) * P], src, ident[:])
                    last.then_inc(tr_full, 1)

            def mix(b, g):
                v = [v_s[:, t, g * HD:(g + 1) * HD] for t in range(BT)]
                pe.wait_ge(v_out, 2 * b + 2)
                dst = pj_take(b, PJ_MIX[g][0])
                pe.wait_ge(trans_out0, 4 * b + g + 1)
                mm(dst[:], v[0], prob_t[:, 0, :], start=True, stop=True).then_inc(pj_full, 1)
                dst = pj_take(b, PJ_MIX[g][1])
                pe.wait_ge(trans_out12, 8 * b + 2 * g + 2)
                mm(dst[:], v[0], prob_t[:, 1, :], start=True, stop=False)
                mm(dst[:], v[1], prob_t[:, 2, :], start=False, stop=True).then_inc(pj_full, 1)

            def project_out(b, g):
                if g == 0:
                    need(pe, wo_free, b)
                if isinstance(b, int):
                    pe.wait_ge(w_lo_ready, CH_O[g] + 1)
                w = chunk(CH_O[g]).rearrange("p r (h n) -> p r h n", h=GROUP)
                for t, out_sem in enumerate((mix_out0, mix_out1)):
                    pe.wait_ge(out_sem, 4 * b + g + 1)
                    for h in range(GROUP):
                        for u, v in PASSES:
                            last = mm(wo_bank[:, t * D:(t + 1) * D], mix_s[:, g % 2, t, u, h * P:(h + 1) * P],
                                      w[:, v, h, :], start=(g == t == h == u == v == 0),
                                      stop=(g == KV_HEADS - 1 and h == GROUP - 1 and u == 1), skip_group_check=True)
                if g == KV_HEADS - 1:
                    last.then_inc(wo_full, 1)

            class Tail:

                def __init__(self, pb, order):
                    self.pb, self.order = pb, order

                def take(self, use):
                    need(pe, post_free, POST_USES * self.pb + self.order.index(use))

                def rows_t(self):
                    pe.wait_ge(h2_ready, self.pb + 1)
                    for c in range(DC):
                        for t in range(BT):
                            last = nc.tensor.transpose(post[:, c * SEQ + t * P:c * SEQ + t * P + P],
                                                       row_s[:, t, c * P:c * P + P], ident[:])
                    last.then_inc(post_full, 1)

                def logits(self):
                    self.take("logits")
                    for t in range(BT):
                        for c in range(DC):
                            last = mm(post[:, t * EXPERTS:(t + 1) * EXPERTS], h_t[:, c, t * P:(t + 1) * P],
                                      gate_s[:, c, :], start=(c == 0), stop=(c == DC - 1))
                    last.then_inc(post_full, 1)

                def gate_up(self, m, dst=post, release=None):
                    if release:
                        pe.wait_ge(*release)
                    else:
                        self.take(f"gu{m}")
                    n = SM[m]
                    for i, w in enumerate((swg_s, swu_s)):
                        for c in range(DC):
                            last = mm(dst[0:n, i * SEQ:(i + 1) * SEQ], w[:, c, m * P:m * P + n], h_t[:, c, :],
                                      start=(c == 0), stop=(c == DC - 1))
                    last.then_inc(end_full if release else post_full, 1)

                def keys_t(self):
                    self.take("key_t")
                    pe.wait_ge(key_ready, self.pb + 1)
                    alone(pe, pe_passed)
                    for t in range(BT):
                        last = nc.tensor.transpose(post[0:EXPERTS, t * P:(t + 1) * P], key[:, t, :], ident[:])
                    last.then_inc(post_full, 1)

                def down(self):
                    self.take("down")
                    for t in range(BT):
                        for m, n in enumerate(SM):
                            last = mm(post[:, t * D:(t + 1) * D], sh_s[0:n, m, t * P:(t + 1) * P], swd_s[0:n, m, :],
                                      start=(m == 0), stop=(m == 2))
                    last.then_inc(post_full, 1)

            def row_step(b, tail):
                pe.wait_ge(h_ready, b + 1)
                project(b, 0)
                project(b, 1)
                if tail:
                    project_out(b - 1, 3)
                project(b, 2)
                project(b, 3)
                project_v(b, 0)
                project_v(b, 1)
                project(b, 4)
                if not tail:
                    pe.wait_ge(consts, 4)
                score(b, 0)
                tail.rows_t() if tail else modulation(0)
                project(b, 5)
                score(b, 1)
                if tail:
                    tail.logits()
                else:
                    pe.wait_ge(mod_rows, 2)
                    first_rows(1)
                score(b, 2)
                project(b, 6)
                if tail:
                    tail.gate_up(0)
                else:
                    pe.wait_ge(xt_free, 2)
                    modulation(1)
                score(b, 3)
                project(b, 7)
                score(b, 4)
                if tail:
                    tail.gate_up(1)
                else:
                    pe.wait_ge(mod_rows, 4)
                    first_rows(2)
                score(b, 5)
                project(b, 8)
                transpose_probs(b, 0)
                project(b, 9)
                if tail:
                    tail.keys_t()
                score(b, 6)
                mix(b, 0)
                score(b, 7)
                project_out(b, 0)
                score(b, 8)
                if tail:
                    tail.gate_up(2)
                else:
                    pe.wait_ge(xt_free, 3)
                    first_rows(3)
                transpose_probs(b, 1)
                score(b, 9)
                mix(b, 1)
                score(b, 10)
                score(b, 11)
                transpose_probs(b, 2)
                project_out(b, 1)
                mix(b, 2)
                if tail:
                    tail.down()
                transpose_probs(b, 3)
                project_out(b, 2)
                mix(b, 3)

            row_step(0, None)
            pe.wait_ge(in_tail, 80)
            with pe.Fori(1, BATCH) as b:
                row_step(b, Tail(b - 1, IN_LOOP))
            project_out(BATCH - 1, 3)
            tail = Tail(BATCH - 1, AT_END)
            last_uses = [pj_release(BATCH - 1, PJ_USES - 2), pj_release(BATCH - 1, PJ_USES - 1),
                         work_release(BATCH - 1, WORK_USES - 4), work_release(BATCH - 1, WORK_USES - 3)]
            for a, last_use in zip(acc, last_uses):
                pe.wait_ge(*last_use)
                mm(a[:], zero_s[:, 0:P], zero_s[:], start=True, stop=True, skip_group_check=True)
            tail.rows_t()
            tail.logits()
            tail.gate_up(0, end_bank[0], work_release(BATCH - 1, WORK_USES - 2))
            tail.keys_t()
            tail.gate_up(1, end_bank[1], work_release(BATCH - 1, WORK_USES - 1))
            tail.take("tok_t")
            pe.wait_ge(tok_e_ready, 1)
            nc.tensor.transpose(post[0:CAP, 0:EXPERTS], tok_e[:], ident[0:EXPERTS, 0:EXPERTS]).then_inc(post_full, 1)
            tail.gate_up(2, end_bank[2], (wo_free, BATCH))
            pe.wait_ge(end_free, 3)
            tail.down()

            def group_step(g, u, rows=True, ends=True, back=True, count=None, fills=None, ended=None):
                gu, wa, wb = slot(u)
                if rows:
                    pe.wait_ge(rows_in[u % 2], count)
                    need(pe, hb_ready, g)
                    for c in range(DC):
                        last = nc.tensor.transpose(gt_bank[:, c * P:(c + 1) * P], rows_s[:, u % 2, c * P:(c + 1) * P],
                                                   ident[:])
                    last.then_inc(gt_full, 1)
                if back:
                    v = (u + 1) % 2
                    pe.wait_ge(lo_ready, g - 2)
                    pe.wait_ge(place_ready, g - 2)
                    for t in range(TT):
                        at = acc[t // BT][:, (t % BT) * D:(t % BT + 1) * D]
                        for part in (y_hi[v], y_lo[v]):
                            last = mm(at, place[v][:, t * P:(t + 1) * P], part[:], start=False, stop=True,
                                      skip_group_check=True)
                    last.then_inc(back_done, 1)
                if ends:
                    pe.wait_ge(hid_ready, g)
                    need(pe, hid_t_ready, g - 1)
                    nc.tensor.transpose(ht_bank[0:IA, 0:P], hid_x[:, 0:IA], ident[:])
                    nc.tensor.transpose(ht_bank[0:IB, P:2 * P], hid_x[:, IA:INTER], ident[:]).then_inc(ht_full, 1)
                if rows:
                    pe.wait_ge(hb_ready, g + 1)
                    need(pe, hid_ready, g)
                    pe.wait_ge(in_gu[u], fills)
                    for c in range(DC):
                        for j in range(PER):
                            last = mm(gu_bank[CAP * j:CAP * (j + 1), 0:2 * INTER],
                                      hb_t[:, u % 2, c, CAP * j:CAP * (j + 1)], gu[:, :, j, c, :],
                                      start=(c == 0), stop=(c == DC - 1))
                    last.then_inc(gu_full, 1)
                if ends:
                    gu, wa, wb = slot((u - 1) % RING)
                    pe.wait_ge(hid_t_ready, g)
                    need(pe, lo_ready, g - 1)
                    pe.wait_ge(in_wd[(u - 1) % RING], ended)
                    for i, (hid, w) in enumerate(((hid_ta, wa), (hid_tb, wb))):
                        for j in range(PER):
                            last = mm(y_bank[CAP * j:CAP * (j + 1), 0:D], hid[:, CAP * j:CAP * (j + 1)], w[:, j, :],
                                      start=(i == 0), stop=(i == 1))
                    last.then_inc(y_full, 1)

            def fill(g):
                return 32 * (g // RING + 1)

            pe.wait_ge(post_free, POST_USES * (BATCH - 1) + len(AT_END))
            for u in range(PEELED):
                group_step(u, u, ends=u > 0, back=u > 2, count=16 * (u // 2 + 1), fills=fill(u), ended=fill(u - 1))
            with pe.Fori(0, ROUNDS) as k:
                for i in range(RING):
                    g = PEELED + i
                    group_step(RING * k + g, g % RING, count=8 * RING * k + 16 * (g // 2 + 1),
                               fills=32 * k + fill(g), ended=32 * k + fill(g - 1))
            group_step(GROUPS, GROUPS % RING, rows=False, ended=fill(GROUPS - 1))
            for g in (GROUPS + 1, GROUPS + 2):
                group_step(g, g % RING, rows=False, ends=False)


def kernel(L0_attn_x, L0_attn_wq, L0_attn_wk, L0_attn_wv, L0_attn_wo, L0_ffn_gate_w, L0_ffn_w_gate, L0_ffn_w_up,
           L0_ffn_w_down, L0_ffn_sw_gate, L0_ffn_sw_up, L0_ffn_sw_down, L0_c, L0_wmod):
    import numpy as np
    import concourse.bacc as bacc
    from concourse.bass_utils import run_bass_kernel_spmd

    f32 = np.float32

    def halves(w, heads):
        return np.ascontiguousarray(np.asarray(w).reshape(D, heads, HD // 2, 2).transpose(0, 1, 3, 2).reshape(D, -1))

    def by_group(w):
        w = np.asarray(w).reshape(GROUPS, PER, DC, P, INTER)
        return np.ascontiguousarray(w.transpose(0, 3, 1, 2, 4)).reshape(GROUPS, P, PER * DC * INTER)

    down = np.asarray(L0_ffn_w_down).reshape(GROUPS, PER, INTER, D).transpose(0, 2, 1, 3)

    inv = (1.0 / np.power(f32(10000.0), np.arange(0, HD, 2, dtype=f32) / f32(HD))).astype(f32)
    ang = np.outer(np.arange(SEQ, dtype=f32), inv).astype(f32).T
    cos, sin = np.cos(ang).astype(f32), np.sin(ang).astype(f32)
    cos2, sin2 = np.concatenate([cos, cos]), np.concatenate([-sin, sin])
    scale = f32(1.0 / np.sqrt(f32(HD)))
    rope = np.stack([cos2 * scale, sin2 * scale, cos2, sin2], axis=1).astype(f32)
    qi, ki = np.arange(P)[:, None], np.arange(P)[None, :]
    masks = np.stack([np.where(ki <= qi, 0.0, -1e30), np.where(ki >= qi, 0.0, -1e30), np.eye(P)], axis=1).astype(f32)
    rank = T - (np.arange(TT)[None, :] * P + np.arange(P)[:, None])
    quad = np.arange(P)[:, None] // CAP == np.arange(PER)[None, :]
    small = np.concatenate([rank, quad], axis=1).astype(f32)

    arrays = {
        "x": np.asarray(L0_attn_x), "c_t": np.asarray(L0_c).T, "wmod": np.asarray(L0_wmod),
        "wq": halves(L0_attn_wq, HEADS), "wk": halves(L0_attn_wk, KV_HEADS), "wv": np.asarray(L0_attn_wv),
        "wo": np.asarray(L0_attn_wo), "gate_t": np.asarray(L0_ffn_gate_w).T,
        "w_gate": by_group(L0_ffn_w_gate), "w_up": by_group(L0_ffn_w_up),
        "w_down_a": down[:, 0:IA].reshape(GROUPS, IA, PER * D), "w_down_b": down[:, IA:].reshape(GROUPS, IB, PER * D),
        "sw_gate": np.asarray(L0_ffn_sw_gate), "sw_up": np.asarray(L0_ffn_sw_up),
        "sw_down": np.asarray(L0_ffn_sw_down), "rope": rope, "masks": masks, "small": small,
        "iota_row": np.arange(T, dtype=f32),
    }
    nc = bacc.Bacc("TRN2", target_bir_lowering=False, num_devices=1)
    ins, given = [], {}
    for name, a in arrays.items():
        a = np.ascontiguousarray(a)
        given[f"in_{name}"] = a
        ins.append(nc.dram_tensor(f"in_{name}", a.shape, mybir.dt.from_np(a.dtype), kind="ExternalInput").ap())
    res = nc.dram_tensor("out_0", (BATCH, SEQ, D), F32, kind="ExternalOutput").ap()
    bass_adaln_attention_moe(nc, *ins, res)
    r = run_bass_kernel_spmd(nc, [given], core_ids=[0])
    return r.results[0]["out_0"]
```

```python
from contextlib import ExitStack

import concourse.bass as bass
from concourse import mybir
from concourse.alu_op_type import AluOpType as ALU

ACT = mybir.ActivationFunctionType
F32 = mybir.dt.float32
F32R = mybir.dt.float32r
BF16 = mybir.dt.bfloat16
U32 = mybir.dt.uint32
AX_X = mybir.AxisListType.X

P = 128
BATCH, SEQ, D = 4, 256, 256
HEADS, KV_HEADS, HD = 16, 4, 128
GROUP = HEADS // KV_HEADS
EXPERTS, TOPK, CAP = 64, 6, 32
INTER, SHARED = 176, 352
T = BATCH * SEQ
TT = T // P
DC = D // P
BT = SEQ // P
EPS = 1e-5
PER = P // CAP
GROUPS = EXPERTS // PER
IA, IB = 96, 80
SM = [128, 128, 96]
RING = 6
ROW_BUFS = 6
ROW = D + EXPERTS
PEELED = GROUPS % RING
ROUNDS = GROUPS // RING
BIG = 3.0e38

PASSES = [(0, 0), (0, 1), (1, 0)]
CHUNK = 1024
CH_K, CH_V, CH_Q, CH_O = 0, 2, [1, 3, 4, 5], [6, 7, 8, 9]
CHUNKS = 10
POOL_OUT = [0, 2]
LOW_POOL = 4

PJ_ROPE = [0, 1, 2, 3, 6, 7, 8, 9, 10, 11]
PJ_V = [4, 5]
PJ_MIX = [(12, 13), (14, 15), (16, 17), (18, 19)]
PJ_USES = 20
WORK_SCORE = [0, 1, 2, 3, 4, 5, 9, 10, 11, 15, 16, 17]
WORK_TRANS = [6, 7, 8, 12, 13, 14, 18, 19, 20, 21, 22, 23]
WORK_USES = 24
IN_LOOP = ["h_t", "logits", "gu0", "gu1", "key_t", "gu2", "down"]
IN_LAST = ["h_t", "logits", "key_t"]
AT_END = ["h_t", "logits", "key_t", "tok_t", "down"]
POST_USES = len(IN_LOOP)


def need(eng, sem, value):
    if not isinstance(value, int) or value > 0:
        eng.wait_ge(sem, value)


def alone(eng, passed):
    eng.sem_inc(passed)


class Steps:

    def __init__(self, eng, sem, base):
        self.eng, self.sem, self.base, self.n = eng, sem, base, 0

    def done(self, ins):
        self.n += 1
        ins.then_inc(self.sem, 1)

    def wait(self):
        self.eng.wait_ge(self.sem, self.base + self.n)


def bass_adaln_attention_moe(nc, x, c_t, wmod, wq, wk, wv, wo, gate_t, w_gate, w_up, w_down_a, w_down_b,
                             sw_gate, sw_up, sw_down, rope, masks, small, iota_row, out):
    ctx = ExitStack()
    with ctx:
        def sb(name, shape, dt=F32):
            return ctx.enter_context(nc.sbuf_tensor(name, shape, dt))

        def sem(name):
            return ctx.enter_context(nc.semaphore(name))

        bank = [ctx.enter_context(nc.psum_tensor(f"bank{i}", [P, 512], F32)) for i in range(8)]
        pj, work, wo_bank, post = bank[0:2], bank[2:6], bank[6], bank[7]
        acc, gt_bank, ht_bank, gu_bank, y_bank = bank[0:4], bank[4], bank[5], bank[6], bank[7]
        end_bank = bank[4:7]

        SLOT = 2 * PER * DC * INTER + 2 * PER * D
        with nc.sbuf_tensor("weights", [P, CHUNKS * 2 * CHUNK], F32R) as weights:
            pass
        slots = sb("slots", [P, CHUNKS * 2 * CHUNK])

        def chunk(k):
            return weights[:, k * 2 * CHUNK:(k + 1) * 2 * CHUNK].rearrange("p (r n) -> p r n", r=2)

        def loaded(k):
            return slots[:, (2 * k + 1) * CHUNK:(2 * k + 2) * CHUNK]

        def by_feature(k):
            return chunk(k).rearrange("p r (c n) -> p r c n", c=DC)

        def slot(u):
            mem, at = ((slots, 0), (slots, SLOT), (rotation, 0), (slots, 2 * SLOT), (slots, 3 * SLOT), (slot_a, 0))[u]
            base = mem[:, at:at + SLOT]
            n = PER * DC * INTER
            gu = base[:, 0:2 * n].rearrange("p (m j c i) -> p m j c i", m=2, j=PER, c=DC)
            wa = base[0:IA, 2 * n:2 * n + PER * D].rearrange("p (j d) -> p j d", j=PER)
            wb = base[0:IB, 2 * n + PER * D:SLOT].rearrange("p (j d) -> p j d", j=PER)
            return gu, wa, wb

        with nc.sbuf_tensor("mixing", [P, 5120], F32R) as mixing:
            pass
        slot_a = sb("slot_a", [P, 5120])
        prob_t = mixing[:, 0:3072].rearrange("p (i r n) -> p i r n", i=3, r=2)
        v_s = mixing[:, 3072:5120].rearrange("p (r t n) -> p r t n", r=2, t=BT)
        rotation = sb("rotation", [P, SLOT])
        h_all = rotation[:, 0:2048].rearrange("p (c s) -> p c s", c=DC)
        swap_s = rotation[:, 2048:3072].rearrange("p (g h s) -> p g h s", g=2, h=2)
        rope_s = rotation[:, 3072:4096].rearrange("p (i s) -> p i s", i=4)
        area = sb("area", [P, 6144])
        q_s = area[:, 0:2048].rearrange("p (g h s) -> p g h s", g=2, h=GROUP)
        prob_near = area[:, 2048:3072].rearrange("p (g h s) -> p g h s", g=2, h=GROUP)
        prob_far = area[:, 3072:5120].rearrange("p (g h s) -> p g h s", g=2, h=GROUP)
        k_s = area[:, 5120:6144].rearrange("p (h s) -> p h s", h=KV_HEADS)
        mask_in = area[:, 4096:4480].rearrange("p (m k) -> p m k", m=3)
        iota_s = area[:, 0:1024]
        hb_t = area[:, 1024:1536].rearrange("p (g c s) -> p g c s", g=2, c=DC)
        rows_s = area[:, 1536:3456].rearrange("p (g n) -> p g n", g=ROW_BUFS)
        eg_x = area[:, 3456:3632]
        tg_x = area[:, 3632:3808]
        hid_x = area[:, 3808:3984]
        hid_ta = area[0:IA, 3984:4112]
        hid_tb = area[0:IB, 4112:4240]
        gb_all = area[:, 4240:5264].rearrange("p (b d) -> p b d", b=BATCH)
        w_tmp = area[:, 5264:5268]
        split_s = sb("split_s", [P, 4096], F32R)
        mix_s = split_s[:].rearrange("p (g t r n) -> p g t r n", g=2, t=BT, r=2)
        place = [split_s[:, i * T:(i + 1) * T] for i in range(2)]
        y_hi = [split_s[:, (8 + i) * D:(9 + i) * D] for i in range(2)]
        y_lo = [split_s[:, (10 + i) * D:(11 + i) * D] for i in range(2)]
        x_s = sb("x_s", [P, TT, D])
        h_cur = sb("h_cur", [P, 2, DC, SEQ], F32R)
        mod_s = sb("mod_s", [P, 4 * D])
        mask_near = sb("mask_near", [P, GROUP, P], BF16)
        mask_far = sb("mask_far", [P, 2, 2, P], BF16)
        ident_b = sb("ident_b", [P, P], BF16)
        ident = sb("ident", [P, P])
        gate_s = sb("gate_s", [P, DC, EXPERTS])
        swg_s = sb("swg_s", [P, DC, SHARED])
        swu_s = sb("swu_s", [P, DC, SHARED])
        swd_s = sb("swd_s", [P, 3, D])
        small_s = sb("small_s", [P, TT + PER])
        rank = small_s[:, 0:TT]
        quad = small_s[:, TT:TT + PER]
        row_s = sb("row_s", [P, BT, ROW])
        xn_s = row_s[:, :, 0:D]
        h_t = sb("h_t", [P, DC, SEQ])
        modr_s = mod_s[0:BATCH, :]
        modq_s = h_t[0:BATCH]
        tail_s = sb("tail_s", [P, 8 * SEQ])
        wmod_t = slots[:, 2 * CHUNK * CH_O[3]:2 * CHUNK * CH_O[3] + 4 * D].rearrange("p (c n) -> p c n", c=DC)
        wmod_r = tail_s[:].rearrange("p (c n) -> p c n", c=DC)
        sh_s = tail_s[:, 0:3 * SEQ].rearrange("p (m s) -> p m s", m=3)
        eg_s = tail_s[:, 3 * SEQ:5 * SEQ].rearrange("p (m s) -> p m s", m=2)
        tg_s = tail_s[:, 5 * SEQ:6 * SEQ]
        tmp_s = tail_s[:, 6 * SEQ:8 * SEQ].rearrange("p (t d) -> p t d", t=BT)
        out_tmp = tail_s[:].rearrange("p (b t d) -> p b t d", b=BATCH, t=BT)
        gb_prev = sb("gb_prev", [P, D])
        cand = [sb(f"cand{i}", [EXPERTS, CAP + SEQ]) for i in range(2)]
        ct_s = sb("ct_s", [P, DC, BATCH])
        ce_s = sb("ce_s", [P, DC, BATCH])
        modt_s = sb("modt_s", [P, 2, DC, BATCH])
        stat = sb("stat", [P, BT, 6])
        first_mv = sb("first_mv", [P, TT, 2])
        first_var = sb("first_var", [P, TT])
        first_rstd = sb("first_rstd", [P, TT])
        mv = sb("mv", [P, BT, 2])[:]
        var = sb("var", [P, BT])[:]
        half = sb("half", [P, BT])
        rstd = sb("rstd", [P, BT])[:]
        nmax = sb("nmax", [P, 2, 8])
        psum_p = sb("psum_p", [P, 2, 8])
        rinv = sb("rinv", [P, 2, 8])
        lg = sb("lg", [P, BT, EXPERTS + 2])
        rp = sb("rp", [P, BT, EXPERTS + 2])
        top = sb("top", [P, BT, 8])
        pick = sb("pick", [P, BT, 8])
        nv = sb("nv", [P, BT])
        sm = sb("sm", [P, BT])
        key = sb("key", [P, BT, EXPERTS])
        first = sb("first", [EXPERTS, CAP])
        tok_e = sb("tok_e", [EXPERTS, CAP])
        tok = sb("tok", [P, GROUPS])
        tok_f = sb("tok_f", [P, GROUPS])
        tok_i = sb("tok_i", [P, GROUPS], U32)
        w_slot = sb("w_slot", [P, 2])
        zero_s = sb("zero_s", [P, 512], BF16)

        mod_d = nc.dram_tensor("mod_d", (BATCH, 4 * D), F32, kind="Internal").ap()
        rows_d = nc.dram_tensor("rows_d", (T, ROW), F32, kind="Internal").ap()

        in_c, in_x0, in_x, in_mod_t, in_mod, in_ident = (sem("in_c"), sem("in_x0"), sem("in_x"), sem("in_mod_t"),
                                                         sem("in_mod"), sem("in_ident"))
        in_rope, in_mask, in_tail = sem("in_rope"), sem("in_mask"), sem("in_tail")
        in_chunk = [sem(f"in_chunk{k}") for k in range(CHUNKS)]
        w_hi_ready, w_lo_pool, w_lo_dve, h_hi_ready = (sem("w_hi_ready"), sem("w_lo_pool"), sem("w_lo_dve"),
                                                       sem("h_hi_ready"))
        in_iota, in_gb, in_modrow = sem("in_iota"), sem("in_gb"), sem("in_modrow")
        in_gu = [sem(f"in_gu{u}") for u in range(RING)]
        in_wd = [sem(f"in_wd{u}") for u in range(RING)]
        mod_stored, row_stored, out_stored = sem("mod_stored"), sem("row_stored"), sem("out_stored")
        ce_ready, silu_c, mod_mm, modt_mm, mod_rows, modt_ready = (
            sem("ce_ready"), sem("silu_c"), sem("mod_mm"), sem("modt_mm"), sem("mod_rows"), sem("modt_ready"))
        pre_step = sem("pre_step")
        consts, sentinels = sem("consts"), sem("sentinels")
        var1, rstd1, xn_ready, xt_full, xt_free = (sem("var1"), sem("rstd1"), sem("xn_ready"), sem("xt_full"),
                                                  sem("xt_free"))
        end_full, end_free, down_full, down_scaled = (sem("end_full"), sem("end_free"), sem("down_full"),
                                                      sem("down_scaled"))
        post_step = sem("post_step")
        h_ready, pj_full, sc_full, tr_full, wo_full, post_full = (
            sem("h_ready"), sem("pj_full"), sem("sc_full"), sem("tr_full"), sem("wo_full"), sem("post_full"))
        cos_done, swap_done, sin_done, rope_first, rope_rest = (
            sem("cos_done"), sem("swap_done"), sem("sin_done"), sem("rope_first"), sem("rope_rest"))
        v_hi, v_out, mix_hi, mix_out = sem("v_hi"), sem("v_out"), sem("mix_hi"), sem("mix_out")
        max_done, exp_done, rinv_done = sem("max_done"), sem("exp_done"), sem("rinv_done")
        norm_near, norm_far = sem("norm_near"), sem("norm_far")
        trans_hi, trans_out = sem("trans_hi"), sem("trans_out")
        wo_free, post_free, var2, rstd2, h2_ready = (sem("wo_free"), sem("post_free"), sem("var2"), sem("rstd2"),
                                                     sem("h2_ready"))
        nv_ready, se_ready, score_ready, key_ready, eg_ready, post_done = (
            sem("nv_ready"), sem("se_ready"), sem("score_ready"), sem("key_ready"), sem("eg_ready"), sem("post_done"))
        tok_step, tok_e_ready, tok_ready, first_zero = (sem("tok_step"), sem("tok_e_ready"), sem("tok_ready"),
                                                        sem("first_zero"))
        rows_in = [sem(f"rows_in{i}") for i in range(ROW_BUFS)]
        gt_full, hb_ready, gu_full, eg_x_ready, hid_ready = (
            sem("gt_full"), sem("hb_ready"), sem("gu_full"), sem("eg_x_ready"), sem("hid_ready"))
        ht_full, hid_t_ready, y_full, hi_ready, lo_ready = (sem("ht_full"), sem("hid_t_ready"), sem("y_full"),
                                                            sem("hi_ready"), sem("lo_ready"))
        w_ready, place_ready, back_done, exp_step, acc_done, out_scaled = (
            sem("w_ready"), sem("place_ready"), sem("back_done"), sem("exp_step"), sem("acc_done"), sem("out_scaled"))
        out_ready = [sem(f"out_ready{b}") for b in range(BATCH)]

        dve_passed, pe_passed, pool_passed = sem("dve_passed"), sem("pe_passed"), sem("pool_passed")

        POST_STEPS, EXP_STEPS = 20, 2

        def post_base(pb):
            if isinstance(pb, int) and pb == BATCH - 1:
                return POST_USES * (pb - 1) + len(IN_LAST)
            return POST_USES * pb

        def pj_release(b, n):
            if n in PJ_ROPE:
                return swap_done, 10 * b + PJ_ROPE.index(n) + 1
            if n in PJ_V:
                return v_out, 2 * b + PJ_V.index(n) + 1
            g = [n in m for m in PJ_MIX].index(True)
            return mix_out, 8 * b + 2 * g + PJ_MIX[g].index(n) + 1

        def work_release(b, n):
            if n < 0:
                return work_release(b - 1, n + WORK_USES)
            if n in WORK_SCORE:
                return exp_done, 12 * b + WORK_SCORE.index(n) + 1
            return trans_out, 12 * b + WORK_TRANS.index(n) + 1

        def heads_of(r):
            return k_s[:, 2 * r:2 * r + 2] if r < 2 else q_s[:, (r // 2 - 1) % 2, 2 * (r % 2):2 * (r % 2) + 2]

        def split(k):
            return (w_lo_pool, k + 1) if k < LOW_POOL else (w_lo_dve, k + 1 - LOW_POOL)

        def roped(b, r):
            return (rope_first, 4 * b + r + 1) if r < 4 else (rope_rest, 6 * b + r - 3)

        def gathered(g):
            return 16 * (g // ROW_BUFS + 1)

        block = ctx.enter_context(nc.Block())

        @block.sync
        def _(sp):
            wmod_d = wmod.rearrange("(c p) n -> p c n", p=P)
            x_d = x.rearrange("b (t p) d -> p (b t) d", p=P)
            sp.dma_start(ct_s[:], c_t.rearrange("(c p) b -> p c b", p=P)).then_inc(in_c, 16)
            sp.dma_start(wmod_t, wmod_d[:, :, 0:2 * D]).then_inc(in_mod_t, 16)
            sp.dma_start(x_s[:, 0:BT, :], x_d[:, 0:BT, :]).then_inc(in_x0, 16)
            sp.dma_start(ident[:], masks[:, 2, :]).then_inc(in_ident, 16)

            def load_chunk(k):
                if k in CH_O:
                    g, n = CH_O.index(k), GROUP * HD
                    src, parts = wo[g * n:(g + 1) * n, :].rearrange("(h p) n -> p h n", p=P), GROUP
                elif k in CH_Q:
                    g, n = CH_Q.index(k), GROUP * HD
                    src, parts = wq.rearrange("(c p) n -> p c n", p=P)[:, :, g * n:(g + 1) * n], DC
                else:
                    src, parts = (wk if k == CH_K else wv).rearrange("(c p) n -> p c n", p=P), DC
                sp.dma_start(loaded(k).rearrange("p (c n) -> p c n", c=parts), src).then_inc(in_chunk[k], 16)

            load_chunk(CH_K)
            load_chunk(CH_Q[0])
            sp.dma_start(rope_s, rope).then_inc(in_rope, 16)
            load_chunk(CH_V)
            load_chunk(CH_Q[1])
            sp.dma_start(mask_in, masks).then_inc(in_mask, 16)
            sp.dma_start(wmod_r, wmod_d[:, :, 2 * D:]).then_inc(in_mod, 16)
            sp.dma_start(x_s[:, BT:, :], x_d[:, BT:, :]).then_inc(in_x, 16)
            for k in (*CH_Q[2:], *CH_O):
                load_chunk(k)
            sp.dma_start(small_s[:], small).then_inc(in_tail, 16)
            sp.dma_start(gate_s[:], gate_t.rearrange("(c p) n -> p c n", p=P)).then_inc(in_tail, 16)
            sp.dma_start(swg_s[:], sw_gate.rearrange("(c p) n -> p c n", p=P)).then_inc(in_tail, 16)
            sp.dma_start(swu_s[:], sw_up.rearrange("(c p) n -> p c n", p=P)).then_inc(in_tail, 16)
            sp.dma_start(swd_s[:, 0:2, :], sw_down[0:256, :].rearrange("(m p) n -> p m n", p=P)).then_inc(in_tail, 16)
            sp.dma_start(swd_s[0:SM[2], 2, :], sw_down[256:SHARED, :]).then_inc(in_tail, 16)

            def load_gate_up(u, g):
                gu, wa, wb = slot(u)
                for m, w in enumerate((w_gate, w_up)):
                    sp.dma_start(gu[:, m].rearrange("p j c i -> p (j c i)"),
                                 w[bass.ds(g, 1)].rearrange("g p n -> (g p) n")).then_inc(in_gu[u], 16)

            def load_down(u, g):
                gu, wa, wb = slot(u)
                sp.dma_start(wa.rearrange("p j d -> p (j d)"),
                             w_down_a[bass.ds(g, 1)].rearrange("g p n -> (g p) n")).then_inc(in_wd[u], 16)
                sp.dma_start(wb.rearrange("p j d -> p (j d)"),
                             w_down_b[bass.ds(g, 1)].rearrange("g p n -> (g p) n")).then_inc(in_wd[u], 16)

            def load_slot(u, g):
                load_gate_up(u, g)
                load_down(u, g)

            sp.wait_ge(mod_rows, 4)
            sp.dma_start(mod_d, modr_s).then_inc(mod_stored, 16)
            sp.wait_ge(mod_stored, 16)
            sp.dma_start(mod_s[:], mod_d[0, :].partition_broadcast(P)).then_inc(in_modrow, 16)

            def row_step(b):
                sp.wait_ge(score_ready, b)
                row = bass.ds((b - 1) * SEQ, SEQ)
                sp.dma_start(rows_d[row, :].rearrange("(t p) n -> p t n", p=P), row_s[:]).then_inc(row_stored, 16)
                sp.wait_ge(row_stored, 16 * b)
                if isinstance(b, int):
                    sp.wait_ge(pj_full, PJ_USES * b + PJ_ROPE[-1] + 1)
                    load_slot(0, 0)
                    load_slot(1, 1)
                    sp.wait_ge(*roped(b, 9))
                    load_slot(2, 2)
                    sp.wait_ge(wo_full, KV_HEADS * b + 2)
                    load_slot(3, 3)
                sp.wait_ge(h2_ready if isinstance(b, int) else post_done, b)
                sp.dma_start(mod_s[:], mod_d[bass.ds(b, 1), :].rearrange("b n -> (b n)").partition_broadcast(P))\
                  .then_inc(in_modrow, 16)

            with sp.Fori(1, BATCH - 1) as b:
                row_step(b)
            row_step(BATCH - 1)
            sp.wait_ge(wo_full, KV_HEADS * BATCH)
            load_slot(4, 4)
            sp.dma_start(iota_s, iota_row.partition_broadcast(P)).then_inc(in_iota, 16)
            load_slot(5, 5)
            for b in range(BATCH):
                sp.dma_start(gb_all[:, b, :], mod_d[b, 3 * D:4 * D].partition_broadcast(P)).then_inc(in_gb, 16)
            for g in range(RING, GROUPS + 1):
                if g < GROUPS:
                    sp.wait_ge(gu_full, g - RING + 1)
                    load_gate_up(g % RING, g)
                if g > RING:
                    sp.wait_ge(y_full, g - RING)
                    load_down((g - 1) % RING, g - 1)
            for b in range(BATCH):
                sp.wait_ge(out_ready[b], 1)
                sp.dma_start(out[b].rearrange("(t p) d -> p t d", p=P), x_s[:, BT * b:BT * b + BT, :])\
                  .then_inc(out_stored, 16)
            sp.wait_ge(out_stored, 16 * BATCH)
            sp.wait_ge(row_stored, 16 * BATCH)

        @block.gpsimd
        def _(pool):
            nc.gpsimd.memset(half[:], -0.5).then_inc(sentinels, 1)
            nc.gpsimd.memset(lg[:, :, EXPERTS:], -BIG).then_inc(sentinels, 1)
            nc.gpsimd.memset(pick[:, :, TOPK:], -BIG).then_inc(sentinels, 1)
            nc.gpsimd.memset(zero_s[:], 0.0).then_inc(sentinels, 1)
            pool.wait_ge(sentinels, 1)

            def first_norm(b):
                pool.wait_ge(var1, b + 1)
                tiles = slice(b * BT, (b + 1) * BT)
                nc.gpsimd.tensor_tensor(first_rstd[:, tiles], first_var[:, tiles], half[:], ALU.pow).then_inc(rstd1, 1)

            def split_low(k):
                pool.wait_ge(w_hi_ready, k + 1)
                nc.gpsimd.tensor_tensor(chunk(k)[:, 1], loaded(k), chunk(k)[:, 0].bitcast(F32),
                                        ALU.subtract).then_inc(w_lo_pool, 1)

            first_norm(0)
            for k in range(LOW_POOL):
                split_low(k)
            pool.wait_ge(in_rope, 16)

            def sines(b, r):
                pool.wait_ge(swap_done, 10 * b + r + 1)
                sin = rope_s[:, 3 if r < 2 else 1, :]
                nc.gpsimd.tensor_tensor(swap_s[:, r % 2], swap_s[:, r % 2],
                                        sin.unsqueeze(1).to_broadcast([P, 2, SEQ]), ALU.mult).then_inc(sin_done, 1)
                if r >= 4:
                    pool.wait_ge(sin_done, 10 * b + r + 1)
                    nc.gpsimd.tensor_tensor(heads_of(r), heads_of(r), swap_s[:, r % 2], ALU.add)\
                      .then_inc(rope_rest, 1)

            def normalise(b, g):
                pool.wait_ge(rinv_done, 4 * b + g + 1)
                for t in range(BT):
                    probs = prob_far[:, g % 2, :, t * P:(t + 1) * P]
                    nc.gpsimd.tensor_tensor(probs, probs,
                                            rinv[:, g % 2, GROUP:].unsqueeze(2).to_broadcast([P, GROUP, P]),
                                            ALU.mult).then_inc(norm_far, 1)

            def row_step(b, tail):
                if tail:
                    pool.wait_ge(pj_full, PJ_USES * (b - 1) + PJ_ROPE[-1] + 1)
                    row = h_all[:, :, bass.ds(b * SEQ, SEQ)]
                    nc.gpsimd.tensor_copy(h_cur[:, 0], row).then_inc(h_hi_ready, 1)
                    pool.wait_ge(h_hi_ready, b)
                    alone(pool, pool_passed)
                    nc.gpsimd.tensor_tensor(h_cur[:, 1], row, h_cur[:, 0].bitcast(F32), ALU.subtract)\
                      .then_inc(h_ready, 1)
                sines(b, 0)
                sines(b, 1)
                sines(b, 2)
                sines(b, 3)
                if tail:
                    pool.wait_ge(var2, b)
                    nc.gpsimd.tensor_tensor(rstd, var, half[:], ALU.pow).then_inc(rstd2, 1)
                else:
                    first_norm(1)
                sines(b, 4)
                sines(b, 5)
                sines(b, 6)
                normalise(b, 0)
                sines(b, 7)
                sines(b, 8)
                normalise(b, 1)
                sines(b, 9)
                if not tail:
                    first_norm(2)
                normalise(b, 2)
                if not tail:
                    first_norm(3)
                normalise(b, 3)

            row_step(0, False)
            with pool.Fori(1, BATCH - 1) as b:
                row_step(b, True)
            row_step(BATCH - 1, True)
            pool.wait_ge(var2, BATCH)
            nc.gpsimd.tensor_tensor(rstd, var, half[:], ALU.pow).then_inc(rstd2, 1)

            pool.wait_ge(tok_ready, 1)
            pool.wait_ge(row_stored, 16 * BATCH)
            for g in range(GROUPS):
                if g >= ROW_BUFS:
                    pool.wait_ge(gt_full, g - ROW_BUFS + 1)
                    pool.wait_ge(w_ready, g - ROW_BUFS + 1)
                nc.gpsimd.indirect_dma_start(
                    rows_s[:, g % ROW_BUFS, :], None, rows_d, bass.IndirectOffsetOnAxis(tok_i[:, g:g + 1], axis=0),
                    bounds_check=T - 1, oob_is_err=False).then_inc(rows_in[g % ROW_BUFS], 16)

            for b in POOL_OUT:
                pool.wait_ge(out_scaled, b + 1)
                tiles = x_s[:, BT * b:BT * b + BT, :]
                nc.gpsimd.tensor_tensor(tiles, tiles, out_tmp[:, b], ALU.add).then_inc(out_ready[b], 1)

        @block.scalar
        def _(act):
            act.wait_ge(in_c, 16)
            nc.scalar.activation(ce_s[:], ct_s[:], ACT.Exp, scale=-1.0).then_inc(ce_ready, 1)

            def swap(b, r):
                act.wait_ge(cos_done, 10 * b + r + 1)
                need(act, *(roped(b, r - 2) if r >= 2 else roped(b - 1, r + 8)))
                src = pj[PJ_ROPE[r] % 2][:].rearrange("p (h s) -> p h s", h=2)
                nc.scalar.activation(swap_s[0:64, r % 2], src[64:128], ACT.Copy)
                nc.scalar.activation(swap_s[64:128, r % 2], src[0:64], ACT.Copy).then_inc(swap_done, 1)

            def split_high(k):
                act.wait_ge(in_chunk[k], 16)
                if k == CH_O[3]:
                    act.wait_ge(modt_mm, 1)
                nc.scalar.activation(chunk(k)[:, 0], loaded(k), ACT.Copy).then_inc(w_hi_ready, 1)

            def values(b, t):
                act.wait_ge(pj_full, PJ_USES * b + PJ_V[t] + 1)
                nc.scalar.activation(v_s[:, 0, t, :], pj[PJ_V[t] % 2][:], ACT.Copy).then_inc(v_hi, 1)

            def exps(b, s):
                g, i = divmod(s, 3)
                act.wait_ge(max_done, 12 * b + s + 1)
                scores = work[WORK_SCORE[s] % 4]
                heads = range(GROUP) if i == 0 else (2 * i - 2, 2 * i - 1)
                for n, h in enumerate(heads):
                    w = P if i == 0 else SEQ
                    col = h if i == 0 else GROUP + h
                    dst = prob_near if i == 0 else prob_far
                    last = nc.scalar.activation(dst[:, g % 2, h, :], scores[:, n * w:(n + 1) * w], ACT.Exp,
                                                bias=nmax[:, g % 2, col:col + 1],
                                                accum_out=psum_p[:, g % 2, col:col + 1])
                last.then_inc(exp_done, 1)

            def take_probs(b, g):
                for i in range(3):
                    act.wait_ge(tr_full, 12 * b + 3 * g + i + 1)
                    nc.scalar.activation(prob_t[:, i, 0], work[WORK_TRANS[3 * g + i] % 4][:], ACT.Copy)\
                      .then_inc(trans_hi, 1)

            def take_mix(b, g):
                for t, n in enumerate(PJ_MIX[g]):
                    act.wait_ge(pj_full, PJ_USES * b + n + 1)
                    nc.scalar.activation(mix_s[:, g % 2, t, 0], pj[n % 2][:], ACT.Copy).then_inc(mix_hi, 1)

            def router_exp(pb):
                act.wait_ge(nv_ready, pb + 1)
                for t in range(BT):
                    last = nc.scalar.activation(row_s[:, t, D:ROW], lg[:, t, 0:EXPERTS], ACT.Exp,
                                                bias=nv[:, t:t + 1], accum_out=sm[:, t:t + 1])
                last.then_inc(se_ready, 1)

            def shared_tanh(pb, m):
                act.wait_ge(post_full, post_base(pb) + IN_LOOP.index(f"gu{m}") + 1)
                nc.scalar.activation(eg_s[0:SM[m], m % 2], post[0:SM[m], 0:SEQ], ACT.Tanh, scale=0.5)\
                  .then_inc(eg_ready, 1)

            def row_step(b, tail, shared=True):
                swap(b, 0)
                swap(b, 1)
                swap(b, 2)
                swap(b, 3)
                values(b, 0)
                values(b, 1)
                if not tail:
                    split_high(4)
                swap(b, 4)
                exps(b, 0)
                swap(b, 5)
                exps(b, 1)
                exps(b, 2)
                swap(b, 6)
                if not tail:
                    split_high(5)
                swap(b, 7)
                if tail:
                    router_exp(b - 1)
                if tail and shared:
                    shared_tanh(b - 1, 0)
                exps(b, 3)
                if not tail:
                    split_high(6)
                exps(b, 4)
                exps(b, 5)
                if tail and shared:
                    shared_tanh(b - 1, 1)
                swap(b, 8)
                take_probs(b, 0)
                swap(b, 9)
                exps(b, 6)
                exps(b, 7)
                take_mix(b, 0)
                if tail and shared:
                    shared_tanh(b - 1, 2)
                if not tail:
                    split_high(7)
                exps(b, 8)
                take_probs(b, 1)
                exps(b, 9)
                exps(b, 10)
                take_mix(b, 1)
                if not tail:
                    split_high(8)
                exps(b, 11)
                take_probs(b, 2)
                take_mix(b, 2)
                if not tail:
                    split_high(9)
                take_probs(b, 3)
                take_mix(b, 3)

            for k in range(LOW_POOL):
                split_high(k)
            row_step(0, False)
            with act.Fori(1, BATCH - 1) as b:
                row_step(b, True)
            row_step(BATCH - 1, True, shared=False)

            def end_tanh(n):
                act.wait_ge(end_full, n + 1)
                need(act, end_free, n - 1)
                nc.scalar.activation(eg_s[0:SM[n % 3], n % 2], end_bank[n % 3][0:SM[n % 3], 0:SEQ], ACT.Tanh,
                                     scale=0.5).then_inc(eg_ready, 1)

            for n in range(3):
                end_tanh(n)
            router_exp(BATCH - 1)
            act.wait_ge(score_ready, BATCH)
            nc.scalar.dma_start(rows_d[(BATCH - 1) * SEQ:T, :].rearrange("(t p) n -> p t n", p=P),
                                row_s[:]).then_inc(row_stored, 16)
            for n in range(3, 6):
                end_tanh(n)

            def group_step(g, u, rows=True, ends=True):
                if rows:
                    act.wait_ge(gt_full, g + 1)
                    nc.scalar.activation(hb_t[:, u % 2], gt_bank[:, 0:DC * P].rearrange("p (c s) -> p c s", c=DC),
                                         ACT.Copy).then_inc(hb_ready, 1)
                if ends:
                    act.wait_ge(ht_full, g)
                    nc.scalar.activation(hid_ta, ht_bank[0:IA, 0:P], ACT.Copy)
                    nc.scalar.activation(hid_tb, ht_bank[0:IB, P:2 * P], ACT.Copy).then_inc(hid_t_ready, 1)
                if rows:
                    act.wait_ge(gu_full, g + 1)
                    nc.scalar.activation(eg_x, gu_bank[:, 0:INTER], ACT.Tanh, scale=0.5).then_inc(eg_x_ready, 1)
                if ends:
                    act.wait_ge(y_full, g)
                    act.wait_ge(w_ready, g)
                    v = (u + 1) % 2
                    need(act, back_done, g - 2)
                    nc.scalar.activation(y_hi[v][:], y_bank[:, 0:D], ACT.Copy, scale=w_slot[:, v:v + 1])\
                      .then_inc(hi_ready, 1)

            for u in range(PEELED):
                group_step(u, u, ends=u > 0)
            with act.Fori(0, ROUNDS) as k:
                for i in range(RING):
                    group_step(RING * k + (PEELED + i), (PEELED + i) % RING)
            group_step(GROUPS, GROUPS % RING, rows=False)

        @block.vector
        def _(dve):
            V = nc.vector
            pre = Steps(dve, pre_step, 0)
            dve.wait_ge(ce_ready, 1)
            pre.done(V.tensor_scalar(ce_s[:], ce_s[:], 1.0, None, ALU.add))
            pre.wait()
            pre.done(V.reciprocal(ce_s[:], ce_s[:]))
            pre.wait()
            V.tensor_tensor(ct_s[:], ct_s[:], ce_s[:], ALU.mult).then_inc(silu_c, 1)

            def norm_stats(step, tile0, var_sem, mv=mv, var=var):
                for t in range(BT):
                    last = V.bn_stats(stat[:, t, :], x_s[:, bass.ds(tile0 + t, 1), :].rearrange("p t d -> p (t d)"))
                step.done(last)
                step.wait()
                alone(dve, dve_passed)
                for t in range(BT):
                    last = V.bn_aggr(mv[:, t, :], stat[:, t, :])
                step.done(last)
                step.wait()
                V.tensor_scalar(var, mv[:, :, 1], EPS, None, ALU.add).then_inc(var_sem, 1)

            def norm_apply(dst, tile0, t, mv=mv, rstd=rstd):
                return V.tensor_scalar(dst, x_s[:, bass.ds(tile0 + t, 1), :].rearrange("p t d -> p (t d)"),
                                       mv[:, t, 0:1], rstd[:, t:t + 1], ALU.subtract, ALU.mult)

            def first_stats(b):
                dve.wait_ge(in_x0 if b == 0 else in_x, 16)
                norm_stats(pre, b * BT, var1, first_mv[:, b * BT:(b + 1) * BT], first_var[:, b * BT:(b + 1) * BT])

            def first_apply(b):
                dve.wait_ge(rstd1, b + 1)
                for t in range(BT):
                    last = norm_apply(xn_s[:, t, :], b * BT, t, first_mv[:, b * BT:(b + 1) * BT],
                                      first_rstd[:, b * BT:(b + 1) * BT])
                last.then_inc(xn_ready, 1)

            def first_take(b):
                dve.wait_ge(xt_full, b + 1)
                dve.wait_ge(modt_ready, 2)
                xt = post[:].rearrange("p (c s) -> p c s", c=DC)
                row = h_all[:, :, b * SEQ:(b + 1) * SEQ]
                for c in range(DC):
                    last = V.tensor_scalar(row[:, c], xt[:, c], modt_s[:, 1, c, b:b + 1], modt_s[:, 0, c, b:b + 1],
                                           ALU.mult, ALU.add)
                last.then_inc(xt_free, 1)
                if b == 0:
                    dve.wait_ge(xt_free, 1)
                    pre.done(V.tensor_copy(h_cur[:, 0], row))
                    pre.wait()
                    V.tensor_tensor(h_cur[:, 1], row, h_cur[:, 0].bitcast(F32), ALU.subtract).then_inc(h_ready, 1)

            def take_modulation(m):
                dve.wait_ge(mod_mm, m + 1)
                if m == 0:
                    V.tensor_copy(modr_s[:, D:2 * D], post[0:BATCH, D:2 * D]).then_inc(mod_rows, 1)
                else:
                    V.tensor_scalar(modr_s[:, 2 * D:3 * D], post[0:BATCH, 0:D], 1.0, None, ALU.add)\
                     .then_inc(mod_rows, 1)
                src, at = (post[0:BATCH, 0:D], 0) if m == 0 else (post[0:BATCH, D:2 * D], 3 * D)
                sign, size = modq_s[:, 0], modq_s[:, 1]
                pre.done(V.tensor_scalar(sign, src, 0.0, 2.0, ALU.is_ge, ALU.mult))
                pre.wait()
                pre.done(V.tensor_scalar(sign, sign, -1.0, None, ALU.add))
                pre.wait()
                pre.done(V.tensor_tensor(size, src, sign, ALU.mult))
                pre.wait()
                V.scalar_tensor_tensor(modr_s[:, at:at + D], size, 0.25, sign, ALU.max, ALU.mult)\
                 .then_inc(mod_rows, 1)

            first_stats(0)
            first_apply(0)
            dve.wait_ge(modt_mm, 1)
            mt = wo_bank[:, 0:16].rearrange("p (m c b) -> p m c b", m=2, c=DC)
            V.tensor_copy(modt_s[:, 0], mt[:, 0]).then_inc(modt_ready, 1)
            V.tensor_scalar(modt_s[:, 1], mt[:, 1], 1.0, None, ALU.add).then_inc(modt_ready, 1)
            first_take(0)

            dve.wait_ge(in_mask, 16)
            V.tensor_copy(mask_near[:], mask_in[:, 0].unsqueeze(1).to_broadcast([P, GROUP, P])).then_inc(consts, 1)
            V.tensor_copy(mask_far[:, :, 0], mask_in[:, 1].unsqueeze(1).to_broadcast([P, 2, P])).then_inc(consts, 1)
            V.tensor_copy(mask_far[:, :, 1], mask_in[:, 0].unsqueeze(1).to_broadcast([P, 2, P])).then_inc(consts, 1)
            V.tensor_copy(ident_b[:], mask_in[:, 2]).then_inc(consts, 1)
            dve.wait_ge(consts, 4)
            dve.wait_ge(in_rope, 16)

            def split_low(k):
                dve.wait_ge(w_hi_ready, k + 1)
                V.tensor_tensor(chunk(k)[:, 1], loaded(k), chunk(k)[:, 0].bitcast(F32), ALU.subtract)\
                 .then_inc(w_lo_dve, 1)

            def cosines(b, r):
                dve.wait_ge(pj_full, PJ_USES * b + PJ_ROPE[r] + 1)
                cos = rope_s[:, 2 if r < 2 else 0, :].unsqueeze(1).to_broadcast([P, 2, SEQ])
                V.tensor_tensor(heads_of(r), pj[PJ_ROPE[r] % 2][:].rearrange("p (h s) -> p h s", h=2), cos,
                                ALU.mult).then_inc(cos_done, 1)

            def rotate(b, r):
                dve.wait_ge(sin_done, 10 * b + r + 1)
                dve.wait_ge(cos_done, 10 * b + r + 1)
                V.tensor_tensor(heads_of(r), heads_of(r), swap_s[:, r % 2], ALU.add).then_inc(rope_first, 1)

            def maxima(b, s):
                g, i = divmod(s, 3)
                dve.wait_ge(sc_full, 12 * b + s + 1)
                heads = GROUP if i == 0 else 2
                lo = 0 if i == 0 else GROUP + 2 * (i - 1)
                V.tensor_reduce(nmax[:, g % 2, lo:lo + heads],
                                work[WORK_SCORE[s] % 4][:].rearrange("p (h k) -> p h k", h=heads),
                                AX_X, ALU.max, negate=True).then_inc(max_done, 1)

            def inverses(b, g):
                dve.wait_ge(exp_done, 12 * b + 3 * g + 3)
                V.reciprocal(rinv[:, g % 2], psum_p[:, g % 2]).then_inc(rinv_done, 1)
                dve.wait_ge(rinv_done, 4 * b + g + 1)
                V.tensor_tensor(prob_near[:, g % 2], prob_near[:, g % 2],
                                rinv[:, g % 2, 0:GROUP].unsqueeze(2).to_broadcast([P, GROUP, P]),
                                ALU.mult).then_inc(norm_near, 1)

            def values(b, t):
                dve.wait_ge(v_hi, 2 * b + t + 1)
                V.tensor_tensor(v_s[:, 1, t, :], pj[PJ_V[t] % 2][:], v_s[:, 0, t, :].bitcast(F32), ALU.subtract)\
                 .then_inc(v_out, 1)

            def take_probs(b, g):
                for i in range(3):
                    dve.wait_ge(trans_hi, 12 * b + 3 * g + i + 1)
                    V.tensor_tensor(prob_t[:, i, 1], work[WORK_TRANS[3 * g + i] % 4][:],
                                    prob_t[:, i, 0].bitcast(F32), ALU.subtract).then_inc(trans_out, 1)

            def take_mix(b, g):
                for t, n in enumerate(PJ_MIX[g]):
                    dve.wait_ge(mix_hi, 8 * b + 2 * g + t + 1)
                    V.tensor_tensor(mix_s[:, g % 2, t, 1], pj[n % 2][:], mix_s[:, g % 2, t, 0].bitcast(F32),
                                    ALU.subtract).then_inc(mix_out, 1)

            class Tail:

                def __init__(self, pb, order):
                    steps = pb * POST_STEPS
                    if order == AT_END:
                        steps += 1 - 3
                    self.pb, self.order, self.step = pb, order, Steps(dve, post_step, steps)
                    self.shared = order == IN_LOOP
                    self.tiles = x_s[:, bass.ds(pb * BT, BT), :]

                def residual(self):
                    dve.wait_ge(wo_full, KV_HEADS * (self.pb + 1))
                    dve.wait_ge(in_modrow, 16 * (self.pb + 1))
                    V.tensor_tensor(tmp_s[:], wo_bank[:].rearrange("p (t d) -> p t d", t=BT),
                                    mod_s[:, 0:D].unsqueeze(1).to_broadcast([P, BT, D]), ALU.mult)\
                     .then_inc(wo_free, 1)

                def residual_add(self):
                    dve.wait_ge(wo_free, self.pb + 1)
                    self.step.done(V.tensor_tensor(self.tiles, self.tiles, tmp_s[:], ALU.add))
                    self.step.wait()

                def stats(self):
                    norm_stats(self.step, self.pb * BT, var2)

                def rows(self):
                    dve.wait_ge(rstd2, self.pb + 1)
                    for t in range(BT):
                        last = norm_apply(row_s[:, t, 0:D], self.pb * BT, t)
                    self.step.done(last)

                def rows_modulate(self):
                    self.step.wait()
                    self.step.done(V.tensor_tensor(row_s[:, :, 0:D], row_s[:, :, 0:D],
                                                   mod_s[:, 2 * D:3 * D].unsqueeze(1).to_broadcast([P, BT, D]),
                                                   ALU.mult))
                    self.step.wait()
                    V.tensor_tensor(row_s[:, :, 0:D], row_s[:, :, 0:D],
                                    mod_s[:, D:2 * D].unsqueeze(1).to_broadcast([P, BT, D]), ALU.add)\
                     .then_inc(h2_ready, 1)

                def full(self, use):
                    dve.wait_ge(post_full, post_base(self.pb) + self.order.index(use) + 1)

                def take_h(self):
                    self.full("h_t")
                    if self.order == AT_END:
                        dve.wait_ge(end_full, 3)
                    V.tensor_copy(h_t[:], post[:].rearrange("p (c s) -> p c s", c=DC)).then_inc(post_free, 1)

                def top6(self):
                    self.full("logits")
                    V.tensor_copy(lg[:, :, 0:EXPERTS], post[:, 0:BT * EXPERTS].rearrange("p (t e) -> p t e", t=BT))\
                     .then_inc(post_free, 1)
                    dve.wait_ge(post_free, post_base(self.pb) + self.order.index("logits") + 1)
                    alone(dve, dve_passed)
                    for t in range(BT):
                        last = V.max(top[:, t, :], lg[:, t, 0:EXPERTS])
                    self.step.done(last)
                    self.step.wait()
                    V.tensor_scalar(nv[:], top[:, :, 0], -1.0, None, ALU.mult).then_inc(nv_ready, 1)
                    self.step.done(V.tensor_copy(pick[:, :, 0:TOPK], top[:, :, 0:TOPK]))
                    self.step.wait()
                    alone(dve, dve_passed)
                    for t in range(BT):
                        last = V.match_replace(rp[:, t, :], pick[:, t, :], lg[:, t, :], BIG)
                    self.step.done(last)
                    self.step.wait()
                    for t in range(BT):
                        last = V.tensor_scalar(key[:, t, :], rp[:, t, 0:EXPERTS], BIG / 2,
                                               rank[:, bass.ds(self.pb * BT + t, 1)], ALU.is_ge, ALU.mult)
                    last.then_inc(key_ready, 1)

                def scores(self):
                    dve.wait_ge(se_ready, self.pb + 1)
                    self.step.done(V.reciprocal(sm[:], sm[:]))
                    self.step.wait()
                    for t in range(BT):
                        last = V.tensor_scalar(row_s[:, t, D:ROW], row_s[:, t, D:ROW], sm[:, t:t + 1], None, ALU.mult)
                    last.then_inc(score_ready, 1)

                def hidden(self, n, eg, src, free):
                    m = n % 3
                    k = SM[m]
                    self.step.done(V.scalar_tensor_tensor(tg_s[0:k], eg[0:k], 1.0, src[0:k, 0:SEQ],
                                                          ALU.add, ALU.mult))
                    self.step.wait()
                    V.scalar_tensor_tensor(sh_s[0:k, m], src[0:k, SEQ:2 * SEQ], 0.5, tg_s[0:k], ALU.mult, ALU.mult)\
                     .then_inc(free, 1)

                def shared_hidden(self, m):
                    dve.wait_ge(eg_ready, 3 * self.pb + m + 1)
                    self.hidden(m, eg_s[:, m % 2], post, post_free)

                def end_hidden(self, n):
                    dve.wait_ge(eg_ready, 3 * (BATCH - 2) + n + 1)
                    need(dve, end_free, n)
                    if n == 3:
                        dve.wait_ge(down_full, 1)
                    self.hidden(n, eg_s[:, n % 2], end_bank[n % 3], end_free)

                def take_key(self):
                    self.full("key_t")
                    V.tensor_copy(cand[0][:, CAP:], post[0:EXPERTS, 0:SEQ]).then_inc(post_free, 1)

                def first_round(self, r):
                    if r == 0:
                        dve.wait_ge(post_free, post_base(self.pb) + self.order.index("key_t") + 1)
                        self.step.done(V.tensor_copy(cand[0][:, 0:CAP], first[:]))
                        self.step.wait()
                    alone(dve, dve_passed)
                    self.step.done(V.max(first[:, 8 * r:8 * r + 8], cand[r % 2][:]))
                    self.step.wait()
                    if r < CAP // 8 - 1:
                        alone(dve, dve_passed)
                        self.step.done(V.match_replace(cand[(r + 1) % 2][:], first[:, 8 * r:8 * r + 8],
                                                       cand[r % 2][:], -1.0))
                        self.step.wait()

                def keep_gate(self):
                    self.step.done(V.tensor_copy(gb_prev[:], mod_s[:, 3 * D:4 * D]))

                def shared_out_before(self):
                    dve.wait_ge(down_full, 1)
                    V.tensor_tensor(tmp_s[:], acc[3][:].rearrange("p (t d) -> p t d", t=BT),
                                    gb_prev[:].unsqueeze(1).to_broadcast([P, BT, D]), ALU.mult)\
                     .then_inc(down_scaled, 1)
                    dve.wait_ge(down_scaled, 1)
                    tiles = x_s[:, BT * (self.pb - 1):BT * self.pb, :]
                    V.tensor_tensor(tiles, tiles, tmp_s[:], ALU.add).then_inc(post_done, 1)

                def shared_out(self):
                    self.full("down")
                    if self.order == AT_END:
                        dve.wait_ge(post_done, BATCH - 1)
                    V.tensor_tensor(tmp_s[:], post[:].rearrange("p (t d) -> p t d", t=BT),
                                    mod_s[:, 3 * D:4 * D].unsqueeze(1).to_broadcast([P, BT, D]), ALU.mult)\
                     .then_inc(post_free, 1)
                    dve.wait_ge(post_free, post_base(self.pb) + len(self.order))
                    V.tensor_tensor(self.tiles, self.tiles, tmp_s[:], ALU.add).then_inc(post_done, 1)

            def row_step(b, tail):
                cosines(b, 0)
                cosines(b, 1)
                rotate(b, 0)
                cosines(b, 2)
                rotate(b, 1)
                cosines(b, 3)
                if tail:
                    tail.residual()
                rotate(b, 2)
                values(b, 0)
                if tail:
                    tail.residual_add()
                rotate(b, 3)
                values(b, 1)
                if tail:
                    tail.stats()
                else:
                    first_stats(1)
                cosines(b, 4)
                maxima(b, 0)
                if tail:
                    if not tail.shared:
                        tail.keep_gate()
                    tail.rows()
                else:
                    split_low(4)
                cosines(b, 5)
                if tail:
                    tail.rows_modulate()
                else:
                    first_apply(1)
                maxima(b, 1)
                maxima(b, 2)
                if tail:
                    tail.take_h()
                cosines(b, 6)
                if not tail:
                    take_modulation(0)
                inverses(b, 0)
                cosines(b, 7)
                if tail:
                    tail.top6()
                maxima(b, 3)
                if tail and tail.shared:
                    tail.shared_hidden(0)
                if not tail:
                    first_take(1)
                maxima(b, 4)
                if tail:
                    tail.scores()
                else:
                    split_low(5)
                maxima(b, 5)
                if tail and tail.shared:
                    tail.shared_hidden(1)
                cosines(b, 8)
                inverses(b, 1)
                cosines(b, 9)
                take_probs(b, 0)
                if tail:
                    tail.take_key()
                else:
                    first_stats(2)
                maxima(b, 6)
                maxima(b, 7)
                if not tail:
                    split_low(6)
                take_mix(b, 0)
                if tail and tail.shared:
                    tail.shared_hidden(2)
                maxima(b, 8)
                if tail:
                    tail.first_round(0)
                else:
                    take_modulation(1)
                    split_low(7)
                take_probs(b, 1)
                maxima(b, 9)
                inverses(b, 2)
                maxima(b, 10)
                maxima(b, 11)
                take_mix(b, 1)
                if tail:
                    tail.first_round(1)
                else:
                    first_stats(3)
                take_probs(b, 2)
                inverses(b, 3)
                if not tail:
                    first_apply(2)
                    split_low(8)
                take_mix(b, 2)
                if tail:
                    tail.first_round(2)
                else:
                    first_take(2)
                    first_apply(3)
                    split_low(9)
                take_probs(b, 3)
                if tail:
                    tail.first_round(3)
                    if tail.shared:
                        tail.shared_out()
                take_mix(b, 3)
                if not tail:
                    first_take(3)

            V.memset(first[:], 0.0).then_inc(first_zero, 1)
            dve.wait_ge(first_zero, 1)
            row_step(0, None)
            with dve.Fori(1, BATCH - 1) as b:
                tail = Tail(b - 1, IN_LOOP)
                row_step(b, tail)
                assert tail.step.n == POST_STEPS, tail.step.n
            tail = Tail(BATCH - 2, IN_LAST)
            row_step(BATCH - 1, tail)
            assert tail.step.n == POST_STEPS + 1 - 3, tail.step.n
            tail = Tail(BATCH - 1, AT_END)
            tail.residual()
            tail.residual_add()
            tail.stats()
            tail.end_hidden(0)
            tail.rows()
            tail.rows_modulate()
            tail.end_hidden(1)
            tail.take_h()
            tail.end_hidden(2)
            tail.top6()
            tail.scores()
            tail.take_key()
            for r in range(CAP // 8):
                tail.first_round(r)
            V.tensor_scalar(tok_e[:], first[:], -1.0, float(T), ALU.mult, ALU.add).then_inc(tok_e_ready, 1)
            step = Steps(dve, tok_step, 0)
            tail.end_hidden(3)
            tail.full("tok_t")
            for j in range(PER):
                last = V.tensor_copy(tok[CAP * j:CAP * j + CAP, :],
                                     post[0:CAP, 0:EXPERTS].rearrange("p (g j) -> p g j", j=PER)[:, :, j])
            last.then_inc(post_free, 1)
            dve.wait_ge(post_free, post_base(BATCH - 1) + AT_END.index("tok_t") + 1)
            step.done(V.tensor_scalar(tok_f[:], tok[:], float(T - 1), None, ALU.min))
            step.wait()
            V.tensor_copy(tok_i[:], tok_f[:]).then_inc(tok_ready, 1)
            tail.end_hidden(4)
            tail.end_hidden(5)
            tail.shared_out_before()
            tail.shared_out()
            dve.wait_ge(in_iota, 16)

            def group_step(g, u, rows=True, ends=True, count=None):
                ex = Steps(dve, exp_step, EXP_STEPS * g)
                if rows:
                    v = u % 2
                    dve.wait_ge(rows_in[u % ROW_BUFS], count)
                    ex.done(V.tensor_tensor(w_tmp, rows_s[:, u % ROW_BUFS, bass.ds(PER * g + D, PER)], quad, ALU.mult))
                    ex.wait()
                    need(dve, hi_ready, g - 1)
                    V.tensor_reduce(w_slot[:, v:v + 1], w_tmp, AX_X, ALU.add).then_inc(w_ready, 1)
                    dve.wait_ge(eg_x_ready, g + 1)
                    ex.done(V.scalar_tensor_tensor(tg_x, eg_x, 1.0, gu_bank[:, 0:INTER], ALU.add, ALU.mult))
                    ex.wait()
                    need(dve, ht_full, g)
                    V.scalar_tensor_tensor(hid_x, gu_bank[:, INTER:2 * INTER], 0.5, tg_x, ALU.mult, ALU.mult)\
                     .then_inc(hid_ready, 1)
                if ends:
                    v = (u + 1) % 2
                    need(dve, back_done, g - 2)
                    V.tensor_scalar(place[v][:], iota_s, tok[:, bass.ds(g - 1, 1)], None, ALU.is_equal)\
                     .then_inc(place_ready, 1)
                    dve.wait_ge(hi_ready, g)
                    V.scalar_tensor_tensor(y_lo[v][:], y_bank[:, 0:D], w_slot[:, v:v + 1], y_hi[v][:].bitcast(F32),
                                           ALU.mult, ALU.subtract).then_inc(lo_ready, 1)

            for u in range(PEELED):
                group_step(u, u, ends=u > 0, count=gathered(u))
            with dve.Fori(0, ROUNDS) as k:
                for i in range(RING):
                    u = (PEELED + i) % RING
                    group_step(RING * k + (PEELED + i), u, count=16 * (RING // ROW_BUFS) * k + gathered(PEELED + i))
            group_step(GROUPS, GROUPS % RING, rows=False)

            dve.wait_ge(in_gb, 16 * BATCH)
            dve.wait_ge(post_done, BATCH)

            def scale_out(b):
                dve.wait_ge(acc_done, b + 1)
                V.tensor_tensor(out_tmp[:, b], acc[b][:].rearrange("p (t d) -> p t d", t=BT),
                                gb_all[:, b, :].unsqueeze(1).to_broadcast([P, BT, D]), ALU.mult)\
                 .then_inc(out_scaled, 1)

            def sum_out(b):
                dve.wait_ge(out_scaled, b + 1)
                tiles = x_s[:, BT * b:BT * b + BT, :]
                V.tensor_tensor(tiles, tiles, out_tmp[:, b], ALU.add).then_inc(out_ready[b], 1)

            scale_out(0)
            scale_out(1)
            scale_out(2)
            sum_out(1)
            scale_out(3)
            sum_out(3)

        @block.tensor
        def _(pe):
            mm = nc.tensor.matmul

            def modulation(m):
                pe.wait_ge(in_mod, 16)
                for c in range(DC):
                    last = mm(post[0:BATCH, :], ct_s[:, c, :], wmod_r[:, c, 2 * D * m:2 * D * (m + 1)],
                              start=(c == 0), stop=(c == DC - 1))
                last.then_inc(mod_mm, 1)

            def first_rows(b):
                pe.wait_ge(xn_ready, b + 1)
                for c in range(DC):
                    for t in range(BT):
                        last = nc.tensor.transpose(post[:, c * SEQ + t * P:c * SEQ + t * P + P],
                                                   xn_s[:, t, c * P:c * P + P], ident[:])
                last.then_inc(xt_full, 1)

            pe.wait_ge(in_mod_t, 16)
            pe.wait_ge(silu_c, 1)
            for m in range(2):
                for c2 in range(DC):
                    at = (m * DC + c2) * BATCH
                    for c in range(DC):
                        last = mm(wo_bank[:, at:at + BATCH], wmod_t[:, c, m * D + c2 * P:m * D + c2 * P + P],
                                  ct_s[:, c, :], start=(c == 0), stop=(c == DC - 1))
            last.then_inc(modt_mm, 1)
            pe.wait_ge(in_ident, 16)
            first_rows(0)

            def pj_take(b, n):
                need(pe, *(pj_release(b, n - 2) if n >= 2 else pj_release(b - 1, n + PJ_USES - 2)))
                return pj[n % 2]

            def project(b, r):
                dst = pj_take(b, PJ_ROPE[r])
                k = CH_K if r < 2 else CH_Q[(r - 2) // 2]
                if isinstance(b, int):
                    pe.wait_ge(*split(k))
                for i in range(2):
                    h = 2 * (r % 2) + i
                    for c in range(DC):
                        for u, v in PASSES:
                            last = mm(dst[:, i * SEQ:(i + 1) * SEQ], by_feature(k)[:, u, c, h * HD:(h + 1) * HD],
                                      h_cur[:, v, c, :], start=(c == u == v == 0), stop=(c == DC - 1 and u == 1))
                last.then_inc(pj_full, 1)

            def project_v(b, t):
                dst = pj_take(b, PJ_V[t])
                if isinstance(b, int):
                    pe.wait_ge(*split(CH_V))
                for c in range(DC):
                    for u, v in PASSES:
                        last = mm(dst[:], h_cur[:, u, c, t * P:(t + 1) * P], by_feature(CH_V)[:, v, c, :],
                                  start=(c == u == v == 0), stop=(c == DC - 1 and u == 1))
                last.then_inc(pj_full, 1)

            def score(b, s):
                g, i = divmod(s, 3)
                pe.wait_ge(*roped(b, 2 * g + 3))
                need(pe, *work_release(b, WORK_SCORE[s] - 4))
                dst = work[WORK_SCORE[s] % 4]
                if i == 0:
                    mm(dst[:], ident_b[:], mask_near[:].rearrange("p h k -> p (h k)"), start=True, stop=True)
                    for h in range(GROUP):
                        last = mm(dst[:, h * P:(h + 1) * P], q_s[:, g % 2, h, 0:P], k_s[:, g, 0:P],
                                  start=False, stop=True, skip_group_check=True)
                else:
                    mm(dst[:], ident_b[:], mask_far[:].rearrange("p h m k -> p (h m k)"), start=True, stop=True)
                    for n in range(2):
                        last = mm(dst[:, n * SEQ:(n + 1) * SEQ], q_s[:, g % 2, 2 * (i - 1) + n, P:SEQ], k_s[:, g, :],
                                  start=False, stop=True, skip_group_check=True)
                last.then_inc(sc_full, 1)

            def transpose_probs(b, g):
                for i in range(3):
                    if i == 0:
                        pe.wait_ge(norm_near, 4 * b + g + 1)
                    else:
                        pe.wait_ge(norm_far, 8 * b + 2 * g + i)
                    n = WORK_TRANS[3 * g + i]
                    need(pe, *work_release(b, n - 4))
                    for h in range(GROUP):
                        src = (prob_near[:, g % 2, h, :] if i == 0
                               else prob_far[:, g % 2, h, (i - 1) * P:i * P])
                        last = nc.tensor.transpose(work[n % 4][:, h * P:(h + 1) * P], src, ident[:])
                    last.then_inc(tr_full, 1)

            def mix(b, g):
                pe.wait_ge(v_out, 2 * b + 2)
                for t, blocks in enumerate(([(0, 0)], [(0, 1), (1, 2)])):
                    dst = pj_take(b, PJ_MIX[g][t])
                    for kt, i in blocks:
                        pe.wait_ge(trans_out, 12 * b + 3 * g + i + 1)
                        for u, v in PASSES:
                            last = mm(dst[:], v_s[:, u, kt, g * HD:(g + 1) * HD], prob_t[:, i, v, :],
                                      start=(kt == u == v == 0), stop=(kt == t and u == 1))
                    last.then_inc(pj_full, 1)

            def project_out(b, g, tiles=(0, 1)):
                if g == 0:
                    need(pe, wo_free, b)
                if isinstance(b, int):
                    pe.wait_ge(*split(CH_O[g]))
                w = chunk(CH_O[g]).rearrange("p r (h n) -> p r h n", h=GROUP)
                for t in tiles:
                    pe.wait_ge(mix_out, 8 * b + 2 * g + t + 1)
                    for h in range(GROUP):
                        for u, v in PASSES:
                            last = mm(wo_bank[:, t * D:(t + 1) * D], mix_s[:, g % 2, t, u, h * P:(h + 1) * P],
                                      w[:, v, h, :], start=(g == t == h == u == v == 0),
                                      stop=(g == KV_HEADS - 1 and h == GROUP - 1 and u == 1), skip_group_check=True)
                if t == BT - 1:
                    last.then_inc(wo_full, 1)

            def gate_up(m, dst):
                n = SM[m]
                for i, w in enumerate((swg_s, swu_s)):
                    for c in range(DC):
                        last = mm(dst[0:n, i * SEQ:(i + 1) * SEQ], w[:, c, m * P:m * P + n], h_t[:, c, :],
                                  start=(c == 0), stop=(c == DC - 1))
                return last

            def down(dst, m):
                n = SM[m]
                for t in range(BT):
                    last = mm(dst[:, t * D:(t + 1) * D], sh_s[0:n, m, t * P:(t + 1) * P], swd_s[0:n, m, :],
                              start=(m == t == 0), stop=(m == 2), skip_group_check=True)
                return last

            class Tail:

                def __init__(self, pb, order):
                    self.pb, self.order, self.shared = pb, order, order == IN_LOOP

                def take(self, use):
                    need(pe, post_free, post_base(self.pb) + self.order.index(use))

                def rows_t(self):
                    pe.wait_ge(h2_ready, self.pb + 1)
                    for c in range(DC):
                        for t in range(BT):
                            last = nc.tensor.transpose(post[:, c * SEQ + t * P:c * SEQ + t * P + P],
                                                       row_s[:, t, c * P:c * P + P], ident[:])
                    last.then_inc(post_full, 1)

                def logits(self):
                    self.take("logits")
                    for t in range(BT):
                        for c in range(DC):
                            last = mm(post[:, t * EXPERTS:(t + 1) * EXPERTS], h_t[:, c, t * P:(t + 1) * P],
                                      gate_s[:, c, :], start=(c == 0), stop=(c == DC - 1))
                    last.then_inc(post_full, 1)

                def gate_up(self, m):
                    self.take(f"gu{m}")
                    gate_up(m, post).then_inc(post_full, 1)

                def keys_t(self):
                    self.take("key_t")
                    pe.wait_ge(key_ready, self.pb + 1)
                    alone(pe, pe_passed)
                    for t in range(BT):
                        last = nc.tensor.transpose(post[0:EXPERTS, t * P:(t + 1) * P], key[:, t, :], ident[:])
                    last.then_inc(post_full, 1)

                def down(self):
                    self.take("down")
                    down(post, 0)
                    down(post, 1)
                    down(post, 2).then_inc(post_full, 1)

            def row_step(b, tail):
                pe.wait_ge(h_ready, b + 1)
                project(b, 0)
                project(b, 1)
                if tail:
                    project_out(b - 1, 3, [0])
                project(b, 2)
                project(b, 3)
                if tail:
                    project_out(b - 1, 3, [1])
                project_v(b, 0)
                project_v(b, 1)
                project(b, 4)
                if not tail:
                    pe.wait_ge(consts, 4)
                score(b, 0)
                project(b, 5)
                score(b, 1)
                score(b, 2)
                project(b, 6)
                if tail:
                    tail.rows_t()
                else:
                    modulation(0)
                project(b, 7)
                if tail:
                    tail.logits()
                score(b, 3)
                if tail and tail.shared:
                    tail.gate_up(0)
                if not tail:
                    pe.wait_ge(mod_rows, 2)
                    first_rows(1)
                score(b, 4)
                score(b, 5)
                if tail and tail.shared:
                    tail.gate_up(1)
                if not tail:
                    pe.wait_ge(xt_free, 2)
                    modulation(1)
                project(b, 8)
                transpose_probs(b, 0)
                project(b, 9)
                if tail:
                    tail.keys_t()
                score(b, 6)
                score(b, 7)
                mix(b, 0)
                if tail and tail.shared:
                    tail.gate_up(2)
                score(b, 8)
                if not (tail and tail.shared):
                    transpose_probs(b, 1)
                project_out(b, 0)
                if tail and tail.shared:
                    transpose_probs(b, 1)
                score(b, 9)
                score(b, 10)
                mix(b, 1)
                score(b, 11)
                transpose_probs(b, 2)
                project_out(b, 1)
                mix(b, 2)
                if tail and tail.shared:
                    tail.down()
                if not tail:
                    pe.wait_ge(mod_rows, 4)
                    first_rows(2)
                transpose_probs(b, 3)
                project_out(b, 2)
                if not tail:
                    pe.wait_ge(xt_free, 3)
                    first_rows(3)
                mix(b, 3)

            row_step(0, None)
            pe.wait_ge(in_tail, 96)
            with pe.Fori(1, BATCH - 1) as b:
                row_step(b, Tail(b - 1, IN_LOOP))
            row_step(BATCH - 1, Tail(BATCH - 2, IN_LAST))
            project_out(BATCH - 1, 3)
            tail = Tail(BATCH - 1, AT_END)

            def zero(a):
                mm(acc[a][:], zero_s[:, 0:P], zero_s[:], start=True, stop=True, skip_group_check=True)

            pe.wait_ge(*work_release(BATCH - 1, WORK_USES - 2))
            gate_up(0, end_bank[0]).then_inc(end_full, 1)
            pe.wait_ge(*work_release(BATCH - 1, WORK_USES - 1))
            gate_up(1, end_bank[1]).then_inc(end_full, 1)
            pe.wait_ge(wo_free, BATCH)
            gate_up(2, end_bank[2]).then_inc(end_full, 1)
            last_uses = [pj_release(BATCH - 1, PJ_USES - 2), pj_release(BATCH - 1, PJ_USES - 1),
                         work_release(BATCH - 1, WORK_USES - 4)]
            for a, last_use in enumerate(last_uses):
                pe.wait_ge(*last_use)
                zero(a)
            tail.rows_t()
            pe.wait_ge(*work_release(BATCH - 1, WORK_USES - 3))
            pe.wait_ge(end_free, 1)
            down(acc[3], 0)
            tail.logits()
            pe.wait_ge(end_free, 2)
            down(acc[3], 1)
            pe.wait_ge(end_free, 3)
            down(acc[3], 2).then_inc(down_full, 1)
            tail.keys_t()
            for m in range(2):
                pe.wait_ge(end_free, m + 1)
                gate_up(m, end_bank[m]).then_inc(end_full, 1)
            gate_up(2, end_bank[2]).then_inc(end_full, 1)
            tail.take("tok_t")
            pe.wait_ge(tok_e_ready, 1)
            nc.tensor.transpose(post[0:CAP, 0:EXPERTS], tok_e[:], ident[0:EXPERTS, 0:EXPERTS]).then_inc(post_full, 1)
            tail.take("down")
            for m in range(3):
                pe.wait_ge(end_free, 4 + m)
                last = down(post, m)
            last.then_inc(post_full, 1)

            def add_rows(v, b):
                for t in range(BT * b, BT * b + BT):
                    at = acc[b][:, (t % BT) * D:(t % BT + 1) * D]
                    for part in (y_hi[v], y_lo[v]):
                        last = mm(at, place[v][:, t * P:(t + 1) * P], part[:], start=False, stop=True,
                                  skip_group_check=True)
                return last

            def group_step(g, u, rows=True, ends=True, back=True, count=None, fills=None, ended=None):
                gu, wa, wb = slot(u)

                def hidden_t():
                    pe.wait_ge(hid_ready, g)
                    need(pe, hid_t_ready, g - 1)
                    nc.tensor.transpose(ht_bank[0:IA, 0:P], hid_x[:, 0:IA], ident[:])
                    nc.tensor.transpose(ht_bank[0:IB, P:2 * P], hid_x[:, IA:INTER], ident[:]).then_inc(ht_full, 1)

                if rows:
                    pe.wait_ge(rows_in[u % ROW_BUFS], count)
                    need(pe, hb_ready, g)
                    for c in range(DC):
                        last = nc.tensor.transpose(gt_bank[:, c * P:(c + 1) * P],
                                                   rows_s[:, u % ROW_BUFS, c * P:(c + 1) * P], ident[:])
                    last.then_inc(gt_full, 1)
                if ends and not rows:
                    hidden_t()
                if back:
                    pe.wait_ge(lo_ready, g - 2)
                    pe.wait_ge(place_ready, g - 2)
                    for b in range(BATCH):
                        last = add_rows((u + 1) % 2, b)
                    last.then_inc(back_done, 1)
                if ends and rows:
                    hidden_t()
                if rows:
                    pe.wait_ge(hb_ready, g + 1)
                    need(pe, hid_ready, g)
                    pe.wait_ge(in_gu[u], fills)
                    for c in range(DC):
                        for j in range(PER):
                            last = mm(gu_bank[CAP * j:CAP * (j + 1), 0:2 * INTER],
                                      hb_t[:, u % 2, c, CAP * j:CAP * (j + 1)], gu[:, :, j, c, :],
                                      start=(c == 0), stop=(c == DC - 1))
                    last.then_inc(gu_full, 1)
                if ends:
                    gu, wa, wb = slot((u - 1) % RING)
                    pe.wait_ge(hid_t_ready, g)
                    need(pe, lo_ready, g - 1)
                    pe.wait_ge(in_wd[(u - 1) % RING], ended)
                    for i, (hid, w) in enumerate(((hid_ta, wa), (hid_tb, wb))):
                        for j in range(PER):
                            last = mm(y_bank[CAP * j:CAP * (j + 1), 0:D], hid[:, CAP * j:CAP * (j + 1)], w[:, j, :],
                                      start=(i == 0), stop=(i == 1))
                    last.then_inc(y_full, 1)

            def fill(g):
                return 32 * (g // RING + 1)

            for u in range(PEELED):
                if u == 1:
                    pe.wait_ge(down_scaled, 1)
                    zero(3)
                    pe.wait_ge(post_free, post_base(BATCH - 1) + len(AT_END))
                group_step(u, u, ends=u > 0, back=u > 2, count=gathered(u), fills=fill(u), ended=fill(u - 1))
            with pe.Fori(0, ROUNDS) as k:
                for i in range(RING):
                    g = PEELED + i
                    group_step(RING * k + g, g % RING, count=16 * (RING // ROW_BUFS) * k + gathered(g),
                               fills=32 * k + fill(g), ended=32 * k + fill(g - 1))
            group_step(GROUPS, GROUPS % RING, rows=False, ended=fill(GROUPS - 1))
            even, odd = (GROUPS - 2) % 2, (GROUPS - 1) % 2
            pe.wait_ge(lo_ready, GROUPS - 1)
            pe.wait_ge(place_ready, GROUPS - 1)
            for b in range(BATCH - 1):
                add_rows(even, b)
            pe.wait_ge(lo_ready, GROUPS)
            pe.wait_ge(place_ready, GROUPS)
            for b in range(BATCH - 1):
                add_rows(odd, b).then_inc(acc_done, 1)
            add_rows(even, BATCH - 1)
            add_rows(odd, BATCH - 1).then_inc(acc_done, 1)


def kernel(L0_attn_x, L0_attn_wq, L0_attn_wk, L0_attn_wv, L0_attn_wo, L0_ffn_gate_w, L0_ffn_w_gate, L0_ffn_w_up,
           L0_ffn_w_down, L0_ffn_sw_gate, L0_ffn_sw_up, L0_ffn_sw_down, L0_c, L0_wmod):
    import numpy as np
    import concourse.bacc as bacc
    from concourse.bass_utils import run_bass_kernel_spmd

    f32 = np.float32

    def halves(w, heads):
        return np.ascontiguousarray(np.asarray(w).reshape(D, heads, HD // 2, 2).transpose(0, 1, 3, 2).reshape(D, -1))

    def by_group(w):
        w = np.asarray(w).reshape(GROUPS, PER, DC, P, INTER)
        return np.ascontiguousarray(w.transpose(0, 3, 1, 2, 4)).reshape(GROUPS, P, PER * DC * INTER)

    down = np.asarray(L0_ffn_w_down).reshape(GROUPS, PER, INTER, D).transpose(0, 2, 1, 3)

    inv = (1.0 / np.power(f32(10000.0), np.arange(0, HD, 2, dtype=f32) / f32(HD))).astype(f32)
    ang = np.outer(np.arange(SEQ, dtype=f32), inv).astype(f32).T
    cos, sin = np.cos(ang).astype(f32), np.sin(ang).astype(f32)
    cos2, sin2 = np.concatenate([cos, cos]), np.concatenate([-sin, sin])
    scale = f32(1.0 / np.sqrt(f32(HD)))
    rope = np.stack([cos2 * scale, sin2 * scale, cos2, sin2], axis=1).astype(f32)
    qi, ki = np.arange(P)[:, None], np.arange(P)[None, :]
    masks = np.stack([np.where(ki <= qi, 0.0, -1e30), np.where(ki >= qi, 0.0, -1e30), np.eye(P)], axis=1).astype(f32)
    rank = T - (np.arange(TT)[None, :] * P + np.arange(P)[:, None])
    quad = np.arange(P)[:, None] // CAP == np.arange(PER)[None, :]
    small = np.concatenate([rank, quad], axis=1).astype(f32)

    arrays = {
        "x": np.asarray(L0_attn_x), "c_t": np.asarray(L0_c).T, "wmod": np.asarray(L0_wmod),
        "wq": halves(L0_attn_wq, HEADS), "wk": halves(L0_attn_wk, KV_HEADS), "wv": np.asarray(L0_attn_wv),
        "wo": np.asarray(L0_attn_wo), "gate_t": np.asarray(L0_ffn_gate_w).T,
        "w_gate": by_group(L0_ffn_w_gate), "w_up": by_group(L0_ffn_w_up),
        "w_down_a": down[:, 0:IA].reshape(GROUPS, IA, PER * D), "w_down_b": down[:, IA:].reshape(GROUPS, IB, PER * D),
        "sw_gate": np.asarray(L0_ffn_sw_gate), "sw_up": np.asarray(L0_ffn_sw_up),
        "sw_down": np.asarray(L0_ffn_sw_down), "rope": rope, "masks": masks, "small": small,
        "iota_row": np.arange(T, dtype=f32),
    }
    nc = bacc.Bacc("TRN2", target_bir_lowering=False, num_devices=1)
    ins, given = [], {}
    for name, a in arrays.items():
        a = np.ascontiguousarray(a)
        given[f"in_{name}"] = a
        ins.append(nc.dram_tensor(f"in_{name}", a.shape, mybir.dt.from_np(a.dtype), kind="ExternalInput").ap())
    res = nc.dram_tensor("out_0", (BATCH, SEQ, D), F32, kind="ExternalOutput").ap()
    bass_adaln_attention_moe(nc, *ins, res)
    r = run_bass_kernel_spmd(nc, [given], core_ids=[0])
    return r.results[0]["out_0"]
```
